# Optimizing a Trainium2 kernel written in Bass

```python
import numpy as np
import jax
import jax.numpy as jnp

def _softmax(x, axis=-1):
    return jax.nn.softmax(x, axis=axis)

def _gelu(x):
    return jax.nn.gelu(x, approximate=True)

def _silu(x):
    return jax.nn.silu(x)

def _sigmoid(x):
    return jax.nn.sigmoid(x)

def _layernorm(x, axis=-1, eps=1e-05):
    m = jnp.mean(x, axis=axis, keepdims=True)
    v = jnp.var(x, axis=axis, keepdims=True)
    return (x - m) / jnp.sqrt(v + eps)

def _scatter_add(tgt, idx, src, axis=0):
    return tgt.at[idx].add(src)

def _segment_sum(src, seg, n):
    return jax.ops.segment_sum(src, seg, n)
kernel_name = 'mk_prb_d4_jaxref_r8_1af2cd'

def setup_inputs(seed: int=0):
    np.random.seed(seed)
    _w = jnp.asarray

    def _L0_attn_setup():
        import jax, jax.numpy as jnp
        import numpy as np
        B, L, D = (4, 1024, 128)
        N = D
        EPS = 1e-05

        def _ssm_scan(a, x):

            def combine(c1, c2):
                a1, b1 = c1
                a2, b2 = c2
                return (a1 * a2, a2 * b1 + b2)
            _, h = jax.lax.associative_scan(combine, (a, x), axis=1)
            return h
        key = jax.random.key(seed)
        ks = jax.random.split(key, 9)
        s = 1.0 / np.sqrt(D)
        return {'x': jax.random.normal(ks[0], (B, L, D), dtype=jnp.float32), 'norm_w': jnp.ones((D,), dtype=jnp.float32), 'A_w': jax.random.uniform(ks[1], (N, D), minval=-s, maxval=s), 'A_b': jax.random.uniform(ks[2], (N,), minval=-s, maxval=s), 'B_w': jax.random.uniform(ks[3], (N, D), minval=-s, maxval=s), 'C_w': jax.random.uniform(ks[4], (N, D), minval=-s, maxval=s), 'D_w': jax.random.uniform(ks[5], (N, D), minval=-s, maxval=s), 'out_w': jax.random.uniform(ks[6], (D, N), minval=-s, maxval=s), 'out_b': jax.random.uniform(ks[7], (D,), minval=-s, maxval=s)}
    _L0_attn_in = _L0_attn_setup()

    def _L0_ffn_setup():
        import jax, jax.numpy as jnp
        import numpy as np
        B, S = (4, 64)
        H = 128
        I = 352
        E = 8
        K = 2
        IS = 176
        key = jax.random.key(seed)
        ks = jax.random.split(key, 8)

        def init(k, shape, fan_in):
            return (jax.random.normal(k, shape, jnp.float32) / np.sqrt(fan_in)).astype(jnp.float32)
        return {'hidden_states': jax.random.normal(ks[0], (B, S, H), jnp.float32), 'gate_w': init(ks[1], (H, E), H), 'Wg': init(ks[2], (E, H, I), H), 'Wu': init(ks[3], (E, H, I), H), 'Wd': init(ks[4], (E, I, H), I), 'Sg': init(ks[5], (H, IS), H), 'Su': init(ks[6], (H, IS), H), 'Sd': init(ks[7], (IS, H), IS)}
    _L0_ffn_in = _L0_ffn_setup()

    def _L1_attn_setup():
        import jax, jax.numpy as jnp
        import numpy as np
        from jax.scipy.linalg import solve_triangular
        B, T, D = (2, 512, 128)
        HEAD_DIM = 128
        CHUNK = 64

        def _forward(out, W_write, W_read, W_alpha, W_beta, A_log, dt_bias):
            Bs, Ts, Ds = out.shape
            d, C = (HEAD_DIM, CHUNK)
            H = Ds // d
            x = out.astype(jnp.float32)
            rk = x.reshape(Bs, Ts, H, d)
            rk = rk / jnp.maximum(jnp.linalg.norm(rk, axis=-1, keepdims=True), 1e-12)
            rk = jnp.swapaxes(rk, 1, 2)
            wk = jnp.pad(rk[:, :, :-1], ((0, 0), (0, 0), (1, 0), (0, 0)))
            v = jnp.einsum('btd,ed->bte', x, W_write).reshape(Bs, Ts, H, d)
            v = jnp.swapaxes(v, 1, 2)
            beta = jax.nn.sigmoid(jnp.einsum('btd,hd->bth', x, W_beta))
            beta = jnp.swapaxes(beta, 1, 2)[..., None]
            log_decay = -jnp.exp(A_log)[None, None, :] * jax.nn.softplus(jnp.einsum('btd,hd->bth', x, W_alpha) + dt_bias)
            log_decay = jnp.swapaxes(log_decay, 1, 2)
            v_scaled = v * beta
            wk_scaled = wk * beta
            pad = -Ts % C
            if pad:
                p4 = ((0, 0), (0, 0), (0, pad), (0, 0))
                rk = jnp.pad(rk, p4)
                wk = jnp.pad(wk, p4)
                v_scaled = jnp.pad(v_scaled, p4)
                wk_scaled = jnp.pad(wk_scaled, p4)
                log_decay = jnp.pad(log_decay, ((0, 0), (0, 0), (0, pad)))
            Tp = Ts + pad
            N = Tp // C
            chunk = lambda a: a.reshape(Bs, H, N, C, d)
            rk, wk, v_scaled, wk_scaled = map(chunk, (rk, wk, v_scaled, wk_scaled))
            log_decay = log_decay.reshape(Bs, H, N, C)
            cum = jnp.cumsum(log_decay, -1)
            L_mask = jnp.tril(jnp.exp(jnp.tril(cum[..., :, None] - cum[..., None, :])))
            decay_exp = jnp.exp(cum)[..., None]
            chunk_end_decay = jnp.exp(cum[..., -1])
            M = jnp.tril(-(wk_scaled @ jnp.swapaxes(wk, -1, -2)) * L_mask, -1)
            eye = jnp.eye(C, dtype=x.dtype)
            A = solve_triangular(eye - M, jnp.broadcast_to(eye, M.shape), lower=True, unit_diagonal=True)
            intra = jnp.tril(rk @ jnp.swapaxes(wk, -1, -2) * L_mask, -1)
            rk_decay = rk * decay_exp
            tail_decay = jnp.exp(cum[..., -1:] - cum)[..., None]
            wk_pos = jnp.swapaxes(wk * tail_decay, -1, -2)
            wk_scaled_dec = wk_scaled * decay_exp
            toN = lambda a: jnp.moveaxis(a, 2, 0)

            def step(S, inp):
                A_i, vsc_i, wkd_i, rkd_i, intra_i, wkp_i, ced_i = inp
                v_new = A_i @ vsc_i - A_i @ wkd_i @ S
                o_i = rkd_i @ S + intra_i @ v_new
                S = ced_i[..., None, None] * S + wkp_i @ v_new
                return (S, o_i)
            S0 = jnp.zeros((Bs, H, d, d), x.dtype)
            _, o = jax.lax.scan(step, S0, (toN(A), toN(v_scaled), toN(wk_scaled_dec), toN(rk_decay), toN(intra), toN(wk_pos), jnp.moveaxis(chunk_end_decay, 2, 0)))
            o = jnp.moveaxis(o, 0, 2).reshape(Bs, H, Tp, d)
            o = jnp.swapaxes(o, 1, 2).reshape(Bs, Tp, Ds)[:, :Ts]
            return out + jnp.einsum('btd,ed->bte', o, W_read).astype(out.dtype)
        key = jax.random.key(seed)
        ks = jax.random.split(key, 7)
        H = D // HEAD_DIM
        out = jax.random.normal(ks[0], (B, T, D), dtype=jnp.float32)
        scale = D ** (-0.5)
        W_write = jax.random.normal(ks[1], (D, D), jnp.float32) * scale
        W_read = jax.random.normal(ks[2], (D, D), jnp.float32) * scale
        W_alpha = jax.random.normal(ks[3], (H, D), jnp.float32) * scale
        W_beta = jax.random.normal(ks[4], (H, D), jnp.float32) * scale
        A_log = jnp.log(jax.random.uniform(ks[5], (H,), jnp.float32, 0.05, 16.0))
        dt_bias = jnp.ones((H,), jnp.float32)
        return {'out': out, 'W_write': W_write, 'W_read': W_read, 'W_alpha': W_alpha, 'W_beta': W_beta, 'A_log': A_log, 'dt_bias': dt_bias}
    _L1_attn_in = _L1_attn_setup()

    def _L1_ffn_setup():
        import jax, jax.numpy as jnp
        import numpy as np
        DIM = 128
        DEPTH = 2
        HEADS = 8
        DIM_HEAD = 64
        WINDOW = 64
        INNER = HEADS * DIM_HEAD
        HID = int(DIM * 4 * 2 / 3)
        B, N = (2, 1024)
        QK_SCALE = 8.0

        def shift_token(t):
            t1, t2 = jnp.split(t, 2, axis=-1)
            t2 = jnp.pad(t2, ((0, 0), (1, 0), (0, 0)))[:, :-1]
            return jnp.concatenate([t1, t2], axis=-1)

        def l2norm(t):
            return t / jnp.clip(jnp.linalg.norm(t, axis=-1, keepdims=True), 1e-12)

        def rotate_half(x):
            x1, x2 = jnp.split(x, 2, axis=-1)
            return jnp.concatenate([-x2, x1], axis=-1)

        def rotary_xpos(q, k):
            n = q.shape[-2]
            half_idx = jnp.arange(0, DIM_HEAD, 2, dtype=jnp.float32)
            inv_freq = 1.0 / 10000.0 ** (half_idx / DIM_HEAD)
            t = jnp.arange(n, dtype=jnp.float32)
            freqs = t[:, None] * inv_freq[None, :]
            freqs = jnp.concatenate([freqs, freqs], axis=-1)
            base = (half_idx + 0.4 * DIM_HEAD) / (1.4 * DIM_HEAD)
            power = (t - n // 2) / float(WINDOW // 2)
            scale = base[None, :] ** power[:, None]
            scale = jnp.concatenate([scale, scale], axis=-1)
            cos, sin = (jnp.cos(freqs), jnp.sin(freqs))
            q = q * cos * scale + rotate_half(q) * sin * scale
            k = k * cos / scale + rotate_half(k) * sin / scale
            return (q, k)

        def local_attention(q, k, v):
            b, h, n, d = q.shape
            w = n // WINDOW
            bq = q.reshape(b, h, w, WINDOW, d) * QK_SCALE
            bk = k.reshape(b, h, w, WINDOW, d)
            bv = v.reshape(b, h, w, WINDOW, d)

            def look_around(t):
                p = jnp.pad(t, ((0, 0), (0, 0), (1, 0), (0, 0), (0, 0)))
                return jnp.concatenate([p[:, :, :w], p[:, :, 1:]], axis=3)
            bk, bv = (look_around(bk), look_around(bv))
            bt = jnp.arange(n).reshape(w, WINDOW)
            btp = jnp.pad(bt, ((1, 0), (0, 0)), constant_values=-1)
            btk = jnp.concatenate([btp[:w], btp[1:]], axis=1)
            sim = jnp.einsum('bhwid,bhwjd->bhwij', bq, bk)
            i = bt[:, :, None]
            j = btk[:, None, :]
            mask = (i < j) | (i > j + WINDOW) | (j == -1)
            sim = jnp.where(mask, -jnp.finfo(sim.dtype).max, sim)
            attn = jax.nn.softmax(sim, axis=-1)
            out = jnp.einsum('bhwij,bhwjd->bhwid', attn, bv)
            return out.reshape(b, h, n, d)

        def _layer(x, wqkv, qs, ksc, wo, lg, lb, w1, b1, w2, b2):
            b, n, _ = x.shape
            h = shift_token(x)
            qkv = h @ wqkv
            q, k, v = jnp.split(qkv, 3, axis=-1)
            to_heads = lambda t: t.reshape(b, n, HEADS, DIM_HEAD).transpose(0, 2, 1, 3)
            q, k, v = (to_heads(q), to_heads(k), to_heads(v))
            q = l2norm(q) * qs
            k = l2norm(k) * ksc
            q, k = rotary_xpos(q, k)
            o = local_attention(q, k, v)
            o = o.transpose(0, 2, 1, 3).reshape(b, n, INNER)
            x = x + o @ wo
            h = shift_token(x)
            mu = h.mean(-1, keepdims=True)
            var = h.var(-1, keepdims=True)
            h = (h - mu) / jnp.sqrt(var + 1e-05) * lg + lb
            h = h @ w1 + b1
            a, g = jnp.split(h, 2, axis=-1)
            h = a * jax.nn.gelu(g, approximate=False)
            x = x + h @ w2 + b2
            return x
        key = jax.random.key(seed)
        ks = jax.random.split(key, 6)
        return {'x': jax.random.normal(ks[0], (B, N, DIM), jnp.float32), 'wqkv': jax.random.normal(ks[1], (DEPTH, DIM, 3 * INNER), jnp.float32) * 0.02, 'q_scale': jnp.ones((DEPTH, DIM_HEAD), jnp.float32), 'k_scale': jnp.ones((DEPTH, DIM_HEAD), jnp.float32), 'wo': jax.random.normal(ks[2], (DEPTH, INNER, DIM), jnp.float32) * 0.02, 'ln_g': jnp.ones((DEPTH, DIM), jnp.float32), 'ln_b': jnp.zeros((DEPTH, DIM), jnp.float32), 'w1': jax.random.normal(ks[3], (DEPTH, DIM, 2 * HID), jnp.float32) * 0.02, 'b1': jnp.zeros((DEPTH, 2 * HID), jnp.float32), 'w2': jax.random.normal(ks[4], (DEPTH, HID, DIM), jnp.float32) * 0.02, 'b2': jnp.zeros((DEPTH, DIM), jnp.float32)}
    _L1_ffn_in = _L1_ffn_setup()

    def _L2_attn_setup():
        import jax, jax.numpy as jnp
        import numpy as np
        N_EMBD = 128
        N_HEAD = 16
        HEAD_DIM = N_EMBD // N_HEAD
        LATENT_DIM = N_EMBD // 2
        B, T = (4, 256)
        key = jax.random.key(seed)
        ks = jax.random.split(key, 5)

        def init(k, fan_in, fan_out):
            bound = 1.0 / np.sqrt(fan_in)
            return jax.random.uniform(k, (fan_in, fan_out), jnp.float32, -bound, bound)
        return {'x': jax.random.normal(ks[0], (B, T, N_EMBD), jnp.float32), 'Wc_down': init(ks[1], N_EMBD, LATENT_DIM), 'Wq_up': init(ks[2], LATENT_DIM, N_EMBD), 'Wkv_up': init(ks[3], LATENT_DIM, 2 * HEAD_DIM), 'Wc_proj': init(ks[4], N_EMBD, N_EMBD)}
    _L2_attn_in = _L2_attn_setup()

    def _L2_ffn_setup():
        import jax, jax.numpy as jnp
        import numpy as np
        DIM = 128
        DEPTH = 6
        HEADS = 16
        DIM_HEAD = 64
        WINDOW = 32
        INNER = HEADS * DIM_HEAD
        DIM_INNER = int(DIM * 4 * 2 / 3)
        QK_SCALE = 8.0

        def shift_tokens(t):
            a, s = jnp.split(t, 2, -1)
            s = jnp.pad(s, ((0, 0), (1, 0), (0, 0)))[:, :-1]
            return jnp.concatenate([a, s], -1)

        def l2norm(t):
            return t / jnp.maximum(jnp.linalg.norm(t, axis=-1, keepdims=True), 1e-12)

        def rotate_half(x):
            x1, x2 = jnp.split(x, 2, -1)
            return jnp.concatenate([-x2, x1], -1)

        def rotary_tables(n):
            half = jnp.arange(0, DIM_HEAD, 2, dtype=jnp.float32)
            inv_freq = 1.0 / 10000.0 ** (half / DIM_HEAD)
            t = jnp.arange(n, dtype=jnp.float32)
            freqs = t[:, None] * inv_freq[None, :]
            freqs = jnp.concatenate([freqs, freqs], -1)
            base_scale = (half + 0.4 * DIM_HEAD) / (1.4 * DIM_HEAD)
            power = (t - n // 2) / (WINDOW // 2)
            scale = base_scale[None, :] ** power[:, None]
            scale = jnp.concatenate([scale, scale], -1)
            return (freqs, scale)

        def local_attention(q, k, v):
            b, h, n, d = q.shape
            w = WINDOW
            nw = n // w
            bq = q.reshape(b, h, nw, w, d)
            bk = k.reshape(b, h, nw, w, d)
            bv = v.reshape(b, h, nw, w, d)

            def look(t):
                p = jnp.pad(t, ((0, 0), (0, 0), (1, 0), (0, 0), (0, 0)))
                return jnp.concatenate([p[:, :, :nw], p[:, :, 1:]], axis=3)
            bk2, bv2 = (look(bk), look(bv))
            seq = jnp.arange(n).reshape(nw, w)
            seq_p = jnp.pad(seq, ((1, 0), (0, 0)), constant_values=-1)
            jt = jnp.concatenate([seq_p[:nw], seq_p[1:]], axis=1)
            it = seq[:, :, None]
            jb = jt[:, None, :]
            mask = (it < jb) | (it > jb + w) | (jb == -1)
            sim = jnp.einsum('bhwie,bhwje->bhwij', bq, bk2) * QK_SCALE
            sim = jnp.where(mask, -jnp.finfo(sim.dtype).max, sim)
            attn = jax.nn.softmax(sim, -1)
            out = jnp.einsum('bhwij,bhwje->bhwie', attn, bv2)
            return out.reshape(b, h, n, d)

        def attn_layer(x, Wqkv, qs, ksc, Wo):
            b, n, _ = x.shape
            qkv = x @ Wqkv
            q, k, v = jnp.split(qkv, 3, -1)
            sh = lambda t: t.reshape(b, n, HEADS, DIM_HEAD).transpose(0, 2, 1, 3)
            q, k, v = (sh(q), sh(k), sh(v))
            q = l2norm(q) * qs
            k = l2norm(k) * ksc
            freqs, scale = rotary_tables(n)
            cos, sin = (jnp.cos(freqs), jnp.sin(freqs))
            q = q * cos * scale + rotate_half(q) * sin * scale
            inv = 1.0 / scale
            k = k * cos * inv + rotate_half(k) * sin * inv
            out = local_attention(q, k, v)
            out = out.transpose(0, 2, 1, 3).reshape(b, n, INNER)
            return out @ Wo

        def ffn_layer(x, g, bln, W1, b1, W2, b2):
            mu = x.mean(-1, keepdims=True)
            var = ((x - mu) ** 2).mean(-1, keepdims=True)
            xn = (x - mu) / jnp.sqrt(var + 1e-05) * g + bln
            hg = xn @ W1 + b1
            a, gate = jnp.split(hg, 2, -1)
            return a * jax.nn.gelu(gate, approximate=False) @ W2 + b2
        key = jax.random.key(seed)
        ks = jax.random.split(key, 8)
        B, N = (2, 256)
        init = lambda k, shape: jax.random.normal(k, shape, jnp.float32) * 0.02
        return {'x': jax.random.normal(ks[0], (B, N, DIM), jnp.float32), 'Wqkv': init(ks[1], (DEPTH, DIM, 3 * INNER)), 'q_scale': jnp.ones((DEPTH, DIM_HEAD), jnp.float32), 'k_scale': jnp.ones((DEPTH, DIM_HEAD), jnp.float32), 'Wo': init(ks[2], (DEPTH, INNER, DIM)), 'ln_g': jnp.ones((DEPTH, DIM), jnp.float32), 'ln_b': jnp.zeros((DEPTH, DIM), jnp.float32), 'W1': init(ks[3], (DEPTH, DIM, 2 * DIM_INNER)), 'b1': jnp.zeros((DEPTH, 2 * DIM_INNER), jnp.float32), 'W2': init(ks[4], (DEPTH, DIM_INNER, DIM)), 'b2': jnp.zeros((DEPTH, DIM), jnp.float32)}
    _L2_ffn_in = _L2_ffn_setup()

    def _L3_attn_setup():
        import jax, jax.numpy as jnp
        import numpy as np
        D_MODEL = 128
        NUM_HEADS = 16
        DEPTH = D_MODEL // NUM_HEADS
        MAX_LEN = 625
        EPS = 1e-06

        def _make_rel_pos_emb():
            pos = np.arange(-MAX_LEN, MAX_LEN + 1, dtype=np.float32)[:, None]
            dim = np.arange(D_MODEL, dtype=np.float32)[None, :]
            angle = pos / 1250 ** (2 * (dim // 2) / D_MODEL)
            pe = np.where(dim % 2 == 0, np.sin(angle), np.cos(angle)).astype(np.float32)
            return jnp.asarray(pe)

        def _rel_shift(x):
            B, H, L, _ = x.shape
            x_padded = jnp.pad(x, ((0, 0), (0, 0), (0, 0), (1, 0)))
            x_padded = x_padded.reshape(B, H, 2 * L, L)
            x_shifted = x_padded[:, :, 1:, :].reshape(B, H, L, 2 * L - 1)
            return x_shifted[:, :, :, :L]
        key = jax.random.key(seed)
        ks = jax.random.split(key, 8)
        B, L = (2, 128)
        s = 1.0 / np.sqrt(D_MODEL)
        return {'x': jax.random.normal(ks[0], (B, L, D_MODEL), jnp.float32), 'gamma': jnp.ones((D_MODEL,), jnp.float32), 'beta': jnp.zeros((D_MODEL,), jnp.float32), 'Wq': jax.random.normal(ks[1], (D_MODEL, D_MODEL), jnp.float32) * s, 'Wk': jax.random.normal(ks[2], (D_MODEL, D_MODEL), jnp.float32) * s, 'Wv': jax.random.normal(ks[3], (D_MODEL, D_MODEL), jnp.float32) * s, 'Wr': jax.random.normal(ks[4], (D_MODEL, D_MODEL), jnp.float32) * s, 'u_bias': jax.random.normal(ks[5], (NUM_HEADS, DEPTH), jnp.float32) * 0.02, 'v_bias': jax.random.normal(ks[6], (NUM_HEADS, DEPTH), jnp.float32) * 0.02, 'Wo': jax.random.normal(ks[7], (D_MODEL, D_MODEL), jnp.float32) * s, 'bo': jnp.zeros((D_MODEL,), jnp.float32), 'rel_pos_emb': _make_rel_pos_emb()}
    _L3_attn_in = _L3_attn_setup()

    def _L3_ffn_setup():
        import jax, jax.numpy as jnp
        import numpy as np
        FF_DIM = 256
        TOP_K = 2
        key = jax.random.key(seed)
        k1, k2, k3, k4 = jax.random.split(key, 4)
        B, S, D, E, F = (2, 256, 128, 8, FF_DIM)
        std = 0.006
        return {'x': jax.random.normal(k1, (B, S, D), dtype=jnp.float32), 'gate_w': jax.random.normal(k2, (D, E), dtype=jnp.float32) * 0.02, 'gate_up_w': jax.random.normal(k3, (E, D, 2 * F), dtype=jnp.float32) * std, 'down_w': jax.random.normal(k4, (E, F, D), dtype=jnp.float32) * std}
    _L3_ffn_in = _L3_ffn_setup()
    _d = {'L0_attn_x': _L0_attn_in['x'], 'L0_attn_norm_w': _L0_attn_in['norm_w'], 'L0_attn_A_w': _L0_attn_in['A_w'], 'L0_attn_A_b': _L0_attn_in['A_b'], 'L0_attn_B_w': _L0_attn_in['B_w'], 'L0_attn_C_w': _L0_attn_in['C_w'], 'L0_attn_D_w': _L0_attn_in['D_w'], 'L0_attn_out_w': _L0_attn_in['out_w'], 'L0_attn_out_b': _L0_attn_in['out_b'], 'L0_ffn_gate_w': _L0_ffn_in['gate_w'], 'L0_ffn_Wg': _L0_ffn_in['Wg'], 'L0_ffn_Wu': _L0_ffn_in['Wu'], 'L0_ffn_Wd': _L0_ffn_in['Wd'], 'L0_ffn_Sg': _L0_ffn_in['Sg'], 'L0_ffn_Su': _L0_ffn_in['Su'], 'L0_ffn_Sd': _L0_ffn_in['Sd'], 'L1_attn_W_write': _L1_attn_in['W_write'], 'L1_attn_W_read': _L1_attn_in['W_read'], 'L1_attn_W_alpha': _L1_attn_in['W_alpha'], 'L1_attn_W_beta': _L1_attn_in['W_beta'], 'L1_attn_A_log': _L1_attn_in['A_log'], 'L1_attn_dt_bias': _L1_attn_in['dt_bias'], 'L1_ffn_wqkv': _L1_ffn_in['wqkv'], 'L1_ffn_q_scale': _L1_ffn_in['q_scale'], 'L1_ffn_k_scale': _L1_ffn_in['k_scale'], 'L1_ffn_wo': _L1_ffn_in['wo'], 'L1_ffn_ln_g': _L1_ffn_in['ln_g'], 'L1_ffn_ln_b': _L1_ffn_in['ln_b'], 'L1_ffn_w1': _L1_ffn_in['w1'], 'L1_ffn_b1': _L1_ffn_in['b1'], 'L1_ffn_w2': _L1_ffn_in['w2'], 'L1_ffn_b2': _L1_ffn_in['b2'], 'L2_attn_Wc_down': _L2_attn_in['Wc_down'], 'L2_attn_Wq_up': _L2_attn_in['Wq_up'], 'L2_attn_Wkv_up': _L2_attn_in['Wkv_up'], 'L2_attn_Wc_proj': _L2_attn_in['Wc_proj'], 'L2_ffn_Wqkv': _L2_ffn_in['Wqkv'], 'L2_ffn_q_scale': _L2_ffn_in['q_scale'], 'L2_ffn_k_scale': _L2_ffn_in['k_scale'], 'L2_ffn_Wo': _L2_ffn_in['Wo'], 'L2_ffn_ln_g': _L2_ffn_in['ln_g'], 'L2_ffn_ln_b': _L2_ffn_in['ln_b'], 'L2_ffn_W1': _L2_ffn_in['W1'], 'L2_ffn_b1': _L2_ffn_in['b1'], 'L2_ffn_W2': _L2_ffn_in['W2'], 'L2_ffn_b2': _L2_ffn_in['b2'], 'L3_attn_gamma': _L3_attn_in['gamma'], 'L3_attn_beta': _L3_attn_in['beta'], 'L3_attn_Wq': _L3_attn_in['Wq'], 'L3_attn_Wk': _L3_attn_in['Wk'], 'L3_attn_Wv': _L3_attn_in['Wv'], 'L3_attn_Wr': _L3_attn_in['Wr'], 'L3_attn_u_bias': _L3_attn_in['u_bias'], 'L3_attn_v_bias': _L3_attn_in['v_bias'], 'L3_attn_Wo': _L3_attn_in['Wo'], 'L3_attn_bo': _L3_attn_in['bo'], 'L3_attn_rel_pos_emb': _L3_attn_in['rel_pos_emb'], 'L3_ffn_gate_w': _L3_ffn_in['gate_w'], 'L3_ffn_gate_up_w': _L3_ffn_in['gate_up_w'], 'L3_ffn_down_w': _L3_ffn_in['down_w']}
    _x0 = _d['L0_attn_x']
    _d['L0_attn_x'] = jax.random.normal(jax.random.fold_in(jax.random.key(seed), 1), (8, 256, 128), dtype=_x0.dtype)
    del _x0
    return _d

def reference(L0_attn_x, L0_attn_norm_w, L0_attn_A_w, L0_attn_A_b, L0_attn_B_w, L0_attn_C_w, L0_attn_D_w, L0_attn_out_w, L0_attn_out_b, L0_ffn_gate_w, L0_ffn_Wg, L0_ffn_Wu, L0_ffn_Wd, L0_ffn_Sg, L0_ffn_Su, L0_ffn_Sd, L1_attn_W_write, L1_attn_W_read, L1_attn_W_alpha, L1_attn_W_beta, L1_attn_A_log, L1_attn_dt_bias, L1_ffn_wqkv, L1_ffn_q_scale, L1_ffn_k_scale, L1_ffn_wo, L1_ffn_ln_g, L1_ffn_ln_b, L1_ffn_w1, L1_ffn_b1, L1_ffn_w2, L1_ffn_b2, L2_attn_Wc_down, L2_attn_Wq_up, L2_attn_Wkv_up, L2_attn_Wc_proj, L2_ffn_Wqkv, L2_ffn_q_scale, L2_ffn_k_scale, L2_ffn_Wo, L2_ffn_ln_g, L2_ffn_ln_b, L2_ffn_W1, L2_ffn_b1, L2_ffn_W2, L2_ffn_b2, L3_attn_gamma, L3_attn_beta, L3_attn_Wq, L3_attn_Wk, L3_attn_Wv, L3_attn_Wr, L3_attn_u_bias, L3_attn_v_bias, L3_attn_Wo, L3_attn_bo, L3_attn_rel_pos_emb, L3_ffn_gate_w, L3_ffn_gate_up_w, L3_ffn_down_w):

    def _L0_attn_ref(x, norm_w, A_w, A_b, B_w, C_w, D_w, out_w, out_b):
        import jax, jax.numpy as jnp
        import numpy as np
        B, L, D = (4, 1024, 128)
        N = D
        EPS = 1e-05

        def _ssm_scan(a, x):

            def combine(c1, c2):
                a1, b1 = c1
                a2, b2 = c2
                return (a1 * a2, a2 * b1 + b2)
            _, h = jax.lax.associative_scan(combine, (a, x), axis=1)
            return h
        residual = x
        norm = jnp.sqrt(jnp.mean(x * x, axis=-1, keepdims=True) + EPS)
        xn = x * (norm_w / norm)
        a = jax.nn.sigmoid(jnp.einsum('bld,nd->bln', xn, A_w) + A_b)
        b = jnp.einsum('bld,nd->bln', xn, B_w)
        c = jax.nn.sigmoid(jnp.einsum('bld,nd->bln', xn, C_w))
        d = jax.nn.sigmoid(jnp.einsum('bld,nd->bln', xn, D_w))
        h = c * _ssm_scan(a, d * b)
        y = jnp.einsum('bln,dn->bld', h, out_w) + out_b
        return y + residual

    def _L0_ffn_ref(hidden_states, gate_w, Wg, Wu, Wd, Sg, Su, Sd):
        import jax, jax.numpy as jnp
        import numpy as np
        B, S = (4, 64)
        H = 128
        I = 352
        E = 8
        K = 2
        IS = 176
        b, s, h = hidden_states.shape
        x = hidden_states.reshape(-1, h)
        T = x.shape[0]
        logits = x @ gate_w
        top_v, top_i = jax.lax.top_k(logits, K)
        top_p = jax.nn.softmax(top_v, axis=-1)
        combine = jnp.zeros((T, E), x.dtype).at[jnp.arange(T)[:, None], top_i].add(top_p)
        g = jnp.einsum('th,ehi->tei', x, Wg)
        u = jnp.einsum('th,ehi->tei', x, Wu)
        d = jnp.einsum('tei,eih->teh', jax.nn.silu(g) * u, Wd)
        expert_out = jnp.einsum('te,teh->th', combine, d)
        shared = jax.nn.silu(x @ Sg) * (x @ Su) @ Sd
        return (expert_out + shared).reshape(b, s, h)

    def _L1_attn_ref(out, W_write, W_read, W_alpha, W_beta, A_log, dt_bias):
        import jax, jax.numpy as jnp
        import numpy as np
        from jax.scipy.linalg import solve_triangular
        B, T, D = (2, 512, 128)
        HEAD_DIM = 128
        CHUNK = 64

        def _forward(out, W_write, W_read, W_alpha, W_beta, A_log, dt_bias):
            Bs, Ts, Ds = out.shape
            d, C = (HEAD_DIM, CHUNK)
            H = Ds // d
            x = out.astype(jnp.float32)
            rk = x.reshape(Bs, Ts, H, d)
            rk = rk / jnp.maximum(jnp.linalg.norm(rk, axis=-1, keepdims=True), 1e-12)
            rk = jnp.swapaxes(rk, 1, 2)
            wk = jnp.pad(rk[:, :, :-1], ((0, 0), (0, 0), (1, 0), (0, 0)))
            v = jnp.einsum('btd,ed->bte', x, W_write).reshape(Bs, Ts, H, d)
            v = jnp.swapaxes(v, 1, 2)
            beta = jax.nn.sigmoid(jnp.einsum('btd,hd->bth', x, W_beta))
            beta = jnp.swapaxes(beta, 1, 2)[..., None]
            log_decay = -jnp.exp(A_log)[None, None, :] * jax.nn.softplus(jnp.einsum('btd,hd->bth', x, W_alpha) + dt_bias)
            log_decay = jnp.swapaxes(log_decay, 1, 2)
            v_scaled = v * beta
            wk_scaled = wk * beta
            pad = -Ts % C
            if pad:
                p4 = ((0, 0), (0, 0), (0, pad), (0, 0))
                rk = jnp.pad(rk, p4)
                wk = jnp.pad(wk, p4)
                v_scaled = jnp.pad(v_scaled, p4)
                wk_scaled = jnp.pad(wk_scaled, p4)
                log_decay = jnp.pad(log_decay, ((0, 0), (0, 0), (0, pad)))
            Tp = Ts + pad
            N = Tp // C
            chunk = lambda a: a.reshape(Bs, H, N, C, d)
            rk, wk, v_scaled, wk_scaled = map(chunk, (rk, wk, v_scaled, wk_scaled))
            log_decay = log_decay.reshape(Bs, H, N, C)
            cum = jnp.cumsum(log_decay, -1)
            L_mask = jnp.tril(jnp.exp(jnp.tril(cum[..., :, None] - cum[..., None, :])))
            decay_exp = jnp.exp(cum)[..., None]
            chunk_end_decay = jnp.exp(cum[..., -1])
            M = jnp.tril(-(wk_scaled @ jnp.swapaxes(wk, -1, -2)) * L_mask, -1)
            eye = jnp.eye(C, dtype=x.dtype)
            A = solve_triangular(eye - M, jnp.broadcast_to(eye, M.shape), lower=True, unit_diagonal=True)
            intra = jnp.tril(rk @ jnp.swapaxes(wk, -1, -2) * L_mask, -1)
            rk_decay = rk * decay_exp
            tail_decay = jnp.exp(cum[..., -1:] - cum)[..., None]
            wk_pos = jnp.swapaxes(wk * tail_decay, -1, -2)
            wk_scaled_dec = wk_scaled * decay_exp
            toN = lambda a: jnp.moveaxis(a, 2, 0)

            def step(S, inp):
                A_i, vsc_i, wkd_i, rkd_i, intra_i, wkp_i, ced_i = inp
                v_new = A_i @ vsc_i - A_i @ wkd_i @ S
                o_i = rkd_i @ S + intra_i @ v_new
                S = ced_i[..., None, None] * S + wkp_i @ v_new
                return (S, o_i)
            S0 = jnp.zeros((Bs, H, d, d), x.dtype)
            _, o = jax.lax.scan(step, S0, (toN(A), toN(v_scaled), toN(wk_scaled_dec), toN(rk_decay), toN(intra), toN(wk_pos), jnp.moveaxis(chunk_end_decay, 2, 0)))
            o = jnp.moveaxis(o, 0, 2).reshape(Bs, H, Tp, d)
            o = jnp.swapaxes(o, 1, 2).reshape(Bs, Tp, Ds)[:, :Ts]
            return out + jnp.einsum('btd,ed->bte', o, W_read).astype(out.dtype)
        return _forward(out, W_write, W_read, W_alpha, W_beta, A_log, dt_bias)

    def _L1_ffn_ref(x, wqkv, q_scale, k_scale, wo, ln_g, ln_b, w1, b1, w2, b2):
        import jax, jax.numpy as jnp
        import numpy as np
        DIM = 128
        DEPTH = 2
        HEADS = 8
        DIM_HEAD = 64
        WINDOW = 64
        INNER = HEADS * DIM_HEAD
        HID = int(DIM * 4 * 2 / 3)
        B, N = (2, 1024)
        QK_SCALE = 8.0

        def shift_token(t):
            t1, t2 = jnp.split(t, 2, axis=-1)
            t2 = jnp.pad(t2, ((0, 0), (1, 0), (0, 0)))[:, :-1]
            return jnp.concatenate([t1, t2], axis=-1)

        def l2norm(t):
            return t / jnp.clip(jnp.linalg.norm(t, axis=-1, keepdims=True), 1e-12)

        def rotate_half(x):
            x1, x2 = jnp.split(x, 2, axis=-1)
            return jnp.concatenate([-x2, x1], axis=-1)

        def rotary_xpos(q, k):
            n = q.shape[-2]
            half_idx = jnp.arange(0, DIM_HEAD, 2, dtype=jnp.float32)
            inv_freq = 1.0 / 10000.0 ** (half_idx / DIM_HEAD)
            t = jnp.arange(n, dtype=jnp.float32)
            freqs = t[:, None] * inv_freq[None, :]
            freqs = jnp.concatenate([freqs, freqs], axis=-1)
            base = (half_idx + 0.4 * DIM_HEAD) / (1.4 * DIM_HEAD)
            power = (t - n // 2) / float(WINDOW // 2)
            scale = base[None, :] ** power[:, None]
            scale = jnp.concatenate([scale, scale], axis=-1)
            cos, sin = (jnp.cos(freqs), jnp.sin(freqs))
            q = q * cos * scale + rotate_half(q) * sin * scale
            k = k * cos / scale + rotate_half(k) * sin / scale
            return (q, k)

        def local_attention(q, k, v):
            b, h, n, d = q.shape
            w = n // WINDOW
            bq = q.reshape(b, h, w, WINDOW, d) * QK_SCALE
            bk = k.reshape(b, h, w, WINDOW, d)
            bv = v.reshape(b, h, w, WINDOW, d)

            def look_around(t):
                p = jnp.pad(t, ((0, 0), (0, 0), (1, 0), (0, 0), (0, 0)))
                return jnp.concatenate([p[:, :, :w], p[:, :, 1:]], axis=3)
            bk, bv = (look_around(bk), look_around(bv))
            bt = jnp.arange(n).reshape(w, WINDOW)
            btp = jnp.pad(bt, ((1, 0), (0, 0)), constant_values=-1)
            btk = jnp.concatenate([btp[:w], btp[1:]], axis=1)
            sim = jnp.einsum('bhwid,bhwjd->bhwij', bq, bk)
            i = bt[:, :, None]
            j = btk[:, None, :]
            mask = (i < j) | (i > j + WINDOW) | (j == -1)
            sim = jnp.where(mask, -jnp.finfo(sim.dtype).max, sim)
            attn = jax.nn.softmax(sim, axis=-1)
            out = jnp.einsum('bhwij,bhwjd->bhwid', attn, bv)
            return out.reshape(b, h, n, d)

        def _layer(x, wqkv, qs, ksc, wo, lg, lb, w1, b1, w2, b2):
            b, n, _ = x.shape
            h = shift_token(x)
            qkv = h @ wqkv
            q, k, v = jnp.split(qkv, 3, axis=-1)
            to_heads = lambda t: t.reshape(b, n, HEADS, DIM_HEAD).transpose(0, 2, 1, 3)
            q, k, v = (to_heads(q), to_heads(k), to_heads(v))
            q = l2norm(q) * qs
            k = l2norm(k) * ksc
            q, k = rotary_xpos(q, k)
            o = local_attention(q, k, v)
            o = o.transpose(0, 2, 1, 3).reshape(b, n, INNER)
            x = x + o @ wo
            h = shift_token(x)
            mu = h.mean(-1, keepdims=True)
            var = h.var(-1, keepdims=True)
            h = (h - mu) / jnp.sqrt(var + 1e-05) * lg + lb
            h = h @ w1 + b1
            a, g = jnp.split(h, 2, axis=-1)
            h = a * jax.nn.gelu(g, approximate=False)
            x = x + h @ w2 + b2
            return x
        for l in range(DEPTH):
            x = _layer(x, wqkv[l], q_scale[l], k_scale[l], wo[l], ln_g[l], ln_b[l], w1[l], b1[l], w2[l], b2[l])
        return x

    def _L2_attn_ref(x, Wc_down, Wq_up, Wkv_up, Wc_proj):
        import jax, jax.numpy as jnp
        import numpy as np
        N_EMBD = 128
        N_HEAD = 16
        HEAD_DIM = N_EMBD // N_HEAD
        LATENT_DIM = N_EMBD // 2
        B, T = (4, 256)
        Bsz, Tlen, C = x.shape
        latent = x @ Wc_down
        q = (latent @ Wq_up).reshape(Bsz, Tlen, N_HEAD, HEAD_DIM)
        kv = latent @ Wkv_up
        k, v = (kv[..., :HEAD_DIM], kv[..., HEAD_DIM:])
        scale = 1.0 / np.sqrt(HEAD_DIM)
        att = jnp.einsum('bthd,bsd->bhts', q, k) * scale
        causal = jnp.tril(jnp.ones((Tlen, Tlen), dtype=bool))
        att = jnp.where(causal[None, None], att, -jnp.inf)
        att = jax.nn.softmax(att, axis=-1)
        y = jnp.einsum('bhts,bsd->bthd', att, v).reshape(Bsz, Tlen, C)
        return y @ Wc_proj

    def _L2_ffn_ref(x, Wqkv, q_scale, k_scale, Wo, ln_g, ln_b, W1, b1, W2, b2):
        import jax, jax.numpy as jnp
        import numpy as np
        DIM = 128
        DEPTH = 6
        HEADS = 16
        DIM_HEAD = 64
        WINDOW = 32
        INNER = HEADS * DIM_HEAD
        DIM_INNER = int(DIM * 4 * 2 / 3)
        QK_SCALE = 8.0

        def shift_tokens(t):
            a, s = jnp.split(t, 2, -1)
            s = jnp.pad(s, ((0, 0), (1, 0), (0, 0)))[:, :-1]
            return jnp.concatenate([a, s], -1)

        def l2norm(t):
            return t / jnp.maximum(jnp.linalg.norm(t, axis=-1, keepdims=True), 1e-12)

        def rotate_half(x):
            x1, x2 = jnp.split(x, 2, -1)
            return jnp.concatenate([-x2, x1], -1)

        def rotary_tables(n):
            half = jnp.arange(0, DIM_HEAD, 2, dtype=jnp.float32)
            inv_freq = 1.0 / 10000.0 ** (half / DIM_HEAD)
            t = jnp.arange(n, dtype=jnp.float32)
            freqs = t[:, None] * inv_freq[None, :]
            freqs = jnp.concatenate([freqs, freqs], -1)
            base_scale = (half + 0.4 * DIM_HEAD) / (1.4 * DIM_HEAD)
            power = (t - n // 2) / (WINDOW // 2)
            scale = base_scale[None, :] ** power[:, None]
            scale = jnp.concatenate([scale, scale], -1)
            return (freqs, scale)

        def local_attention(q, k, v):
            b, h, n, d = q.shape
            w = WINDOW
            nw = n // w
            bq = q.reshape(b, h, nw, w, d)
            bk = k.reshape(b, h, nw, w, d)
            bv = v.reshape(b, h, nw, w, d)

            def look(t):
                p = jnp.pad(t, ((0, 0), (0, 0), (1, 0), (0, 0), (0, 0)))
                return jnp.concatenate([p[:, :, :nw], p[:, :, 1:]], axis=3)
            bk2, bv2 = (look(bk), look(bv))
            seq = jnp.arange(n).reshape(nw, w)
            seq_p = jnp.pad(seq, ((1, 0), (0, 0)), constant_values=-1)
            jt = jnp.concatenate([seq_p[:nw], seq_p[1:]], axis=1)
            it = seq[:, :, None]
            jb = jt[:, None, :]
            mask = (it < jb) | (it > jb + w) | (jb == -1)
            sim = jnp.einsum('bhwie,bhwje->bhwij', bq, bk2) * QK_SCALE
            sim = jnp.where(mask, -jnp.finfo(sim.dtype).max, sim)
            attn = jax.nn.softmax(sim, -1)
            out = jnp.einsum('bhwij,bhwje->bhwie', attn, bv2)
            return out.reshape(b, h, n, d)

        def attn_layer(x, Wqkv, qs, ksc, Wo):
            b, n, _ = x.shape
            qkv = x @ Wqkv
            q, k, v = jnp.split(qkv, 3, -1)
            sh = lambda t: t.reshape(b, n, HEADS, DIM_HEAD).transpose(0, 2, 1, 3)
            q, k, v = (sh(q), sh(k), sh(v))
            q = l2norm(q) * qs
            k = l2norm(k) * ksc
            freqs, scale = rotary_tables(n)
            cos, sin = (jnp.cos(freqs), jnp.sin(freqs))
            q = q * cos * scale + rotate_half(q) * sin * scale
            inv = 1.0 / scale
            k = k * cos * inv + rotate_half(k) * sin * inv
            out = local_attention(q, k, v)
            out = out.transpose(0, 2, 1, 3).reshape(b, n, INNER)
            return out @ Wo

        def ffn_layer(x, g, bln, W1, b1, W2, b2):
            mu = x.mean(-1, keepdims=True)
            var = ((x - mu) ** 2).mean(-1, keepdims=True)
            xn = (x - mu) / jnp.sqrt(var + 1e-05) * g + bln
            hg = xn @ W1 + b1
            a, gate = jnp.split(hg, 2, -1)
            return a * jax.nn.gelu(gate, approximate=False) @ W2 + b2
        for i in range(DEPTH):
            x = attn_layer(shift_tokens(x), Wqkv[i], q_scale[i], k_scale[i], Wo[i]) + x
            x = ffn_layer(shift_tokens(x), ln_g[i], ln_b[i], W1[i], b1[i], W2[i], b2[i]) + x
        return x

    def _L3_attn_ref(x, gamma, beta, Wq, Wk, Wv, Wr, u_bias, v_bias, Wo, bo, rel_pos_emb):
        import jax, jax.numpy as jnp
        import numpy as np
        D_MODEL = 128
        NUM_HEADS = 16
        DEPTH = D_MODEL // NUM_HEADS
        MAX_LEN = 625
        EPS = 1e-06

        def _make_rel_pos_emb():
            pos = np.arange(-MAX_LEN, MAX_LEN + 1, dtype=np.float32)[:, None]
            dim = np.arange(D_MODEL, dtype=np.float32)[None, :]
            angle = pos / 1250 ** (2 * (dim // 2) / D_MODEL)
            pe = np.where(dim % 2 == 0, np.sin(angle), np.cos(angle)).astype(np.float32)
            return jnp.asarray(pe)

        def _rel_shift(x):
            B, H, L, _ = x.shape
            x_padded = jnp.pad(x, ((0, 0), (0, 0), (0, 0), (1, 0)))
            x_padded = x_padded.reshape(B, H, 2 * L, L)
            x_shifted = x_padded[:, :, 1:, :].reshape(B, H, L, 2 * L - 1)
            return x_shifted[:, :, :, :L]
        B, L, _ = x.shape
        mu = jnp.mean(x, axis=-1, keepdims=True)
        var = jnp.mean(jnp.square(x - mu), axis=-1, keepdims=True)
        xn = (x - mu) * jax.lax.rsqrt(var + EPS) * gamma + beta

        def heads(t):
            return t.reshape(B, L, NUM_HEADS, DEPTH).transpose(0, 2, 1, 3)
        q = heads(xn @ Wq)
        k = heads(xn @ Wk)
        v = heads(xn @ Wv)
        idx = jnp.arange(2 * L - 1) - (L - 1) + MAX_LEN
        r_emb = rel_pos_emb[idx]
        r = (r_emb @ Wr).reshape(2 * L - 1, NUM_HEADS, DEPTH).transpose(1, 0, 2)
        AC = jnp.einsum('bhld,bhmd->bhlm', q + u_bias[None, :, None, :], k)
        BD = jnp.einsum('bhld,hrd->bhlr', q + v_bias[None, :, None, :], r)
        score = (AC + _rel_shift(BD)) / jnp.sqrt(jnp.float32(DEPTH))
        attn = jax.nn.softmax(score, axis=-1)
        out = jnp.einsum('bhlm,bhmd->bhld', attn, v)
        out = out.transpose(0, 2, 1, 3).reshape(B, L, D_MODEL)
        return out @ Wo + bo

    def _L3_ffn_ref(x, gate_w, gate_up_w, down_w):
        import jax, jax.numpy as jnp
        import numpy as np
        FF_DIM = 256
        TOP_K = 2
        B, S, D = x.shape
        E = gate_up_w.shape[0]
        F = down_w.shape[1]
        x_flat = x.reshape(B * S, D)
        router_logits = x_flat @ gate_w
        router_probs = jax.nn.softmax(router_logits, axis=-1)
        top_k_probs, top_k_idx = jax.lax.top_k(router_probs, TOP_K)
        top_k_probs = top_k_probs / jnp.sum(top_k_probs, axis=-1, keepdims=True)
        gate_up = jnp.einsum('nd,edh->enh', x_flat, gate_up_w)
        gate_out = gate_up[..., :F]
        up_out = gate_up[..., F:]
        hidden = jax.nn.silu(gate_out) * up_out
        expert_out = jnp.einsum('enf,efd->end', hidden, down_w)
        out_t = jnp.transpose(expert_out, (1, 0, 2))
        sel = jnp.take_along_axis(out_t, top_k_idx[:, :, None], axis=1)
        output = jnp.sum(sel * top_k_probs[:, :, None], axis=1)
        return output.reshape(B, S, D)
    x = L0_attn_x
    xn = _layernorm(x, axis=-1)
    x = x + _L0_attn_ref(xn, L0_attn_norm_w, L0_attn_A_w, L0_attn_A_b, L0_attn_B_w, L0_attn_C_w, L0_attn_D_w, L0_attn_out_w, L0_attn_out_b) + _L0_ffn_ref(xn, L0_ffn_gate_w, L0_ffn_Wg, L0_ffn_Wu, L0_ffn_Wd, L0_ffn_Sg, L0_ffn_Su, L0_ffn_Sd)
    xn = _layernorm(x, axis=-1)
    x = x + _L1_attn_ref(xn, L1_attn_W_write, L1_attn_W_read, L1_attn_W_alpha, L1_attn_W_beta, L1_attn_A_log, L1_attn_dt_bias) + _L1_ffn_ref(xn, L1_ffn_wqkv, L1_ffn_q_scale, L1_ffn_k_scale, L1_ffn_wo, L1_ffn_ln_g, L1_ffn_ln_b, L1_ffn_w1, L1_ffn_b1, L1_ffn_w2, L1_ffn_b2)
    xn = _layernorm(x, axis=-1)
    x = x + _L2_attn_ref(xn, L2_attn_Wc_down, L2_attn_Wq_up, L2_attn_Wkv_up, L2_attn_Wc_proj) + _L2_ffn_ref(xn, L2_ffn_Wqkv, L2_ffn_q_scale, L2_ffn_k_scale, L2_ffn_Wo, L2_ffn_ln_g, L2_ffn_ln_b, L2_ffn_W1, L2_ffn_b1, L2_ffn_W2, L2_ffn_b2)
    xn = _layernorm(x, axis=-1)
    x = x + _L3_attn_ref(xn, L3_attn_gamma, L3_attn_beta, L3_attn_Wq, L3_attn_Wk, L3_attn_Wv, L3_attn_Wr, L3_attn_u_bias, L3_attn_v_bias, L3_attn_Wo, L3_attn_bo, L3_attn_rel_pos_emb) + _L3_ffn_ref(xn, L3_ffn_gate_w, L3_ffn_gate_up_w, L3_ffn_down_w)
    return x

_drawn_inputs = setup_inputs


def setup_inputs(seed=0):
    import zlib

    import numpy as np

    out = dict(_drawn_inputs(seed))
    spreads = {'L0_attn_norm_w': (1.0, 0.6),
     'L1_ffn_q_scale': (1.0, 0.6),
     'L1_ffn_k_scale': (1.0, 0.6),
     'L1_ffn_ln_g': (1.0, 0.6),
     'L1_ffn_ln_b': (0.0, 0.8),
     'L1_ffn_b1': (0.0, 0.8),
     'L1_ffn_b2': (0.0, 0.1),
     'L2_ffn_q_scale': (1.0, 0.6),
     'L2_ffn_k_scale': (1.0, 0.6),
     'L2_ffn_ln_g': (1.0, 0.6),
     'L2_ffn_ln_b': (0.0, 0.8),
     'L2_ffn_b1': (0.0, 0.8),
     'L2_ffn_b2': (0.0, 0.8),
     'L3_attn_gamma': (1.0, 0.6),
     'L3_attn_beta': (0.0, 2.0),
     'L3_attn_bo': (0.0, 2.0)}
    factors = {'L0_attn_A_w': 6.993,
     'L0_attn_A_b': 8.0,
     'L0_attn_C_w': 4.129,
     'L0_attn_D_w': 4.128,
     'L1_attn_W_write': 8.0,
     'L1_attn_W_read': 8.0,
     'L1_attn_W_alpha': 8.0,
     'L1_attn_W_beta': 8.0,
     'L1_ffn_wqkv': 6.763,
     'L1_ffn_wo': 6.785,
     'L1_ffn_w1': 8.0,
     'L1_ffn_w2': 8.0,
     'L2_attn_Wc_down': 8.0,
     'L2_attn_Wq_up': 8.0,
     'L2_attn_Wkv_up': 8.0,
     'L2_attn_Wc_proj': 8.0,
     'L2_ffn_W1': 8.0,
     'L2_ffn_W2': 8.0,
     'L3_attn_Wr': 26.316,
     'L3_attn_u_bias': 179.103,
     'L3_attn_v_bias': 64.0,
     'L3_attn_rel_pos_emb': 25.746,
     'L3_ffn_gate_w': 64.0,
     'L3_ffn_gate_up_w': 64.0,
     'L3_ffn_down_w': 64.0,
     'L3_attn_Wq': 7.563,
     'L3_attn_Wk': 8.0,
     'L3_attn_Wv': 5.308,
     'L3_attn_Wo': 5.357}
    for name, (base, spread) in spreads.items():
        noise = np.random.default_rng([zlib.crc32(name.encode()), seed]).standard_normal(out[name].shape)
        drawn = base * np.exp(spread * noise) if base else spread * noise
        out[name] = jnp.asarray(drawn.astype(out[name].dtype))
    for name, factor in factors.items():
        out[name] = (out[name] * factor).astype(out[name].dtype)
    return out
```

```python
from contextlib import ExitStack

import numpy as np

import concourse.bass as bass
from concourse import mybir
from concourse.alu_op_type import AluOpType as ALU

F32 = mybir.dt.float32
ACT = mybir.ActivationFunctionType
AX = mybir.AxisListType

P = 128
BATCH, LEN, DIM = 8, 256, 128
TOK = BATCH * LEN
BANK = 512
CH = TOK // BANK
TILES = TOK // P
HIDDEN = 384
NEG = -1.0e30


class Core:

    def __init__(self, nc, ctx, dram):
        self.nc, self.ctx, self.dram = nc, ctx, dram
        self.psum = ctx.enter_context(nc.psum_tensor("psum", [P, 8, BANK], F32))
        self.x, self.xn, self.y, self.h = (
            ctx.enter_context(nc.sbuf_tensor("stream_" + n, [P, TOK], F32)) for n in ("x", "xn", "y", "h"))
        self.c = {}

    def keep(self, name, shape):
        self.c[name] = self.ctx.enter_context(self.nc.sbuf_tensor("c_" + name, shape, F32))
        return self.c[name]


class Stage:

    count = 0

    def __init__(self, core):
        self.nc, self.core = core.nc, core
        self.ctx = ExitStack()
        self.sems = {}
        Stage.count += 1
        self.tag = f"s{Stage.count}"

    def __enter__(self):
        return self

    def __exit__(self, *args):
        self.ctx.close()

    def sb(self, name, shape):
        return self.ctx.enter_context(self.nc.sbuf_tensor(f"{self.tag}_{name}", shape, F32))

    def sem(self, name):
        if name not in self.sems:
            self.sems[name] = self.ctx.enter_context(self.nc.semaphore(f"{self.tag}_{name}"))
        return self.sems[name]

    def block(self):
        return self.nc.Block(no_gpsimd_drain=True)

    def clear(self):
        nums = sorted(s.num for s in self.sems.values())
        first = last = nums[0]
        for n in nums[1:] + [None]:
            if n != last + 1:
                self.nc.gpsimd.sem_clear(range(first, last + 1))
                first = n
            last = n
        self.nc.all_engine_barrier(sem_only=True)


def cols(i, width, size=None):
    return bass.ds(i * width, size or width)


def over(ap, *dims):
    return bass.AP(ap.tensor, ap.offset, [list(ap.ap[0])] + [list(d) for d in dims])


def load_constants(core, names):
    with Stage(core) as st:
        bufs = [(core.keep(n, list(core.dram[n].shape)), core.dram[n]) for n in names]
        with st.block() as block:
            @block.sync
            def _(sp):
                for buf, src in bufs[0::2]:
                    sp.dma_start(buf[:], src).then_inc(st.sem("loaded_sp"), 16)
                sp.wait_ge(st.sem("loaded_sp"), 16 * len(bufs[0::2]))

            @block.scalar
            def _(act):
                for buf, src in bufs[1::2]:
                    act.dma_start(buf[:], src).then_inc(st.sem("loaded_act"), 16)
                act.wait_ge(st.sem("loaded_act"), 16 * len(bufs[1::2]))
        st.clear()


def load_stream(core):
    nc, psum = core.nc, core.psum
    with Stage(core) as st:
        sem = st.sem
        rows = st.sb("rows", [P, TILES, P])
        with st.block() as block:
            @block.sync
            def _(sp):
                for c in range(CH):
                    src = core.dram["x"].rearrange("(t p) d -> p t d", p=P)[:, 4 * c:4 * c + 4, :]
                    sp.dma_start(rows[:, 4 * c:4 * c + 4, :], src).then_inc(sem(f"rows{c}"), 16)

            @block.tensor
            def _(pe):
                for t in range(TILES):
                    if t % 4 == 0:
                        pe.wait_ge(sem(f"rows{t // 4}"), 16)
                    pe.transpose(psum[:, t // 4, cols(t % 4, P)], rows[:, t, :],
                                 core.c["ident"][:, :]).then_inc(sem("turned"), 1)

            @block.vector
            def _(dve):
                for c in range(CH):
                    dve.wait_ge(sem("turned"), 4 * c + 4)
                    dve.tensor_copy(core.x[:, cols(c, BANK)], psum[:, c, :]).then_inc(sem("copied"), 1)
        st.clear()


def store_stream(core, src, out):
    nc, psum = core.nc, core.psum
    with Stage(core) as st:
        sem = st.sem
        rows = st.sb("rows", [P, TILES, P])
        with st.block() as block:
            @block.tensor
            def _(pe):
                for t in range(TILES):
                    pe.transpose(psum[:, t // 4, cols(t % 4, P)], src[:, cols(t, P)],
                                 core.c["ident"][:, :]).then_inc(sem("turned"), 1)

            @block.vector
            def _(dve):
                for c in range(CH):
                    dve.wait_ge(sem("turned"), 4 * c + 4)
                    dve.tensor_copy(rows[:, 4 * c:4 * c + 4, :],
                                    psum[:, c, :].rearrange("p (t d) -> p t d", t=4)).then_inc(sem("copied"), 1)

            @block.sync
            def _(sp):
                for c in range(CH):
                    sp.wait_ge(sem("copied"), c + 1)
                    dst = out.rearrange("(t p) d -> p t d", p=P)[:, 4 * c:4 * c + 4, :]
                    sp.dma_start(dst, rows[:, 4 * c:4 * c + 4, :]).then_inc(sem("stored"), 16)
                sp.wait_ge(sem("stored"), 16 * CH)
        st.clear()


def layernorm(core, src, dst, eps, gain=None, bias=None, shift=False):
    nc, psum = core.nc, core.psum
    with Stage(core) as st:
        sem = st.sem
        sq = st.sb("sq", [P, CH, BANK])
        std = st.sb("std", [P, CH, BANK])
        shifted = st.sb("shifted", [P, TOK]) if shift else None
        x = shifted if shift else src
        half = P // 2
        with st.block() as block:
            @block.tensor
            def _(pe):
                for c in range(CH):
                    if shift:
                        pe.wait_ge(sem("shifted"), c + 1)
                        pe.wait_ge(sem("kept"), c + 1)
                    pe.matmul(psum[:, c, :], core.c["mean"][:, :], x[:, cols(c, BANK)],
                              start=True, stop=True).then_inc(sem("mean"), 1)
                for c in range(CH):
                    pe.wait_ge(sem("squared"), c + 1)
                    pe.matmul(psum[:, 4 + c, :], core.c["mean"][:, :], sq[:, c, :],
                              start=True, stop=True).then_inc(sem("var"), 1)

            @block.vector
            def _(dve):
                for c in range(CH):
                    if shift:
                        two = shifted[half:, cols(c, BANK)].rearrange("p (b t) -> p b t", b=2)
                        of = src[half:, cols(c, BANK)].rearrange("p (b t) -> p b t", b=2)
                        dve.memset(two[:, :, 0:1], 0.0)
                        dve.tensor_copy(two[:, :, 1:LEN], of[:, :, 0:LEN - 1]).then_inc(sem("shifted"), 1)
                if shift:
                    dve.wait_ge(sem("shifted"), CH)
                for c in range(CH):
                    if shift:
                        dve.wait_ge(sem("kept"), c + 1)
                    dve.wait_ge(sem("mean"), c + 1)
                    dve.tensor_tensor(dst[:, cols(c, BANK)], x[:, cols(c, BANK)], psum[:, c, :],
                                      ALU.subtract).then_inc(sem("centred"), 1)
                for c in range(CH):
                    dve.wait_ge(sem("centred"), CH)
                    dve.wait_ge(sem("std"), c + 1)
                    dve.reciprocal(std[:, c, :], std[:, c, :]).then_inc(sem("inverse"), 1)
                for c in range(CH):
                    dve.wait_ge(sem("inverse"), c + 1)
                    dve.tensor_tensor(dst[:, cols(c, BANK)], dst[:, cols(c, BANK)], std[:, c, :],
                                      ALU.mult).then_inc(sem("normed"), 1)
                if gain is not None:
                    for c in range(CH):
                        dve.wait_ge(sem("normed"), c + 1)
                        dve.tensor_scalar(dst[:, cols(c, BANK)], dst[:, cols(c, BANK)], gain, bias,
                                          ALU.mult, ALU.add).then_inc(sem("scaled"), 1)

            @block.scalar
            def _(act):
                if shift:
                    for c in range(CH):
                        act.activation(shifted[0:half, cols(c, BANK)], src[0:half, cols(c, BANK)],
                                       ACT.Copy).then_inc(sem("kept"), 1)
                for c in range(CH):
                    act.wait_ge(sem("centred"), c + 1)
                    act.activation(sq[:, c, :], dst[:, cols(c, BANK)], ACT.Square).then_inc(sem("squared"), 1)
                for c in range(CH):
                    act.wait_ge(sem("var"), c + 1)
                    act.activation(std[:, c, :], psum[:, 4 + c, :], ACT.Sqrt,
                                   bias=core.c["small"][:, eps:eps + 1]).then_inc(sem("std"), 1)
        st.clear()


def gated_scan(core):
    nc, psum = core.nc, core.psum
    with Stage(core) as st:
        sem = st.sem
        names = ("sq", "rms", "xr", "a", "c", "d", "db", "h", "part")
        sq, rms, xr, a, c, d, db, h, part = (st.sb(n, [P, BANK]) for n in names)
        w = core.c["l0_w"]
        A_b, out_b, norm_w = (core.c["l0_cols"][:, i:i + 1] for i in range(3))
        with nc.Fori(0, CH) as g:
            with st.block() as block:
                @block.scalar
                def _(act):
                    act.activation(sq[:, :], core.xn[:, cols(g, BANK)], ACT.Square).then_inc(sem("squared"), 1)
                    act.wait_ge(sem("mean_square"), 1)
                    act.activation(rms[:, :], psum[:, 0, :], ACT.Sqrt,
                                   bias=core.c["small"][:, 0:1]).then_inc(sem("rms"), 1)
                    act.wait_ge(sem("products"), 1)
                    act.activation(a[:, :], psum[:, 1, :], ACT.Sigmoid, bias=A_b).then_inc(sem("gates"), 1)
                    act.wait_ge(sem("products"), 3)
                    act.activation(d[:, :], psum[:, 3, :], ACT.Sigmoid).then_inc(sem("gates"), 1)
                    act.wait_ge(sem("products"), 4)
                    act.activation(c[:, :], psum[:, 4, :], ACT.Sigmoid).then_inc(sem("gates"), 1)

                @block.tensor
                def _(pe):
                    pe.wait_ge(sem("squared"), 1)
                    pe.matmul(psum[:, 0, :], core.c["mean"][:, :], sq[:, :], start=True,
                              stop=True).then_inc(sem("mean_square"), 1)
                    pe.wait_ge(sem("rms_normed"), 1)
                    for i, k in enumerate((0, 1, 3, 2)):
                        pe.matmul(psum[:, 1 + i, :], w[:, k, :], xr[:, :], start=True,
                                  stop=True).then_inc(sem("products"), 1)
                    pe.wait_ge(sem("gated"), 1)
                    pe.matmul(psum[:, 5, :], w[:, 4, :], h[:, :], start=True, stop=True).then_inc(sem("out"), 1)

                @block.vector
                def _(dve):
                    dve.wait_ge(sem("rms"), 1)
                    dve.reciprocal(rms[:, :], rms[:, :]).then_inc(sem("inverse_rms"), 1)
                    dve.wait_ge(sem("inverse_rms"), 1)
                    dve.scalar_tensor_tensor(xr[:, :], core.xn[:, cols(g, BANK)], norm_w, rms[:, :],
                                             ALU.mult, ALU.mult).then_inc(sem("rms_normed"), 1)
                    dve.wait_ge(sem("gates"), 2)
                    dve.wait_ge(sem("products"), 2)
                    dve.tensor_tensor(db[:, :], d[:, :], psum[:, 2, :], ALU.mult).then_inc(sem("db"), 1)
                    dve.wait_ge(sem("db"), 1)
                    for b in range(BANK // LEN):
                        dve.tensor_tensor_scan(part[:, cols(b, LEN)], a[:, cols(b, LEN)], db[:, cols(b, LEN)],
                                               0.0, ALU.mult, ALU.add).then_inc(sem("scanned"), 1)
                    dve.wait_ge(sem("scanned"), 2)
                    dve.wait_ge(sem("gates"), 3)
                    dve.tensor_tensor(h[:, :], part[:, :], c[:, :], ALU.mult).then_inc(sem("gated"), 1)
                    dve.wait_ge(sem("gated"), 1)
                    dve.tensor_tensor(db[:, :], core.x[:, cols(g, BANK)], core.xn[:, cols(g, BANK)],
                                      ALU.add).then_inc(sem("residual"), 1)
                    dve.wait_ge(sem("residual"), 1)
                    dve.wait_ge(sem("out"), 1)
                    dve.scalar_tensor_tensor(core.x[:, cols(g, BANK)], psum[:, 5, :], out_b, db[:, :],
                                             ALU.add, ALU.add).then_inc(sem("done"), 1)
            st.clear()


def experts(core, level, n_exp, hidden, softmax_first, shared):
    nc, psum, dram = core.nc, core.psum, core.dram
    nic = hidden // P
    wg_d, wu_d, wd_d = (dram[f"{level}_{n}"] for n in ("wg", "wu", "wd"))
    with Stage(core) as st:
        sem = st.sem
        gate_w = core.c[level + "_gate"]
        E = n_exp
        logits = st.sb("logits", [P, TILES, E])
        comb = st.sb("comb", [P, TILES, E])
        top = st.sb("top", [P, TILES])
        total = st.sb("total", [P, TILES])
        gt = st.sb("gt", [P, TILES, E, E])
        eq = st.sb("eq", [P, TILES, E, E])
        rank = st.sb("rank", [P, TILES, E])
        combT = st.sb("combT", [E, TOK])
        mine = (lambda t: t[:, :, :].unsqueeze(3).to_broadcast([P, TILES, E, E]))
        with st.block() as block:
            @block.tensor
            def _(pe):
                for t in range(TILES):
                    mm = pe.matmul(psum[:, 0, cols(t, E)], core.xn[:, cols(t, P)], gate_w[:, :],
                                   start=True, stop=True)
                mm.then_inc(sem("logits"), 1)
                pe.wait_ge(sem("weights"), 1)
                for t in range(TILES):
                    mm = pe.transpose(psum[0:E, 4 + t // 4, cols(t % 4, P)], comb[:, t, :], core.c["ident"][:, :])
                mm.then_inc(sem("turned"), 1)

            @block.vector
            def _(dve):
                step = [0]

                def chained(ins):
                    step[0] += 1
                    ins.then_inc(sem("vector_step"), 1)
                    dve.wait_ge(sem("vector_step"), step[0])

                dve.wait_ge(sem("logits"), 1)
                chained(dve.tensor_copy(logits[:, :, :], psum[:, 0, 0:TILES * E].rearrange("p (t e) -> p t e", e=E)))
                chained(dve.tensor_reduce(top[:, :], logits[:, :, :], AX.X, ALU.max))
                dve.tensor_tensor(comb[:, :, :], logits[:, :, :],
                                  over(top[:, :], [1, TILES], [0, E]), ALU.subtract).then_inc(sem("less_top"), 1)
                dve.wait_ge(sem("exp"), 1)
                if softmax_first:
                    chained(dve.tensor_reduce(total[:, :], comb[:, :, :], AX.X, ALU.add))
                    chained(dve.reciprocal(total[:, :], total[:, :]))
                    chained(dve.tensor_tensor(comb[:, :, :], comb[:, :, :],
                                              over(total[:, :], [1, TILES], [0, E]), ALU.mult))
                    chained(dve.tensor_copy(logits[:, :, :], comb[:, :, :]))
                e_ap = over(logits[:, :, :], [E, TILES], [1, E], [0, E])
                f_ap = over(logits[:, :, :], [E, TILES], [0, E], [1, E])
                chained(dve.tensor_tensor(gt[:, :, :, :], f_ap, e_ap, ALU.is_gt))
                chained(dve.tensor_tensor(eq[:, :, :, :], f_ap, e_ap, ALU.is_equal))
                chained(dve.tensor_tensor(eq[:, :, :, :].rearrange("p t e f -> p t (e f)"),
                                          eq[:, :, :, :].rearrange("p t e f -> p t (e f)"),
                                          over(core.c["below"][:, :], [0, TILES], [1, E * E]), ALU.mult))
                chained(dve.tensor_tensor(gt[:, :, :, :], gt[:, :, :, :], eq[:, :, :, :], ALU.add))
                chained(dve.tensor_reduce(rank[:, :, :], gt[:, :, :, :], AX.X, ALU.add))
                chained(dve.tensor_scalar(rank[:, :, :], rank[:, :, :], 1.5, None, ALU.is_lt))
                chained(dve.tensor_tensor(comb[:, :, :], comb[:, :, :], rank[:, :, :], ALU.mult))
                chained(dve.tensor_reduce(total[:, :], comb[:, :, :], AX.X, ALU.add))
                chained(dve.reciprocal(total[:, :], total[:, :]))
                dve.tensor_tensor(comb[:, :, :], comb[:, :, :], over(total[:, :], [1, TILES], [0, E]),
                                  ALU.mult).then_inc(sem("weights"), 1)
                dve.wait_ge(sem("turned"), 1)
                dve.tensor_copy(combT[:, :], psum[0:E, 4:8, :].rearrange("p b n -> p (b n)")).then_inc(sem("combT"), 1)

            @block.scalar
            def _(act):
                act.wait_ge(sem("less_top"), 1)
                act.activation(comb[:, :, :], comb[:, :, :], ACT.Exp).then_inc(sem("exp"), 1)

            @block.sync
            def _(sp):
                sp.wait_ge(sem("combT"), 1)
                sp.dma_start(core.comb_d, combT[:, :]).then_inc(sem("stored"), 16)
                sp.wait_ge(sem("stored"), 16)
        st.clear()

    with Stage(core) as st:
        sem = st.sem
        sg = st.sb("sg", [P, 2, BANK])
        hid = st.sb("hid", [P, 2, BANK])
        wg = st.sb("wg", [P, 2, hidden])
        wu = st.sb("wu", [P, 2, hidden])
        wd = st.sb("wd", [P, 2, nic, DIM])
        cb = st.sb("cb", [P, 2, TOK])
        xc = st.sb("xc", [P, 2, BANK])

        def run(block, jobs, weigh, first):
            steps = [(j, buf, c, ic) for j, (buf, n) in enumerate(jobs) for c in range(CH) for ic in range(n)]
            units = [(j, buf, c) for j, (buf, n) in enumerate(jobs) for c in range(CH)]

            @block.tensor
            def _(pe):
                if first:
                    for c in range(CH):
                        pe.matmul(psum[:, 4 + c, :], core.c["ident"][:, :], core.x[:, cols(c, BANK)],
                                  start=True, stop=False, skip_group_check=True)

                def up(k):
                    j, buf, c, ic = steps[k]
                    if c == 0 and ic == 0:
                        pe.wait_ge(sem(f"w{j}"), 32)
                    rhs = core.xn[:, cols(c, BANK)]
                    if k >= 2:
                        pe.wait_ge(sem("hidden"), k - 1)
                    pe.matmul(psum[:, k % 2, :], wg[:, buf, cols(ic, P)], rhs, start=True,
                              stop=True).then_inc(sem("gate"), 1)
                    if weigh:
                        pe.wait_ge(sem("weighed"), units.index((j, buf, c)) + 1)
                        rhs = xc[:, units.index((j, buf, c)) % 2, :]
                    pe.matmul(psum[:, 2 + k % 2, :], wu[:, buf, cols(ic, P)], rhs, start=True,
                              stop=True).then_inc(sem("up"), 1)

                def down(k):
                    j, buf, c, ic = steps[k]
                    if c == 0 and ic == 0:
                        pe.wait_ge(sem(f"wd{j}"), 16)
                    pe.wait_ge(sem("hidden"), k + 1)
                    pe.matmul(psum[:, 4 + c, :], wd[:, buf, ic, :], hid[:, k % 2, :], start=False,
                              stop=False, skip_group_check=True).then_inc(sem("down"), 1)

                up(0)
                for k in range(len(steps)):
                    if k + 1 < len(steps):
                        up(k + 1)
                    down(k)

            @block.scalar
            def _(act):
                for k in range(len(steps)):
                    act.wait_ge(sem("gate"), k + 1)
                    if k >= 2:
                        act.wait_ge(sem("hidden"), k - 1)
                    act.activation(sg[:, k % 2, :], psum[:, k % 2, :], ACT.Silu).then_inc(sem("silu"), 1)

            @block.vector
            def _(dve):
                done = [0]

                def weigh_chunk(u):
                    j, buf, c = units[u]
                    if c == 0:
                        dve.wait_ge(sem(f"cb{j}"), 16)
                    if u >= 2:
                        before = sum(1 for s in steps if units.index(s[:3]) <= u - 2)
                        dve.wait_ge(sem("up"), before)
                    dve.tensor_tensor(xc[:, u % 2, :], core.xn[:, cols(c, BANK)], cb[:, buf, cols(c, BANK)],
                                      ALU.mult).then_inc(sem("weighed"), 1)
                if weigh:
                    weigh_chunk(0)
                for k in range(len(steps)):
                    j, buf, c, ic = steps[k]
                    if weigh and ic == 0 and units.index((j, buf, c)) + 1 < len(units):
                        weigh_chunk(units.index((j, buf, c)) + 1)
                    dve.wait_ge(sem("silu"), k + 1)
                    dve.wait_ge(sem("up"), k + 1)
                    if k >= 2:
                        dve.wait_ge(sem("down"), k - 1)
                    dve.tensor_tensor(hid[:, k % 2, :], sg[:, k % 2, :], psum[:, 2 + k % 2, :],
                                      ALU.mult).then_inc(sem("hidden"), 1)

        def load(q, buf, e, j):
            q.dma_start(wg[:, buf, :], wg_d[e, :, :].rearrange("a p n -> p (a n)")).then_inc(sem(f"w{j}"), 16)
            q.dma_start(wu[:, buf, :], wu_d[e, :, :].rearrange("a p n -> p (a n)")).then_inc(sem(f"w{j}"), 16)
            q.dma_start(wd[:, buf, :, :], wd_d[e, :, :].rearrange("a (c p) n -> p (a c) n", p=P)).then_inc(sem(f"wd{j}"), 16)

        with st.block() as block:
            if shared:
                run(block, [(0, dram[shared + "_wg"].shape[1] // P)], False, True)
            else:
                @block.tensor
                def _(pe):
                    for c in range(CH):
                        mm = pe.matmul(psum[:, 4 + c, :], core.c["ident"][:, :], core.x[:, cols(c, BANK)],
                                       start=True, stop=False, skip_group_check=True)
                    mm.then_inc(sem("opened"), 1)

            @block.sync
            def _(sp):
                if shared:
                    n = dram[shared + "_wg"].shape[1]
                    sp.dma_start(wg[:, 0, 0:n], dram[shared + "_wg"]).then_inc(sem("w0"), 16)
                    sp.dma_start(wu[:, 0, 0:n], dram[shared + "_wu"]).then_inc(sem("w0"), 16)
                    sp.dma_start(wd[:, 0, 0:n // P, :],
                                 dram[shared + "_wd"].rearrange("(c p) n -> p c n", p=P)).then_inc(sem("wd0"), 16)
        st.clear()
        with nc.Fori(0, n_exp // 2) as pair:
            with st.block() as block:
                run(block, [(0, nic), (1, nic)], True, False)

                @block.sync
                def _(sp):
                    for j in range(2):
                        load(sp, j, bass.ds(pair * 2 + j, 1), j)
                        sp.dma_start(cb[:, j, :], core.comb_d[bass.ds(pair * 2 + j, 1), :].partition_broadcast(P)
                                     ).then_inc(sem(f"cb{j}"), 16)
            st.clear()
        with st.block() as block:
            @block.vector
            def _(dve):
                for c in range(CH):
                    dve.tensor_copy(core.x[:, cols(c, BANK)], psum[:, 4 + c, :]).then_inc(sem("copied"), 1)
        st.clear()


def delta_rule(core):
    nc, psum = core.nc, core.psum
    C = 64
    NC = BANK // C
    NT = BANK // P
    with Stage(core) as st:
        sem = st.sem
        wide = lambda n: st.sb(n, [P, NT, P])
        flat = lambda t: t[:, :, :].rearrange("p t n -> p (t n)")
        bank = lambda i: psum[:, i, :].rearrange("p (t n) -> p t n", t=NT)
        sq, norm, rk, wk, beta, z, soft, cum, dec, tail = (
            wide(n) for n in ("sq", "norm", "rk", "wk", "beta", "z", "soft", "cum", "dec", "tail"))
        wks, wkd, wkt, rkd, xb, ncum = (wide(n) for n in ("wks", "wkd", "wkt", "rkd", "xb", "ncum"))
        LT, T, N, TD, ND, TO, NO, intraT = (wide(n) for n in ("LT", "T", "N", "TD", "ND", "TO", "NO", "intraT"))
        T2, N2, T4, N4, N8, X1, X2, X3, X4 = (wide(n) for n in ("T2", "N2", "T4", "N4", "N8", "X1", "X2", "X3", "X4"))
        Q, QT, Z1, Z2, PP, R = (wide(n) for n in ("Q", "QT", "Z1", "Z2", "PP", "R"))
        wkd_t, wkt_t, vsc, U, WT, vn, oT = (wide(n) for n in ("wkd_t", "wkt_t", "vsc", "U", "WT", "vn", "oT"))
        S = st.sb("S", [P, 2, P])
        neg_a = st.sb("neg_a", [P, 1])
        dt_bias = core.c["l1_scal"][:, 1:2]
        ident4 = over(core.c["ident"][:, :], [0, NT], [1, P])
        with st.block() as block:
            @block.scalar
            def _(act):
                act.activation(neg_a[:, :], core.c["l1_scal"][:, 0:1], ACT.Exp).then_inc(sem("exp_a"), 1)

            @block.vector
            def _(dve):
                dve.wait_ge(sem("exp_a"), 1)
                dve.tensor_scalar(neg_a[:, :], neg_a[:, :], -1.0, None, ALU.mult).then_inc(sem("neg_a"), 1)
        st.clear()
        with nc.Fori(0, CH) as g:
            with st.block() as block:
                x_g = core.xn[:, cols(g, BANK)]

                @block.scalar
                def _(act):
                    act.activation(flat(sq), x_g, ACT.Square).then_inc(sem("squared"), 1)
                    act.wait_ge(sem("mean_square"), 1)
                    act.activation(flat(norm), psum[:, 0, :], ACT.Sqrt, scale=float(P)).then_inc(sem("norm"), 1)
                    act.wait_ge(sem("beta_logit"), 1)
                    act.activation(flat(beta), psum[:, 1, :], ACT.Exp, scale=-1.0).then_inc(sem("beta_exp"), 1)
                    act.wait_ge(sem("abs_z"), 1)
                    act.activation(flat(soft), flat(soft), ACT.Exp, scale=-1.0).then_inc(sem("exp_z"), 1)
                    act.wait_ge(sem("exp_z"), 1)
                    act.activation(flat(soft), flat(soft), ACT.Ln, bias=core.c["small"][:, 2:3]).then_inc(sem("ln_z"), 1)
                    act.wait_ge(sem("cum"), 1)
                    act.activation(flat(dec), flat(cum), ACT.Exp).then_inc(sem("dec"), 1)
                    act.wait_ge(sem("to_end"), 1)
                    act.activation(flat(tail), flat(tail), ACT.Exp).then_inc(sem("tail"), 1)
                    act.wait_ge(sem("masked"), 1)
                    act.activation(flat(LT), flat(LT), ACT.Exp).then_inc(sem("LT"), 1)
                    act.wait_ge(sem("N_turned"), 1)
                    act.activation(flat(N), psum[:, 6, :], ACT.Copy).then_inc(sem("N"), 1)
                    act.wait_ge(sem("T2"), 1)
                    act.activation(flat(T2), psum[:, 0, :], ACT.Copy).then_inc(sem("T2_kept"), 1)
                    act.wait_ge(sem("T4"), 1)
                    act.activation(flat(T4), psum[:, 2, :], ACT.Copy).then_inc(sem("T4_kept"), 1)
                    for i, (buf, b) in enumerate(((wkd_t, 6), (wkt_t, 7), (vsc, 3))):
                        act.wait_ge(sem("token_major"), i + 1)
                        act.activation(flat(buf), psum[:, b, :], ACT.Copy).then_inc(sem("token_major_kept"), 1)
                    act.wait_ge(sem("N8"), 1)
                    act.activation(flat(N8), psum[:, 4, :], ACT.Copy).then_inc(sem("N8_kept"), 1)
                    act.wait_ge(sem("QT"), 1)
                    act.activation(flat(QT), psum[:, 3, :], ACT.Copy).then_inc(sem("QT_kept"), 1)
                    act.wait_ge(sem("P_turned"), 1)
                    act.activation(flat(PP), psum[:, 4, :], ACT.Copy).then_inc(sem("P_kept"), 1)
                    act.wait_ge(sem("WT"), 1)
                    act.activation(flat(WT), psum[:, 1, :], ACT.Copy).then_inc(sem("WT_kept"), 1)

                @block.tensor
                def _(pe):
                    def tiles(b, lhsT, rhs, name, turn=False):
                        for t in range(NT):
                            if turn:
                                mm = pe.transpose(bank(b)[:, t, :], lhsT[:, t, :], core.c["ident"][:, :])
                            else:
                                mm = pe.matmul(bank(b)[:, t, :], lhsT[:, t, :], rhs[:, t, :], start=True, stop=True)
                        mm.then_inc(sem(name), 1)

                    pe.matmul(psum[:, 1, :], core.c["l1_rows"][:, 0, :], x_g, start=True, stop=True).then_inc(sem("beta_logit"), 1)
                    pe.matmul(psum[:, 2, :], core.c["l1_rows"][:, 1, :], x_g, start=True, stop=True).then_inc(sem("alpha_logit"), 1)
                    pe.wait_ge(sem("squared"), 1)
                    pe.matmul(psum[:, 0, :], core.c["mean"][:, :], flat(sq), start=True, stop=True).then_inc(sem("mean_square"), 1)
                    pe.wait_ge(sem("neg_cum"), 1)
                    for t in range(NT):
                        pe.matmul(bank(3)[:, t, :], core.c["ones"][0:1, :], cum[0:1, t, :], start=True, stop=False)
                        mm = pe.matmul(bank(3)[:, t, :], ncum[0:1, t, :], core.c["ones"][0:1, :], start=False, stop=True)
                    mm.then_inc(sem("cum_diff"), 1)
                    pe.wait_ge(sem("wks"), 1)
                    tiles(4, wk, wks, "gram")
                    tiles(5, wk, rk, "reads")
                    pe.wait_ge(sem("T"), 1)
                    tiles(6, T, None, "N_turned", turn=True)
                    pe.wait_ge(sem("NO"), 1)
                    tiles(0, ND, TD, "T2")
                    tiles(1, TD, ND, "N2")
                    pe.wait_ge(sem("N2_kept"), 1)
                    pe.wait_ge(sem("T2_kept"), 1)
                    tiles(2, N2, T2, "T4")
                    pe.wait_ge(sem("N"), 1)
                    tiles(5, T2, N2, "N4")
                    tiles(1, N2, X1, "X2")
                    pe.wait_ge(sem("scaled"), 1)
                    tiles(6, wkd, None, "token_major", turn=True)
                    tiles(7, wkt, None, "token_major", turn=True)
                    for t in range(NT):
                        mm = pe.matmul(bank(3)[:, t, :], xb[:, t, :], core.c["l1_w"][:, 0, :], start=True, stop=True)
                    mm.then_inc(sem("token_major"), 1)
                    pe.wait_ge(sem("N4_kept"), 1)
                    pe.wait_ge(sem("T4_kept"), 1)
                    tiles(4, T4, N4, "N8")
                    pe.wait_ge(sem("X2_kept"), 1)
                    tiles(0, N4, X2, "X3")
                    pe.wait_ge(sem("X3_kept"), 1)
                    pe.wait_ge(sem("N8_kept"), 1)
                    tiles(1, N8, X3, "X4")
                    pe.wait_ge(sem("X4_kept"), 1)
                    tiles(2, NO, X4, "Q")
                    pe.wait_ge(sem("token_major_kept"), 3)
                    tiles(3, X4, NO, "QT")
                    tiles(4, X4, None, "P_turned", turn=True)
                    pe.wait_ge(sem("QT_kept"), 1)
                    pe.wait_ge(sem("Q_kept"), 1)
                    tiles(5, QT, Q, "Q2")
                    pe.wait_ge(sem("Z1_kept"), 1)
                    tiles(6, QT, Z1, "Z2")
                    pe.wait_ge(sem("P_kept"), 1)
                    pe.wait_ge(sem("Z2_kept"), 1)
                    tiles(7, PP, Z2, "R")
                    pe.wait_ge(sem("R_kept"), 1)
                    tiles(0, R, vsc, "U")
                    tiles(1, wkd_t, R, "WT")
                    done = 0
                    for c in range(4):
                        for b in range(2):
                            t, lo = 2 * b + c // 2, (c % 2) * C
                            half = slice(lo, lo + C)
                            if c > 0:
                                pe.wait_ge(sem("WT_kept"), 1)
                                pe.wait_ge(sem("state"), 2 * (c - 1) + b + 1)
                                pe.matmul(psum[half, 2 + b, 0:P], WT[:, t, half], S[:, b, :],
                                          start=True, stop=True).then_inc(sem("read"), 1)
                        for b in range(2):
                            t, lo = 2 * b + c // 2, (c % 2) * C
                            half = slice(lo, lo + C)
                            if c > 0:
                                pe.matmul(psum[:, 4 + b, cols(c, C)], S[:, b, :], rkd[:, t, half],
                                          start=True, stop=False)
                            pe.wait_ge(sem("v_new"), 2 * c + b + 1)
                            mm = pe.matmul(psum[:, 4 + b, cols(c, C)], vn[half, t, :], intraT[half, t, half],
                                           start=(c == 0), stop=True)
                            if c == 3:
                                mm.then_inc(sem("outputs"), 1)
                            if c < 3:
                                mm = pe.matmul(psum[:, 6 + b, 0:P], wkt_t[half, t, :], vn[half, t, :],
                                               start=True, stop=True)
                                mm.then_inc(sem("write"), 1)
                    pe.wait_ge(sem("oT"), 1)
                    pe.matmul(psum[:, 0, :], core.c["l1_w"][:, 1, :], flat(oT), start=True, stop=True).then_inc(sem("projected"), 1)

                @block.vector
                def _(dve):
                    def keep(buf, b, name, wait):
                        dve.wait_ge(sem(wait), 1)
                        dve.tensor_copy(flat(buf), psum[:, b, :]).then_inc(sem(name), 1)

                    dve.wait_ge(sem("norm"), 1)
                    dve.tensor_scalar(flat(norm), flat(norm), 1e-12, None, ALU.max).then_inc(sem("guarded"), 1)
                    dve.wait_ge(sem("guarded"), 1)
                    dve.reciprocal(flat(norm), flat(norm)).then_inc(sem("inverse"), 1)
                    dve.wait_ge(sem("inverse"), 1)
                    dve.tensor_tensor(flat(rk), x_g, flat(norm), ALU.mult).then_inc(sem("rk"), 1)
                    dve.wait_ge(sem("rk"), 1)
                    wk2 = flat(wk).rearrange("p (b t) -> p b t", b=2)
                    rk2 = flat(rk).rearrange("p (b t) -> p b t", b=2)
                    dve.memset(wk2[:, :, 0:1], 0.0).then_inc(sem("wk"), 1)
                    dve.tensor_copy(wk2[:, :, 1:LEN], rk2[:, :, 0:LEN - 1]).then_inc(sem("wk"), 1)
                    dve.wait_ge(sem("beta_exp"), 1)
                    dve.tensor_scalar(flat(beta), flat(beta), 1.0, None, ALU.add).then_inc(sem("beta_sum"), 1)
                    dve.wait_ge(sem("beta_sum"), 1)
                    dve.reciprocal(flat(beta), flat(beta)).then_inc(sem("beta"), 1)
                    dve.wait_ge(sem("alpha_logit"), 1)
                    dve.tensor_scalar(flat(z), psum[:, 2, :], dt_bias, None, ALU.add).then_inc(sem("z"), 1)
                    dve.wait_ge(sem("z"), 1)
                    dve.scalar_tensor_tensor(flat(soft), flat(z), -1.0, flat(z), ALU.mult, ALU.max).then_inc(sem("abs_z"), 1)
                    dve.wait_ge(sem("ln_z"), 1)
                    dve.scalar_tensor_tensor(flat(z), flat(z), 0.0, flat(soft), ALU.max, ALU.add).then_inc(sem("softplus"), 1)
                    dve.wait_ge(sem("softplus"), 1)
                    dve.tensor_scalar(flat(z), flat(z), neg_a[:, :], None, ALU.mult).then_inc(sem("log_decay"), 1)
                    dve.wait_ge(sem("log_decay"), 1)
                    dve.tensor_tensor_scan(flat(cum), core.c["reset"][:, :], flat(z), 0.0, ALU.mult, ALU.add).then_inc(sem("cum"), 1)
                    dve.wait_ge(sem("cum"), 1)
                    dve.tensor_scalar(flat(ncum)[0:1, :], flat(cum)[0:1, :], -1.0, None, ALU.mult).then_inc(sem("neg_cum"), 1)
                    ends = over(flat(cum)[:, C - 1:], [C, NC], [0, C])
                    dve.tensor_tensor(flat(tail).rearrange("p (c t) -> p c t", c=NC), ends,
                                      flat(cum).rearrange("p (c t) -> p c t", c=NC), ALU.subtract).then_inc(sem("to_end"), 1)
                    dve.wait_ge(sem("wk"), 2)
                    dve.wait_ge(sem("beta"), 1)
                    dve.tensor_tensor(flat(wks), flat(wk), flat(beta), ALU.mult).then_inc(sem("wks"), 1)
                    dve.tensor_tensor(flat(xb), x_g, flat(beta), ALU.mult).then_inc(sem("xb"), 1)
                    dve.wait_ge(sem("cum_diff"), 1)
                    dve.tensor_tensor(flat(LT).rearrange("p (t n) -> p t n", t=NT), bank(3),
                                      over(core.c["chunk_mask"][:, :], [0, NT], [1, P]), ALU.add).then_inc(sem("masked"), 1)
                    dve.wait_ge(sem("dec"), 1)
                    dve.wait_ge(sem("wks"), 1)
                    dve.tensor_tensor(flat(wkd), flat(wks), flat(dec), ALU.mult)
                    dve.tensor_tensor(flat(rkd), flat(rk), flat(dec), ALU.mult)
                    dve.wait_ge(sem("tail"), 1)
                    dve.tensor_tensor(flat(wkt), flat(wk), flat(tail), ALU.mult).then_inc(sem("scaled"), 1)
                    dve.wait_ge(sem("LT"), 1)
                    dve.wait_ge(sem("gram"), 1)
                    dve.scalar_tensor_tensor(flat(T), psum[:, 4, :], -1.0, flat(LT), ALU.mult, ALU.mult).then_inc(sem("T"), 1)
                    dve.wait_ge(sem("reads"), 1)
                    dve.tensor_tensor(flat(intraT), psum[:, 5, :], flat(LT), ALU.mult).then_inc(sem("intraT"), 1)
                    dve.wait_ge(sem("T"), 1)
                    diag = over(core.c["block16"][:, :], [0, NT], [1, P])
                    dve.tensor_tensor(TD[:, :, :], T[:, :, :], diag, ALU.mult).then_inc(sem("TD"), 1)
                    dve.wait_ge(sem("TD"), 1)
                    dve.tensor_tensor(X1[:, :, :], TD[:, :, :], ident4, ALU.add).then_inc(sem("X1"), 1)
                    dve.wait_ge(sem("N"), 1)
                    dve.tensor_tensor(ND[:, :, :], N[:, :, :], diag, ALU.mult).then_inc(sem("ND"), 1)
                    dve.wait_ge(sem("ND"), 1)
                    dve.tensor_tensor(NO[:, :, :], N[:, :, :], ND[:, :, :], ALU.subtract).then_inc(sem("NO"), 1)
                    keep(N2, 1, "N2_kept", "N2")
                    keep(N4, 5, "N4_kept", "N4")

                    def plus(buf, b, old, name, wait):
                        dve.wait_ge(sem(wait), 1)
                        dve.tensor_tensor(flat(buf), psum[:, b, :], flat(old), ALU.add).then_inc(sem(name), 1)

                    plus(X2, 1, X1, "X2_kept", "X2")
                    dve.wait_ge(sem("X2_kept"), 1)
                    plus(X3, 0, X2, "X3_kept", "X3")
                    dve.wait_ge(sem("X3_kept"), 1)
                    plus(X4, 1, X3, "X4_kept", "X4")
                    keep(Q, 2, "Q_kept", "Q")
                    dve.wait_ge(sem("Q2"), 1)
                    dve.tensor_tensor(Z1[:, :, :], bank(5), ident4, ALU.add).then_inc(sem("Z1_kept"), 1)
                    dve.wait_ge(sem("Z1_kept"), 1)
                    plus(Z2, 6, Z1, "Z2_kept", "Z2")
                    keep(R, 7, "R_kept", "R")
                    keep(U, 0, "U_kept", "U")
                    dve.wait_ge(sem("U_kept"), 1)
                    for c in range(4):
                        for b in range(2):
                            t, lo = 2 * b + c // 2, (c % 2) * C
                            half = slice(lo, lo + C)
                            if c == 0:
                                dve.tensor_copy(vn[half, t, :], U[half, t, :]).then_inc(sem("v_new"), 1)
                            else:
                                dve.wait_ge(sem("read"), 2 * (c - 1) + b + 1)
                                dve.tensor_tensor(vn[half, t, :], U[half, t, :], psum[half, 2 + b, 0:P],
                                                  ALU.subtract).then_inc(sem("v_new"), 1)
                        for b in range(2):
                            if c == 3:
                                continue
                            end = flat(dec)[:, b * LEN + (c + 1) * C - 1:b * LEN + (c + 1) * C]
                            dve.wait_ge(sem("write"), 2 * c + b + 1)
                            if c == 0:
                                dve.tensor_copy(S[:, b, :], psum[:, 6 + b, 0:P]).then_inc(sem("state"), 1)
                            else:
                                dve.wait_ge(sem("state"), 2 * (c - 1) + b + 1)
                                dve.scalar_tensor_tensor(S[:, b, :], S[:, b, :], end, psum[:, 6 + b, 0:P],
                                                         ALU.mult, ALU.add).then_inc(sem("state"), 1)
                    dve.wait_ge(sem("outputs"), 2)
                    dve.tensor_copy(flat(oT).rearrange("p (b n) -> p b n", b=2),
                                    psum[:, 4:6, 0:LEN]).then_inc(sem("oT"), 1)
                    dve.tensor_tensor(flat(z), core.x[:, cols(g, BANK)], x_g, ALU.add).then_inc(sem("residual"), 1)
                    dve.wait_ge(sem("residual"), 1)
                    dve.wait_ge(sem("projected"), 1)
                    dve.tensor_tensor(core.x[:, cols(g, BANK)], psum[:, 0, :], flat(z), ALU.add).then_inc(sem("done"), 1)
            st.clear()


def mlp(core, w):
    psum = core.psum
    with Stage(core) as st:
        sem = st.sem
        gel = st.sb("gel", [P, 2, BANK])
        hid = st.sb("hid", [P, 2, BANK])
        nic = HIDDEN // P
        steps = [(c, ic) for c in range(CH) for ic in range(nic)]
        with st.block() as block:
            @block.tensor
            def _(pe):
                def up(k):
                    c, ic = steps[k]
                    rhs = core.h[:, cols(c, BANK)]
                    if k >= 2:
                        pe.wait_ge(sem("hidden"), k - 1)
                    pe.matmul(psum[:, k % 2, :], w["w1"][:, HIDDEN + ic * P:HIDDEN + ic * P + P], rhs,
                              start=True, stop=True).then_inc(sem("gate"), 1)
                    pe.matmul(psum[:, 2 + k % 2, :], w["w1"][:, cols(ic, P)], rhs, start=True,
                              stop=True).then_inc(sem("up"), 1)

                up(0)
                for k, (c, ic) in enumerate(steps):
                    if k + 1 < len(steps):
                        up(k + 1)
                    pe.wait_ge(sem("hidden"), k + 1)
                    pe.matmul(psum[:, 4 + c, :], w["w2"][:, ic, :], hid[:, k % 2, :],
                              start=(ic == 0), stop=(ic == nic - 1)).then_inc(sem("down"), 1)

            @block.scalar
            def _(act):
                for k, (c, ic) in enumerate(steps):
                    act.wait_ge(sem("gate"), k + 1)
                    if k >= 2:
                        act.wait_ge(sem("hidden"), k - 1)
                    act.activation(gel[:, k % 2, :], psum[:, k % 2, :], ACT.Gelu,
                                   bias=w["cols"][:, nic + ic:nic + ic + 1]).then_inc(sem("gelu"), 1)

            def residual(dve, c):
                dve.wait_ge(sem("down"), (c + 1) * nic)
                y = core.y[:, cols(c, BANK)]
                dve.scalar_tensor_tensor(y, psum[:, 4 + c, :], w["cols"][:, 2 * nic:2 * nic + 1], y,
                                         ALU.add, ALU.add).then_inc(sem("out"), 1)

            @block.vector
            def _(dve):
                for k, (c, ic) in enumerate(steps):
                    dve.wait_ge(sem("gelu"), k + 1)
                    dve.wait_ge(sem("up"), k + 1)
                    if k >= 2:
                        dve.wait_ge(sem("down"), k - 1)
                    dve.scalar_tensor_tensor(hid[:, k % 2, :], psum[:, 2 + k % 2, :], w["cols"][:, ic:ic + 1],
                                             gel[:, k % 2, :], ALU.add, ALU.mult).then_inc(sem("hidden"), 1)
                    if ic == 0 and c > 0:
                        residual(dve, c - 1)
                residual(dve, CH - 1)
        st.clear()


def local_attention(core, heads, window, wqkv, wo, tables, mask):
    nc, psum = core.nc, core.psum
    DH = 64
    G = heads // 8
    W, KW = window, window + P
    with Stage(core) as st:
        sem = st.sem
        hT = st.sb("hT", [P, LEN])
        sq = st.sb("sq", [P, 2, BANK])
        rot = st.sb("rot", [P, 2, BANK])
        qk = st.sb("qk", [P, 2, BANK])
        ss = st.sb("ss", [P, 4 * G, 8])
        rn = st.sb("rn", [P, 4 * G, 8])
        rq = st.sb("rq", [P, 2, 2, heads])
        qT = st.sb("qT", [P, 2, heads // 2, P])
        kT = st.sb("kT", [P, heads // 2, LEN])
        v = st.sb("v", [P, 2, G, BANK])
        v_prev = st.sb("v_prev", [W, G, BANK])
        sm = st.sb("sm", [P, 2, 4, KW])
        pr = st.sb("pr", [P, 2, 4, KW])
        mx = st.sb("mx", [P, heads])
        nb = st.sb("nb", [P, heads])
        total = st.sb("total", [P, heads])
        prT = st.sb("prT", [P, 2, 4, P])
        cornerT = st.sb("cornerT", [W, 2, 4, W])
        o = st.sb("o", [P, G, BANK])
        oT = st.sb("oT", [P, heads // 2, P])
        units = [(t, kind, g) for t in range(2) for kind in range(2) for g in range(G)]
        quads = [(t, n) for t in range(2) for n in range(heads // 4)]
        NQ = heads // 4
        with nc.Fori(0, BATCH) as b:
            with st.block() as block:
                half = P // 2

                @block.tensor
                def _(pe):
                    pe.wait_ge(sem("shifted"), 3)

                    def project(u):
                        t, kind, g = units[u]
                        if u >= 2:
                            pe.wait_ge(sem("rotated"), 2 * (u - 1))
                            pe.wait_ge(sem("squared"), u - 1)
                        pe.matmul(psum[:, u % 2, :], hT[:, cols(t, P)],
                                  wqkv[:, bass.ds(tables["w_at"] + (kind * G + g) * BANK, BANK)]
                                  if tables["w_at"] is not None else wqkv[:, cols(kind * G + g, BANK)],
                                  start=True, stop=True).then_inc(sem("projected"), 1)

                    def project_v(n):
                        t, g = divmod(n, G)
                        if n >= 2:
                            pe.wait_ge(sem("v"), n - 1)
                        pe.matmul(psum[:, 6 + n % 2, :], hT[:, cols(t, P)],
                                  wqkv[:, bass.ds(tables["w_at"] + (2 * G + g) * BANK, BANK)]
                                  if tables["w_at"] is not None else wqkv[:, cols(2 * G + g, BANK)],
                                  start=True, stop=True).then_inc(sem("v_projected"), 1)

                    def turn(u):
                        pe.wait_ge(sem("unit"), u + 1)
                        if u >= 2:
                            pe.wait_ge(sem("unit_kept"), u - 1)
                        for i in range(4):
                            mm = pe.transpose(psum[:, 4 + u % 2, cols(i, P)], qk[:, u % 2, cols(i, P)],
                                              core.c["ident"][:, :])
                        mm.then_inc(sem("unit_turned"), 1)

                    for u in range(len(units)):
                        project(u)
                        if u < 2 * G:
                            project_v(u)
                        if u >= 1:
                            turn(u - 1)
                    turn(len(units) - 1)

                    def scores(n):
                        t, q = quads[n]
                        lo = 0 if t == 0 else P - W
                        hi = P if t == 0 else LEN
                        if n == 0:
                            pe.wait_ge(sem("unit_kept"), len(units))
                            pe.wait_ge(sem("rotated"), 2 * len(units))
                        if n >= 2:
                            pe.wait_ge(sem("masked"), n - 1)
                        for i in range(4):
                            head = 4 * q + i
                            rows = slice((head % 2) * DH, (head % 2) * DH + DH)
                            mm = pe.matmul(psum[:, 2 * (n % 2) + i % 2, (i // 2) * KW:(i // 2) * KW + hi - lo],
                                           qT[rows, t, head // 2, :], kT[rows, head // 2, lo:hi],
                                           start=True, stop=True)
                        mm.then_inc(sem("scores"), 1)

                    def values(n):
                        t, q = quads[n]
                        pe.wait_ge(sem("exp"), 4 * (n + 1))
                        if n >= 1:
                            pe.wait_ge(sem("probs_kept"), n)
                        own = W if t == 1 else 0
                        for i in range(4):
                            mm = pe.transpose(psum[:, 4, cols(i, P)], pr[:, n % 2, i, own:own + P], core.c["ident"][:, :])
                        mm.then_inc(sem("probs_turned"), 1)
                        if t == 1:
                            if q >= 1:
                                pe.wait_ge(sem("corner_kept"), q)
                            for i in range(4):
                                mm = pe.transpose(psum[0:W, 5, cols(i, W)], pr[0:W, n % 2, i, 0:W],
                                                  core.c["ident"][0:W, 0:W])
                            mm.then_inc(sem("corner_turned"), 1)

                    def weigh(n):
                        t, q = quads[n]
                        pe.wait_ge(sem("probs_kept"), n + 1)
                        if t == 1:
                            pe.wait_ge(sem("corner_kept"), q + 1)
                            if q == 0:
                                pe.wait_ge(sem("o"), G)
                        if n == 0:
                            pe.wait_ge(sem("v"), 2 * G)
                        for i in range(4):
                            head = 4 * q + i
                            g, at = divmod(head, 8)
                            out = psum[:, 6 + g, cols(at, DH)]
                            mm = pe.matmul(out, prT[:, n % 2, i, :], v[:, t, g, cols(at, DH)], start=True,
                                           stop=(t == 0), skip_group_check=True)
                            if t == 1:
                                mm = pe.matmul(psum[0:W, 6 + g, cols(at, DH)], cornerT[:, n % 2, i, :],
                                               v_prev[:, g, cols(at, DH)], start=False, stop=True,
                                               skip_group_check=True)
                        mm.then_inc(sem("weighed"), 1)

                    def finish(t):
                        for g in range(G):
                            pe.wait_ge(sem("o"), t * G + g + 1)
                            pe.wait_ge(sem("probs_kept"), (t + 1) * NQ)
                            if g + t * G >= 1:
                                pe.wait_ge(sem("oT"), t * G + g)
                            for i in range(4):
                                mm = pe.transpose(psum[:, 4, cols(i, P)], o[:, g, cols(i, P)], core.c["ident"][:, :])
                            mm.then_inc(sem("o_turned"), 1)
                        pe.wait_ge(sem("oT"), (t + 1) * G)
                        for i in range(heads // 2):
                            mm = pe.matmul(psum[:, 5, 0:P], wo[:, i, :], oT[:, i, :], start=(i == 0),
                                           stop=(i == heads // 2 - 1))
                        mm.then_inc(sem("out"), 1)

                    scores(0)
                    for n in range(len(quads)):
                        if n + 1 < len(quads):
                            scores(n + 1)
                        if n == NQ:
                            finish(0)
                            pe.wait_ge(sem("oT"), G)
                            pe.wait_ge(sem("added"), 1)
                        values(n)
                        weigh(n)
                    finish(1)

                @block.scalar
                def _(act):
                    act.activation(hT[0:half, :], core.y[0:half, cols(b, LEN)], ACT.Copy).then_inc(sem("shifted"), 1)

                    def keep_v(n):
                        t, g = divmod(n, G)
                        act.wait_ge(sem("v_projected"), n + 1)
                        act.activation(v[:, t, g, :], psum[:, 6 + n % 2, :], ACT.Copy).then_inc(sem("v"), 1)
                        if t == 0:
                            act.wait_ge(sem("v"), n + 1)
                            act.activation(v_prev[:, g, :], v[P - W:, 0, g, :], ACT.Copy).then_inc(sem("v_prev"), 1)

                    def keep_unit(u):
                        t, kind, g = units[u]
                        act.wait_ge(sem("unit_turned"), u + 1)
                        src = psum[:, 4 + u % 2, :].rearrange("p (i n) -> p i n", i=4)
                        dst = (qT[:, t, 4 * g:4 * g + 4, :] if kind == 0
                               else kT[:, 4 * g:4 * g + 4, cols(t, P)])
                        act.activation(dst, src, ACT.Copy).then_inc(sem("unit_kept"), 1)

                    for u, (t, kind, g) in enumerate(units):
                        act.wait_ge(sem("projected"), u + 1)
                        if u >= 2:
                            act.wait_ge(sem("summed"), u - 1)
                        act.activation(sq[:, u % 2, :], psum[:, u % 2, :], ACT.Square).then_inc(sem("squared"), 1)
                        act.wait_ge(sem("summed"), u + 1)
                        act.activation(ss[:, u, :], ss[:, u, :], ACT.Sqrt).then_inc(sem("norm"), 1)
                        if u < 2 * G:
                            keep_v(u)
                        if u >= 1:
                            keep_unit(u - 1)
                    keep_unit(len(units) - 1)
                    act.wait_ge(sem("v_prev"), G)

                    def keep_o(t):
                        for g in range(G):
                            act.wait_ge(sem("o_turned"), t * G + g + 1)
                            act.activation(oT[:, 4 * g:4 * g + 4, :],
                                           psum[:, 4, :].rearrange("p (i n) -> p i n", i=4),
                                           ACT.Copy).then_inc(sem("oT"), 1)

                    def exps(n):
                        t, q = quads[n]
                        width = P if t == 0 else KW
                        act.wait_ge(sem("shift"), n + 1)
                        if n >= 2:
                            act.wait_ge(sem("probs_turned"), n - 1)
                            if t == 1 and quads[n - 2][0] == 1:
                                act.wait_ge(sem("corner_turned"), quads[n - 2][1] + 1)
                        for i in range(4):
                            head = 4 * q + i
                            act.activation(pr[:, n % 2, i, 0:width], sm[:, n % 2, i, 0:width], ACT.Exp,
                                           scale=rq[:, t, 0, head:head + 1], bias=nb[:, head:head + 1],
                                           accum_out=total[:, head:head + 1]).then_inc(sem("exp"), 1)

                    exps(0)
                    for n in range(len(quads)):
                        if n + 1 < len(quads):
                            if n + 1 == NQ:
                                act.wait_ge(sem("probs_turned"), NQ)
                                act.activation(prT[:, n % 2, :, :], psum[:, 4, :].rearrange("p (i n) -> p i n", i=4),
                                               ACT.Copy).then_inc(sem("probs_kept"), 1)
                                keep_o(0)
                                exps(n + 1)
                                continue
                            exps(n + 1)
                        t, q = quads[n]
                        act.wait_ge(sem("probs_turned"), n + 1)
                        if n >= 2:
                            act.wait_ge(sem("weighed"), n - 1)
                        act.activation(prT[:, n % 2, :, :], psum[:, 4, :].rearrange("p (i n) -> p i n", i=4),
                                       ACT.Copy).then_inc(sem("probs_kept"), 1)
                        if t == 1:
                            act.wait_ge(sem("corner_turned"), q + 1)
                            act.activation(cornerT[:, n % 2, :, :], psum[0:W, 5, 0:4 * W].rearrange("p (i n) -> p i n", i=4),
                                           ACT.Copy).then_inc(sem("corner_kept"), 1)
                    keep_o(1)

                @block.vector
                def _(dve):
                    of = core.y[half:, cols(b, LEN)]
                    dve.memset(hT[half:, 0:1], 0.0).then_inc(sem("shifted"), 1)
                    dve.tensor_copy(hT[half:, 1:LEN], core.y[half:, bass.ds(b * LEN, LEN - 1)]).then_inc(sem("shifted"), 1)

                    def rotate(u):
                        t, kind, g = units[u]
                        x = psum[:, u % 2, :].rearrange("p (h d) -> p h d", h=8)
                        if u >= 2:
                            dve.wait_ge(sem("unit_turned"), u - 1)
                        tab = tables["buf"]
                        cos = over(tab[:, t, 2 * kind, :], [0, 8], [1, DH])
                        dve.tensor_tensor(qk[:, u % 2, :].rearrange("p (h d) -> p h d", h=8), x, cos,
                                          ALU.mult).then_inc(sem("rotated"), 1)
                        hd = DH // 2
                        y = rot[:, u % 2, :].rearrange("p (h d) -> p h d", h=8)
                        dve.tensor_tensor(y[:, :, 0:hd], x[:, :, hd:DH],
                                          over(tab[:, t, 2 * kind + 1, 0:hd], [0, 8], [1, hd]), ALU.mult)
                        dve.tensor_tensor(y[:, :, hd:DH], x[:, :, 0:hd],
                                          over(tab[:, t, 2 * kind + 1, hd:DH], [0, 8], [1, hd]),
                                          ALU.mult).then_inc(sem("rotated"), 1)

                    def normalise(u):
                        t, kind, g = units[u]
                        dve.wait_ge(sem("norm"), u + 1)
                        dve.tensor_scalar(ss[:, u, :], ss[:, u, :], 1e-12, None, ALU.max).then_inc(sem("guarded"), 1)
                        dve.wait_ge(sem("guarded"), u + 1)
                        dve.reciprocal(rn[:, u, :], ss[:, u, :]).then_inc(sem("inverse"), 1)
                        dve.wait_ge(sem("inverse"), u + 1)
                        dve.wait_ge(sem("rotated"), 2 * (u + 1))
                        x = qk[:, u % 2, :]
                        if kind == 0:
                            dve.tensor_scalar(rq[:, t, 0, cols(g, 8)], rn[:, u, :], 8.0, None, ALU.mult)
                            dve.tensor_scalar(rq[:, t, 1, cols(g, 8)], rn[:, u, :], -8.0, None, ALU.mult)
                            dve.tensor_tensor(x, x, rot[:, u % 2, :], ALU.add).then_inc(sem("unit"), 1)
                        else:
                            dve.tensor_tensor(x, x, rot[:, u % 2, :], ALU.add).then_inc(sem("key_sum"), 1)
                            dve.wait_ge(sem("key_sum"), t * G + g + 1)
                            x3 = x.rearrange("p (h d) -> p h d", h=8)
                            dve.tensor_tensor(x3, x3, over(rn[:, u, :], [1, 8], [0, DH]),
                                              ALU.mult).then_inc(sem("unit"), 1)

                    for u in range(len(units)):
                        dve.wait_ge(sem("squared"), u + 1)
                        dve.tensor_reduce(ss[:, u, :], sq[:, u % 2, :].rearrange("p (h d) -> p h d", h=8),
                                          AX.X, ALU.add).then_inc(sem("summed"), 1)
                        rotate(u)
                        normalise(u)

                    def soft(n):
                        t, q = quads[n]
                        width = P if t == 0 else KW
                        dve.wait_ge(sem("scores"), n + 1)
                        if n >= 2:
                            dve.wait_ge(sem("exp"), 4 * (n - 1))
                        if t == 1 and q == 0:
                            dve.wait_ge(sem("exp"), 4 * NQ)
                        bank2 = psum[:, 2 * (n % 2):2 * (n % 2) + 2, 0:2 * KW].rearrange("p e (j k) -> p j e k", j=2)
                        band = over(mask[:, P - width + W:], [0, 2], [0, 2], [1, width])
                        out = sm[:, n % 2, :, :].rearrange("p (j e) k -> p j e k", e=2)
                        dve.tensor_tensor(out[:, :, :, 0:width], bank2[:, :, :, 0:width], band,
                                          ALU.add).then_inc(sem("masked"), 1)
                        dve.wait_ge(sem("masked"), n + 1)
                        dve.tensor_reduce(mx[:, cols(q, 4)], sm[:, n % 2, :, 0:width], AX.X, ALU.max).then_inc(sem("max"), 1)
                        dve.wait_ge(sem("max"), n + 1)
                        dve.tensor_tensor(nb[:, cols(q, 4)], mx[:, cols(q, 4)], rq[:, t, 1, cols(q, 4)],
                                          ALU.mult).then_inc(sem("shift"), 1)

                    def normal_o(t, g):
                        dve.wait_ge(sem("weighed"), t * NQ + 2 * (g + 1))
                        if t == 1:
                            dve.wait_ge(sem("o_turned"), G)
                        if g == 0:
                            dve.wait_ge(sem("exp"), 4 * NQ * (t + 1))
                            dve.reciprocal(total[:, :], total[:, :]).then_inc(sem("inverse_total"), 1)
                            dve.wait_ge(sem("inverse_total"), t + 1)
                        dve.tensor_tensor(o[:, g, :].rearrange("p (h d) -> p h d", h=8),
                                          psum[:, 6 + g, :].rearrange("p (h d) -> p h d", h=8),
                                          over(total[:, cols(g, 8)], [1, 8], [0, DH]), ALU.mult).then_inc(sem("o"), 1)

                    def add(t):
                        y = core.y[:, bass.ds(b * LEN + t * P, P)]
                        dve.wait_ge(sem("out"), t + 1)
                        dve.tensor_tensor(y, y, psum[:, 5, 0:P], ALU.add).then_inc(sem("added"), 1)

                    for n in range(NQ):
                        soft(n)
                    soft(NQ)
                    for g in range(G):
                        normal_o(0, g)
                    add(0)
                    for n in range(NQ + 1, 2 * NQ):
                        soft(n)
                    for g in range(G):
                        normal_o(1, g)
                    add(1)
            st.clear()


def relative_scores(core):
    nc, psum = core.nc, core.psum
    W3 = 384
    H = 16
    with Stage(core) as st:
        sem = st.sem
        rT = st.sb("rT", [P, BANK])
        r_bd = st.sb("r_bd", [P, H, BANK])
        qv = st.sb("qv", [P, LEN])
        raw = st.sb("raw", [P, 4, 4, W3])
        with st.block() as block:
            @block.tensor
            def _(pe):
                pe.matmul(psum[:, 0, :], core.c["l3_w"][:, 3, :], core.c["l3_remb"][:, :], start=True,
                          stop=True).then_inc(sem("r"), 1)

            @block.vector
            def _(dve):
                dve.wait_ge(sem("r"), 1)
                dve.tensor_copy(rT[:, :], psum[:, 0, :]).then_inc(sem("rT"), 1)
                dve.wait_ge(sem("rT"), 1)
                for h in range(H):
                    dve.tensor_scalar(r_bd[:, h, :], rT[:, :], core.c["head_mask"][:, h:h + 1], None,
                                      ALU.mult).then_inc(sem("r_bd"), 1)
        st.clear()
        with nc.Fori(0, BATCH) as b:
            groups = [(t, k) for t in range(2) for k in range(4)]
            with st.block() as block:
                @block.tensor
                def _(pe):
                    pe.matmul(psum[:, 7, 0:LEN], core.c["l3_w"][:, 0, :], core.h[:, cols(b, LEN)], start=True,
                              stop=True).then_inc(sem("q"), 1)
                    pe.wait_ge(sem("qv"), 1)
                    for n in range(8 * 4):
                        t, h = divmod(n, H)
                        if n >= 6:
                            pe.wait_ge(sem("kept_even" if n % 2 == 0 else "kept_odd"), (n - 6) // 2 + 1)
                        pe.matmul(psum[:, n % 6, 0:W3], qv[:, cols(t, P)], r_bd[:, h, P - P * t:P - P * t + W3],
                                  start=True, stop=True).then_inc(sem("product"), 1)

                @block.vector
                def _(dve):
                    dve.wait_ge(sem("q"), 1)
                    dve.tensor_scalar(qv[:, :], psum[:, 7, 0:LEN], core.c["l3_cols"][:, 1:2], None,
                                      ALU.add).then_inc(sem("qv"), 1)
                    for n in range(0, 32, 2):
                        dve.wait_ge(sem("product"), n + 1)
                        if n >= 16:
                            dve.wait_ge(sem(f"stored{(n - 16) // 4}"), 16)
                        dve.tensor_copy(raw[:, (n // 4) % 4, n % 4, :], psum[:, n % 6, 0:W3]).then_inc(sem("kept_even"), 1)

                @block.scalar
                def _(act):
                    for n in range(1, 32, 2):
                        act.wait_ge(sem("product"), n + 1)
                        if n >= 16:
                            act.wait_ge(sem(f"stored{(n - 16) // 4}"), 16)
                        act.activation(raw[:, (n // 4) % 4, n % 4, :], psum[:, n % 6, 0:W3],
                                       ACT.Copy).then_inc(sem("kept_odd"), 1)

                @block.sync
                def _(sp):
                    for i, (t, k) in enumerate(groups):
                        sp.wait_ge(sem("kept_even"), 2 * i + 2)
                        sp.wait_ge(sem("kept_odd"), 2 * i + 2)
                        dst = core.rel_d[bass.ds(b * 2 + t, 1), :].rearrange("a (p n) -> (a p) n", p=P)
                        sp.dma_start(dst[:, 4 * k * W3:4 * (k + 1) * W3],
                                     raw[:, i % 4, :, :].rearrange("p h n -> p (h n)")).then_inc(sem(f"stored{i}"), 16)
                    for i in range(len(groups)):
                        sp.wait_ge(sem(f"stored{i}"), 16)
            st.clear()


def wide_attention(core, causal):
    nc, psum = core.nc, core.psum
    H, DH = 16, 8
    scale = 1.0 / float(np.sqrt(DH))
    src = core.xn if causal else core.h
    with Stage(core) as st:
        sem = st.sem
        xs = st.sb("xs", [P, LEN])
        lat = st.sb("lat", [P // 2, LEN])
        qT = st.sb("qT", [P, LEN])
        k_bd = st.sb("k_bd", [P, H, LEN])
        v = st.sb("v", [P, 2, P])
        rel = st.sb("rel", [P, 1 if causal else 8, 4, LEN])
        sm = st.sb("sm", [P, 2, BANK])
        pr = st.sb("pr", [P, 2, BANK])
        prT = st.sb("prT", [P, 2, BANK])
        mx = st.sb("mx", [P, 2, H])
        nb = st.sb("nb", [P, 2, H])
        total = st.sb("total", [P, 2, H])
        o = st.sb("o", [P, 2, P])
        oT = st.sb("oT", [P, LEN])
        units = []
        for t in range(2):
            keys = P if causal and t == 0 else LEN
            nh = BANK // keys
            units += [(t, h, nh, keys) for h in range(0, H, nh)]
        n_of = [sum(1 for u in units if u[0] <= t) for t in range(2)]
        with nc.Fori(0, BATCH) as b:
            with st.block() as block:
                @block.sync
                def _(sp):
                    if not causal:
                        for i in range(8):
                            t, k = divmod(i, 4)
                            row = core.rel_d[bass.ds(b * 2 + t, 1), P - 1:P - 1 + P * (core.rel_pitch - 1)]
                            skew = row.rearrange("a (p n) -> (a p) n", p=P)[:, 4 * k * 384:4 * (k + 1) * 384]
                            sp.dma_start(rel[:, i, :, :], skew.rearrange("p (h n) -> p h n", h=4)[:, :, 0:LEN]
                                         ).then_inc(sem(f"rel{i}"), 16)
                        for i in range(8):
                            sp.wait_ge(sem(f"rel{i}"), 16)

                @block.tensor
                def _(pe):
                    pe.wait_ge(sem("x"), 1)
                    if causal:
                        w = core.c["l2_w"]
                        pe.matmul(psum[0:P // 2, 0, 0:LEN], core.c["l2_down"][:, :], xs[:, :], start=True,
                                  stop=True).then_inc(sem("latent"), 1)
                        pe.wait_ge(sem("lat"), 1)
                        pe.matmul(psum[:, 1, 0:LEN], w[:, 0:P], lat[:, :], start=True, stop=True).then_inc(sem("q"), 1)
                        pe.matmul(psum[:, 2, 0:LEN], w[:, P:2 * P], lat[:, :], start=True, stop=True).then_inc(sem("k"), 1)
                        for t in range(2):
                            mm = pe.matmul(psum[:, 3, t * P:t * P + DH], lat[:, cols(t, P)], w[:, 2 * P:2 * P + DH],
                                           start=True, stop=True)
                        mm.then_inc(sem("v"), 1)
                    else:
                        w = core.c["l3_w"]
                        pe.matmul(psum[:, 1, 0:LEN], w[:, 0, :], xs[:, :], start=True, stop=True).then_inc(sem("q"), 1)
                        pe.matmul(psum[:, 2, 0:LEN], w[:, 1, :], xs[:, :], start=True, stop=True).then_inc(sem("k"), 1)
                        for t in range(2):
                            mm = pe.matmul(psum[:, 3, cols(t, P)], xs[:, cols(t, P)], w[:, 2, :], start=True, stop=True)
                        mm.then_inc(sem("v"), 1)

                    def scores(n):
                        t, h, nh, keys = units[n]
                        if n == 0:
                            pe.wait_ge(sem("qT"), 1)
                            pe.wait_ge(sem("k_bd"), 4)
                            pe.wait_ge(sem("v_kept"), 1)
                        if n >= 2:
                            pe.wait_ge(sem("biased"), n - 1)
                        pe.matmul(psum[:, n % 2, :], qT[:, cols(t, P)], k_bd[:, h:h + nh, 0:keys], start=True,
                                  stop=True).then_inc(sem("scores"), 1)

                    scores(0)
                    for n, (t, h, nh, keys) in enumerate(units):
                        if n + 1 < len(units):
                            scores(n + 1)
                        pe.wait_ge(sem("exp"), sum(u[2] for u in units[:n + 1]))
                        if n >= 2:
                            pe.wait_ge(sem("probs_kept"), n - 1)
                        for i in range(4):
                            mm = pe.transpose(psum[:, 2 + n % 2, cols(i, P)], pr[:, n % 2, cols(i, P)], core.c["ident"][:, :])
                        mm.then_inc(sem("probs_turned"), 1)
                        pe.wait_ge(sem("probs_kept"), n + 1)
                        blocks = keys // P
                        for i in range(nh):
                            head = h + i
                            for s in range(blocks):
                                val = v[:, s, 0:DH] if causal else v[:, s, cols(head, DH)]
                                mm = pe.matmul(psum[:, 6 + t, cols(head, DH)], prT[:, n % 2, cols(i * blocks + s, P)],
                                               val, start=(s == 0), stop=(s == blocks - 1))
                        mm.then_inc(sem("weighed"), 1)
                        if n == n_of[0] + 2:
                            pe.wait_ge(sem("o"), 1)
                            pe.transpose(psum[:, 4, 0:P], o[:, 0, :], core.c["ident"][:, :]).then_inc(sem("o_turned"), 1)
                    pe.wait_ge(sem("o"), 2)
                    pe.wait_ge(sem("oT"), 1)
                    pe.transpose(psum[:, 4, 0:P], o[:, 1, :], core.c["ident"][:, :]).then_inc(sem("o_turned"), 1)
                    pe.wait_ge(sem("oT"), 2)
                    proj = core.c["l2_proj"][:, :] if causal else core.c["l3_w"][:, 4, :]
                    pe.matmul(psum[:, 5, 0:LEN], proj, oT[:, :], start=True, stop=True).then_inc(sem("out"), 1)

                @block.scalar
                def _(act):
                    act.activation(xs[:, :], src[:, cols(b, LEN)], ACT.Copy).then_inc(sem("x"), 1)
                    if causal:
                        act.wait_ge(sem("latent"), 1)
                        act.activation(lat[:, :], psum[0:P // 2, 0, 0:LEN], ACT.Copy).then_inc(sem("lat"), 1)
                    act.wait_ge(sem("q"), 1)
                    bias = core.c["small"][:, 3:4] if causal else core.c["l3_cols"][:, 0:1]
                    act.activation(qT[:, :], psum[:, 1, 0:LEN], ACT.Identity, bias=bias).then_inc(sem("qT"), 1)
                    act.wait_ge(sem("v"), 1)
                    act.activation(v[:, :, 0:DH] if causal else v[:, :, :],
                                   psum[:, 3, 0:LEN].rearrange("p (t n) -> p t n", t=2)[:, :, 0:DH if causal else P],
                                   ACT.Copy).then_inc(sem("v_kept"), 1)

                    def exps(n):
                        t, h, nh, keys = units[n]
                        act.wait_ge(sem("shift"), n + 1)
                        if n >= 2:
                            act.wait_ge(sem("probs_turned"), n - 1)
                        for i in range(nh):
                            act.activation(pr[:, n % 2, cols(i, keys)], sm[:, n % 2, cols(i, keys)], ACT.Exp,
                                           scale=scale, bias=nb[:, t, h + i:h + i + 1],
                                           accum_out=total[:, t, h + i:h + i + 1]).then_inc(sem("exp"), 1)

                    exps(0)
                    for n, (t, h, nh, keys) in enumerate(units):
                        if n + 1 < len(units):
                            exps(n + 1)
                        act.wait_ge(sem("probs_turned"), n + 1)
                        if n >= 2:
                            act.wait_ge(sem("weighed"), n - 1)
                        act.activation(prT[:, n % 2, :], psum[:, 2 + n % 2, :], ACT.Copy).then_inc(sem("probs_kept"), 1)
                    for t in range(2):
                        act.wait_ge(sem("o_turned"), t + 1)
                        act.activation(oT[:, cols(t, P)], psum[:, 4, 0:P], ACT.Copy).then_inc(sem("oT"), 1)

                @block.vector
                def _(dve):
                    dve.wait_ge(sem("k"), 1)
                    for i in range(4):
                        dve.tensor_tensor(k_bd[:, 4 * i:4 * i + 4, :], over(psum[:, 2, 0:LEN], [0, 4], [1, LEN]),
                                          over(core.c["head_mask"][:, 4 * i:4 * i + 4], [1, 4], [0, LEN]),
                                          ALU.mult).then_inc(sem("k_bd"), 1)

                    def normal(t):
                        dve.wait_ge(sem("weighed"), n_of[t])
                        dve.reciprocal(total[:, t, :], total[:, t, :]).then_inc(sem("inverse"), 1)
                        dve.wait_ge(sem("inverse"), t + 1)
                        dve.tensor_tensor(o[:, t, :].rearrange("p (h d) -> p h d", h=H),
                                          psum[:, 6 + t, 0:P].rearrange("p (h d) -> p h d", h=H),
                                          over(total[:, t, :], [1, H], [0, DH]), ALU.mult).then_inc(sem("o"), 1)

                    heads_before = 0
                    for n, (t, h, nh, keys) in enumerate(units):
                        dve.wait_ge(sem("scores"), n + 1)
                        if n >= 2:
                            dve.wait_ge(sem("exp"), heads_before - units[n - 1][2])
                        heads_before += nh
                        out = sm[:, n % 2, :].rearrange("p (h k) -> p h k", h=nh)
                        bank = psum[:, n % 2, :].rearrange("p (h k) -> p h k", h=nh)
                        if causal:
                            bias = over(core.c["causal"][:, LEN - keys:], [0, nh], [1, keys])
                        else:
                            i = 4 * t + h // 4
                            if h % 4 == 0:
                                dve.wait_ge(sem(f"rel{i}"), 16)
                            bias = rel[:, i, h % 4:h % 4 + nh, :]
                        dve.tensor_tensor(out, bank, bias, ALU.add).then_inc(sem("biased"), 1)
                        dve.wait_ge(sem("biased"), n + 1)
                        dve.tensor_reduce(mx[:, t, h:h + nh], out, AX.X, ALU.max).then_inc(sem("max"), 1)
                        dve.wait_ge(sem("max"), n + 1)
                        dve.tensor_scalar(nb[:, t, h:h + nh], mx[:, t, h:h + nh], -scale, None,
                                          ALU.mult).then_inc(sem("shift"), 1)
                        if n == n_of[0] + 1:
                            normal(0)
                    normal(1)
                    dve.wait_ge(sem("out"), 1)
                    x = core.x[:, cols(b, LEN)]
                    bo = core.c["small"][:, 3:4] if causal else core.c["l3_cols"][:, 2:3]
                    dve.scalar_tensor_tensor(x, psum[:, 5, 0:LEN], bo, x, ALU.add, ALU.add).then_inc(sem("done"), 1)
            st.clear()


def constants():
    c = {}
    f = np.float32
    c["ident"] = np.eye(P, dtype=f)
    c["mean"] = np.full((P, P), 1.0 / P, f)
    c["small"] = np.tile(np.array([1e-5, 1e-6, 1.0, 0.0], f), (P, 1))
    c["below"] = np.tile(np.tril(np.ones((8, 8), f), -1).reshape(1, 64), (P, 1))
    i = np.arange(P)
    c["ones"] = np.ones((P, P), f)
    inside = (i[:, None] < i[None, :]) & (i[:, None] // 64 == i[None, :] // 64)
    c["chunk_mask"] = np.where(inside, 0.0, NEG).astype(f)
    c["block16"] = (i[:, None] // 16 == i[None, :] // 16).astype(f)
    c["reset"] = np.tile((np.arange(BANK) % 64 != 0).astype(f), (P, 1))
    for name, window in (("l1", 64), ("l2", 32)):
        behind = i[:, None] + window - np.arange(window + P)[None, :]
        band = np.where((behind >= 0) & (behind <= window), 0.0, NEG).astype(f)
        c[name + "_band"] = band
        pos = np.arange(LEN, dtype=f)
        half = np.arange(0, 64, 2, dtype=f)
        freqs = pos[:, None] * (f(1.0) / f(10000.0) ** (half / f(64)))[None, :]
        base = (half + f(0.4 * 64)) / f(1.4 * 64)
        scale = base[None, :] ** ((pos - LEN // 2) / f(window // 2))[:, None]
        two = lambda a: np.concatenate([a, a], -1)
        freqs, scale = two(freqs), two(scale)
        sign = np.where(np.arange(64) < 32, -1.0, 1.0).astype(f)
        tab = np.stack([np.cos(freqs) * scale, np.sin(freqs) * scale * sign,
                        np.cos(freqs) / scale, np.sin(freqs) / scale * sign], 1)
        c[name + "_rotary"] = tab.reshape(2, P, 4, 64).transpose(1, 0, 2, 3).astype(f)
    c["head_mask"] = (i[:, None] // 8 == np.arange(16)[None, :]).astype(f)
    c["causal"] = np.where(np.arange(LEN)[None, :] <= P + i[:, None], 0.0, NEG).astype(f)
    return c


def laid_out(inp):
    c = constants()
    f = np.float32
    col = lambda *v: np.ascontiguousarray(np.stack([np.asarray(x, f) for x in v], 1))
    pad = lambda a, n, ax: np.pad(a, [(0, n - a.shape[ax]) if i == ax % a.ndim else (0, 0) for i in range(a.ndim)])
    c["x"] = inp["L0_attn_x"].reshape(TOK, DIM)
    c["l0_w"] = np.stack([inp[f"L0_attn_{n}_w"].T for n in ("A", "B", "C", "D", "out")], 1)
    c["l0_cols"] = col(inp["L0_attn_A_b"], inp["L0_attn_out_b"], inp["L0_attn_norm_w"])
    c["l0_gate"] = inp["L0_ffn_gate_w"]
    c["l0_wg"] = pad(inp["L0_ffn_Wg"], HIDDEN, -1)
    c["l0_wu"] = pad(inp["L0_ffn_Wu"], HIDDEN, -1)
    c["l0_wd"] = pad(inp["L0_ffn_Wd"], HIDDEN, 1)
    c["l0s_wg"] = pad(inp["L0_ffn_Sg"], 256, -1)
    c["l0s_wu"] = pad(inp["L0_ffn_Su"], 256, -1)
    c["l0s_wd"] = pad(inp["L0_ffn_Sd"], 256, 0)
    c["l1_rows"] = np.stack([np.repeat(inp[n].reshape(DIM, 1), P, 1)
                             for n in ("L1_attn_W_beta", "L1_attn_W_alpha")], 1)
    c["l1_w"] = np.stack([inp["L1_attn_W_write"].T, inp["L1_attn_W_read"].T], 1)
    c["l1_scal"] = np.repeat(np.stack([inp["L1_attn_A_log"], inp["L1_attn_dt_bias"]], 1), P, 0)
    for name, heads in (("l1", 8), ("l2", 16)):
        g = lambda n: inp[next(k for k in inp if k.lower() == f"{name}_ffn_{n}".lower())]
        depth, inner = g("wqkv").shape[0], heads * 64
        c[name + "_wqkv"] = g("wqkv").transpose(1, 0, 2)
        c[name + "_wo"] = g("wo").reshape(depth, heads // 2, P, DIM).transpose(0, 2, 1, 3)
        w1 = g("w1").reshape(depth, DIM, 2, -1)
        b1 = g("b1").reshape(depth, 2, -1)
        c[name + "_w1"] = pad(w1, HIDDEN, -1).reshape(depth, DIM, 2 * HIDDEN)
        c[name + "_w2"] = pad(g("w2"), HIDDEN, 1).reshape(depth, 3, P, DIM).transpose(0, 2, 1, 3)
        b1 = pad(b1, HIDDEN, -1).reshape(depth, 6, P)
        c[name + "_cols"] = np.concatenate([b1, g("b2")[:, None], g("ln_g")[:, None], g("ln_b")[:, None]],
                                           1).transpose(0, 2, 1)
        qs, ks = g("q_scale"), g("k_scale")
        c[name + "_scales"] = np.stack([qs, np.roll(qs, 32, -1), ks, np.roll(ks, 32, -1)], 1)
    c["l2_down"] = inp["L2_attn_Wc_down"]
    kv = inp["L2_attn_Wkv_up"]
    c["l2_w"] = np.concatenate([inp["L2_attn_Wq_up"], np.tile(kv[:, :8], (1, 16)), kv[:, 8:]], 1)
    c["l2_proj"] = inp["L2_attn_Wc_proj"]
    c["l3_w"] = np.stack([inp[f"L3_attn_W{n}"] for n in ("q", "k", "v", "r", "o")], 1)
    c["l3_cols"] = col(inp["L3_attn_u_bias"].reshape(-1), inp["L3_attn_v_bias"].reshape(-1), inp["L3_attn_bo"],
                       inp["L3_attn_gamma"], inp["L3_attn_beta"])
    first = (inp["L3_attn_rel_pos_emb"].shape[0] - 1) // 2 - (LEN - 1)
    c["l3_remb"] = pad(inp["L3_attn_rel_pos_emb"][first:first + 2 * LEN - 1].T, 2 * LEN, -1)
    c["l3_gate"] = inp["L3_ffn_gate_w"]
    gate_up = inp["L3_ffn_gate_up_w"]
    c["l3_wg"], c["l3_wu"] = np.split(gate_up, 2, -1)
    c["l3_wd"] = inp["L3_ffn_down_w"]
    return {k: np.ascontiguousarray(v, f) for k, v in c.items()}


CONST_ALL = ("ident", "mean", "small", "below", "l0_w", "l0_cols", "l0_gate", "ones", "chunk_mask", "block16", "reset",
             "l1_rows", "l1_w", "l1_scal", "l1_band", "l1_rotary", "l2_band",
             "l2_rotary", "head_mask", "causal", "l2_down", "l2_w", "l2_proj", "l3_w", "l3_cols",
             "l3_remb", "l3_gate")


def local_stack(core, level, depth, heads, window):
    nc, dram = core.nc, core.dram
    inner = 3 * heads * 64
    with Stage(core) as st:
        sem = st.sem
        wqkv = st.sb("wqkv", [P, depth, inner])
        wo = st.sb("wo", [P, heads // 2, DIM])
        w1 = st.sb("w1", [P, 2 * HIDDEN])
        w2 = st.sb("w2", [P, HIDDEN // P, DIM])
        wcols = st.sb("cols", [P, 9])
        scales = st.sb("scales", [P, 4, 64])
        tab = st.sb("tab", [P, 2, 4, 64])
        flat_w = wqkv[:, :, :].rearrange("p l n -> p (l n)")
        with st.block() as block:
            @block.vector
            def _(dve):
                for c in range(CH):
                    dve.tensor_copy(core.y[:, cols(c, BANK)], core.xn[:, cols(c, BANK)]).then_inc(sem("started"), 1)

            @block.sync
            def _(sp):
                sp.dma_start(wqkv[:, :, :], dram[level + "_wqkv"]).then_inc(sem("wqkv"), 16)
                sp.wait_ge(sem("wqkv"), 16)
        st.clear()
        with nc.Fori(0, depth) as layer:
            at = bass.ds(layer, 1)
            with st.block() as block:
                @block.sync
                def _(sp):
                    for buf, name in ((wo, "_wo"), (w2, "_w2")):
                        sp.dma_start(buf[:, :, :], dram[level + name][at].rearrange("a p i n -> p (a i) n")
                                     ).then_inc(sem("weights"), 16)
                    for buf, name in ((w1, "_w1"), (wcols, "_cols")):
                        sp.dma_start(buf[:, :], dram[level + name][at].rearrange("a p n -> p (a n)")
                                     ).then_inc(sem("weights"), 16)
                    sp.wait_ge(sem("weights"), 64)

                @block.scalar
                def _(act):
                    act.dma_start(scales[:, :, :].rearrange("p i n -> p (i n)"),
                                  dram[level + "_scales"][at].rearrange("a i n -> a (i n)").partition_broadcast(P)
                                  ).then_inc(sem("scales"), 16)

                @block.vector
                def _(dve):
                    dve.wait_ge(sem("scales"), 16)
                    for t in range(2):
                        dve.tensor_tensor(tab[:, t, :, :], core.c[level + "_rotary"][:, t, :, :],
                                          scales[:, :, :], ALU.mult).then_inc(sem("tables"), 1)
            st.clear()
            local_attention(core, heads, window, flat_w, wo, {"buf": tab, "w_at": layer * inner},
                            core.c[level + "_band"])
            layernorm(core, core.y, core.h, 0, wcols[:, 7:8], wcols[:, 8:9], shift=True)
            mlp(core, {"w1": w1, "w2": w2, "cols": wcols})
        with st.block() as block:
            @block.vector
            def _(dve):
                for c in range(CH):
                    dve.tensor_tensor(core.x[:, cols(c, BANK)], core.x[:, cols(c, BANK)],
                                      core.y[:, cols(c, BANK)], ALU.add).then_inc(sem("summed"), 1)
        st.clear()


def program(nc, dram, out, upto=99, start=0):
    with ExitStack() as ctx:
        core = Core(nc, ctx, dram)
        core.comb_d = nc.dram_tensor("comb_d", (8, TOK), F32, kind="Internal").ap()
        core.rel_pitch = 17 * 384
        core.rel_d = nc.dram_tensor("rel_d", (TILES, P * core.rel_pitch), F32, kind="Internal").ap()
        load_constants(core, CONST_ALL)
        load_stream(core)
        if start <= 0:
            layernorm(core, core.x, core.xn, 0)
            if upto >= 1:
                gated_scan(core)
            if upto >= 2:
                experts(core, "l0", 8, HIDDEN, False, "l0s")
        if start <= 1 and upto >= 3:
            layernorm(core, core.x, core.xn, 0)
            delta_rule(core)
        if start <= 1 and upto >= 4:
            local_stack(core, "l1", 2, 8, 64)
        if start <= 2 and upto >= 5:
            layernorm(core, core.x, core.xn, 0)
            wide_attention(core, True)
        if start <= 2 and upto >= 6:
            local_stack(core, "l2", 6, 16, 32)
        if start <= 3 and upto >= 7:
            layernorm(core, core.x, core.xn, 0)
            layernorm(core, core.xn, core.h, 1, core.c["l3_cols"][:, 3:4], core.c["l3_cols"][:, 4:5])
            relative_scores(core)
            wide_attention(core, False)
        if start <= 3 and upto >= 8:
            experts(core, "l3", 8, 256, True, None)
        store_stream(core, core.x, out)


def kernel(**inputs):
    import concourse.bacc as bacc
    from concourse.bass_utils import run_bass_kernel_spmd

    arrays = laid_out({k: np.asarray(v) for k, v in inputs.items()})
    nc = bacc.Bacc("TRN2", target_bir_lowering=False, num_devices=1)
    dram = {k: nc.dram_tensor("in_" + k, v.shape, F32, kind="ExternalInput").ap() for k, v in arrays.items()}
    out = nc.dram_tensor("out", (TOK, DIM), F32, kind="ExternalOutput").ap()
    program(nc, dram, out)
    r = run_bass_kernel_spmd(nc, [{"in_" + k: v for k, v in arrays.items()}], core_ids=[0])
    return r.results[0]["out"].reshape(BATCH, LEN, DIM)
```

```python
from contextlib import ExitStack

import numpy as np

import concourse.bass as bass
from concourse import mybir
from concourse.alu_op_type import AluOpType as ALU

F32 = mybir.dt.float32
ACT = mybir.ActivationFunctionType
AX = mybir.AxisListType

P = 128
BATCH, LEN, DIM = 8, 256, 128
TOK = BATCH * LEN
BANK = 512
CH = TOK // BANK
TILES = TOK // P
HIDDEN = 384
NEG = -1.0e30


class Core:

    def __init__(self, nc, ctx, dram):
        self.nc, self.ctx, self.dram = nc, ctx, dram
        self.psum = ctx.enter_context(nc.psum_tensor("psum", [P, 8, BANK], F32))
        self.x, self.xn, self.y, self.h = (
            ctx.enter_context(nc.sbuf_tensor("stream_" + n, [P, TOK], F32)) for n in ("x", "xn", "y", "h"))
        self.c = {}

    def keep(self, name, shape):
        self.c[name] = self.ctx.enter_context(self.nc.sbuf_tensor("c_" + name, shape, F32))
        return self.c[name]


class Stage:

    count = 0

    def __init__(self, core):
        self.nc, self.core = core.nc, core
        self.ctx = ExitStack()
        self.sems = {}
        Stage.count += 1
        self.tag = f"s{Stage.count}"

    def __enter__(self):
        return self

    def __exit__(self, *args):
        self.ctx.close()

    def sb(self, name, shape):
        return self.ctx.enter_context(self.nc.sbuf_tensor(f"{self.tag}_{name}", shape, F32))

    def sem(self, name):
        if name not in self.sems:
            self.sems[name] = self.ctx.enter_context(self.nc.semaphore(f"{self.tag}_{name}"))
        return self.sems[name]

    def block(self):
        return self.nc.Block(no_gpsimd_drain=True)

    def clear(self):
        nums = sorted(s.num for s in self.sems.values())
        first = last = nums[0]
        for n in nums[1:] + [None]:
            if n != last + 1:
                self.nc.gpsimd.sem_clear(range(first, last + 1))
                first = n
            last = n
        self.nc.all_engine_barrier(sem_only=True)


def cols(i, width, size=None):
    return bass.ds(i * width, size or width)


def over(ap, *dims):
    return bass.AP(ap.tensor, ap.offset, [list(ap.ap[0])] + [list(d) for d in dims])


def load_constants(core, names):
    with Stage(core) as st:
        bufs = [(core.keep(n, list(core.dram[n].shape)), core.dram[n]) for n in names]
        with st.block() as block:
            @block.sync
            def _(sp):
                for buf, src in bufs[0::2]:
                    sp.dma_start(buf[:], src).then_inc(st.sem("loaded_sp"), 16)
                sp.wait_ge(st.sem("loaded_sp"), 16 * len(bufs[0::2]))

            @block.scalar
            def _(act):
                for buf, src in bufs[1::2]:
                    act.dma_start(buf[:], src).then_inc(st.sem("loaded_act"), 16)
                act.wait_ge(st.sem("loaded_act"), 16 * len(bufs[1::2]))
        st.clear()


def load_stream(core):
    nc, psum = core.nc, core.psum
    with Stage(core) as st:
        sem = st.sem
        rows = st.sb("rows", [P, TILES, P])
        with st.block() as block:
            @block.sync
            def _(sp):
                for c in range(CH):
                    src = core.dram["x"].rearrange("(t p) d -> p t d", p=P)[:, 4 * c:4 * c + 4, :]
                    sp.dma_start(rows[:, 4 * c:4 * c + 4, :], src).then_inc(sem(f"rows{c}"), 16)

            @block.tensor
            def _(pe):
                for t in range(TILES):
                    if t % 4 == 0:
                        pe.wait_ge(sem(f"rows{t // 4}"), 16)
                    pe.transpose(psum[:, t // 4, cols(t % 4, P)], rows[:, t, :],
                                 core.c["ident"][:, :]).then_inc(sem("turned"), 1)

            @block.vector
            def _(dve):
                for c in range(CH):
                    dve.wait_ge(sem("turned"), 4 * c + 4)
                    dve.tensor_copy(core.x[:, cols(c, BANK)], psum[:, c, :]).then_inc(sem("copied"), 1)
        st.clear()


def store_stream(core, src, out):
    nc, psum = core.nc, core.psum
    with Stage(core) as st:
        sem = st.sem
        rows = st.sb("rows", [P, TILES, P])
        with st.block() as block:
            @block.tensor
            def _(pe):
                for t in range(TILES):
                    pe.transpose(psum[:, t // 4, cols(t % 4, P)], src[:, cols(t, P)],
                                 core.c["ident"][:, :]).then_inc(sem("turned"), 1)

            @block.vector
            def _(dve):
                for c in range(CH):
                    dve.wait_ge(sem("turned"), 4 * c + 4)
                    dve.tensor_copy(rows[:, 4 * c:4 * c + 4, :],
                                    psum[:, c, :].rearrange("p (t d) -> p t d", t=4)).then_inc(sem("copied"), 1)

            @block.sync
            def _(sp):
                for c in range(CH):
                    sp.wait_ge(sem("copied"), c + 1)
                    dst = out.rearrange("(t p) d -> p t d", p=P)[:, 4 * c:4 * c + 4, :]
                    sp.dma_start(dst, rows[:, 4 * c:4 * c + 4, :]).then_inc(sem("stored"), 16)
                sp.wait_ge(sem("stored"), 16 * CH)
        st.clear()


def layernorm(core, src, dst, eps, gain=None, bias=None, shift=False):
    nc, psum = core.nc, core.psum
    with Stage(core) as st:
        sem = st.sem
        sq = st.sb("sq", [P, CH, BANK])
        rstd = st.sb("rstd", [P, TILES])
        ones = st.sb("ones", [P, P])
        diagonal = st.sb("diagonal", [P, CH, BANK])
        shifted = st.sb("shifted", [P, TOK]) if shift else None
        x = shifted if shift else src
        half = P // 2
        with st.block() as block:
            @block.tensor
            def _(pe):
                for c in range(CH):
                    if shift:
                        pe.wait_ge(sem("shifted"), c + 1)
                        pe.wait_ge(sem("kept"), c + 1)
                    pe.matmul(psum[:, c, :], core.c["mean"][:, :], x[:, cols(c, BANK)],
                              start=True, stop=True).then_inc(sem("mean"), 1)
                def spread(c):
                    pe.wait_ge(sem("diagonal"), c + 1)
                    pe.matmul(psum[:, 4 + c, :], ones[:, :], diagonal[:, c, :],
                              start=True, stop=True).then_inc(sem("spread"), 1)

                pe.wait_ge(sem("ones"), 1)
                for c in range(CH):
                    pe.wait_ge(sem("squared"), c + 1)
                    for i in range(4):
                        mm = pe.matmul(psum[:, c, i:i + 1], sq[:, c, cols(i, P)], core.c["mean"][:, 0:1],
                                       start=True, stop=True)
                    mm.then_inc(sem("var"), 1)
                    if c >= 1:
                        spread(c - 1)
                spread(CH - 1)

            @block.vector
            def _(dve):
                for c in range(CH):
                    if shift:
                        two = shifted[half:, cols(c, BANK)].rearrange("p (b t) -> p b t", b=2)
                        of = src[half:, cols(c, BANK)].rearrange("p (b t) -> p b t", b=2)
                        dve.memset(two[:, :, 0:1], 0.0)
                        dve.tensor_copy(two[:, :, 1:LEN], of[:, :, 0:LEN - 1]).then_inc(sem("shifted"), 1)
                if shift:
                    dve.wait_ge(sem("shifted"), CH)
                for c in range(CH):
                    if shift:
                        dve.wait_ge(sem("kept"), c + 1)
                    dve.wait_ge(sem("mean"), c + 1)
                    dve.tensor_tensor(dst[:, cols(c, BANK)], x[:, cols(c, BANK)], psum[:, c, :],
                                      ALU.subtract).then_inc(sem("centred"), 1)
                def norm(c):
                    dve.wait_ge(sem("spread"), c + 1)
                    x_c = dst[:, cols(c, BANK)]
                    if gain is None:
                        dve.tensor_tensor(x_c, x_c, psum[:, 4 + c, :], ALU.mult).then_inc(sem("normed"), 1)
                    else:
                        dve.scalar_tensor_tensor(x_c, x_c, gain, psum[:, 4 + c, :],
                                                 ALU.mult, ALU.mult).then_inc(sem("normed"), 1)

                for c in range(CH):
                    dve.wait_ge(sem("centred"), CH)
                    dve.wait_ge(sem("std"), c + 1)
                    dve.reciprocal(rstd[:, cols(c, 4)], rstd[:, cols(c, 4)]).then_inc(sem("inverse"), 1)
                    dve.wait_ge(sem("inverse"), c + 1)
                    dve.tensor_tensor(diagonal[:, c, :].rearrange("p (i n) -> p i n", i=4),
                                      over(core.c["ident"][:, :], [0, 4], [1, P]),
                                      over(rstd[:, cols(c, 4)], [1, 4], [0, P]), ALU.mult).then_inc(sem("diagonal"), 1)
                    if c >= 1:
                        norm(c - 1)
                norm(CH - 1)

            @block.scalar
            def _(act):
                if shift:
                    for c in range(CH):
                        act.activation(shifted[0:half, cols(c, BANK)], src[0:half, cols(c, BANK)],
                                       ACT.Copy).then_inc(sem("kept"), 1)
                for c in range(CH):
                    act.wait_ge(sem("centred"), c + 1)
                    act.activation(sq[:, c, :], dst[:, cols(c, BANK)], ACT.Square).then_inc(sem("squared"), 1)
                for c in range(CH):
                    act.wait_ge(sem("var"), c + 1)
                    act.activation(rstd[:, cols(c, 4)], psum[:, c, 0:4], ACT.Sqrt,
                                   bias=core.c["small"][:, eps:eps + 1]).then_inc(sem("std"), 1)
                if gain is not None:
                    for c in range(CH):
                        act.wait_ge(sem("normed"), c + 1)
                        act.activation(dst[:, cols(c, BANK)], dst[:, cols(c, BANK)], ACT.Identity,
                                       bias=bias).then_inc(sem("scaled"), 1)

            @block.gpsimd
            def _(pool):
                pool.memset(ones[:, :], 1.0).then_inc(sem("ones"), 1)
        st.clear()


def gated_scan(core):
    nc, psum = core.nc, core.psum
    with Stage(core) as st:
        sem = st.sem
        names = ("sq", "rms", "xr", "a", "c", "d", "db", "h", "part")
        sq, rms, xr, a, c, d, db, h, part = (st.sb(n, [P, BANK]) for n in names)
        w = core.c["l0_w"]
        A_b, out_b, norm_w = (core.c["l0_cols"][:, i:i + 1] for i in range(3))
        with nc.Fori(0, CH) as g:
            with st.block() as block:
                @block.scalar
                def _(act):
                    act.activation(sq[:, :], core.xn[:, cols(g, BANK)], ACT.Square).then_inc(sem("squared"), 1)
                    act.wait_ge(sem("mean_square"), 1)
                    act.activation(rms[:, :], psum[:, 0, :], ACT.Sqrt,
                                   bias=core.c["small"][:, 0:1]).then_inc(sem("rms"), 1)
                    act.wait_ge(sem("products"), 1)
                    act.activation(a[:, :], psum[:, 1, :], ACT.Sigmoid, bias=A_b).then_inc(sem("gates"), 1)
                    act.wait_ge(sem("products"), 3)
                    act.activation(d[:, :], psum[:, 3, :], ACT.Sigmoid).then_inc(sem("gates"), 1)
                    act.wait_ge(sem("products"), 4)
                    act.activation(c[:, :], psum[:, 4, :], ACT.Sigmoid).then_inc(sem("gates"), 1)

                @block.tensor
                def _(pe):
                    pe.wait_ge(sem("squared"), 1)
                    pe.matmul(psum[:, 0, :], core.c["mean"][:, :], sq[:, :], start=True,
                              stop=True).then_inc(sem("mean_square"), 1)
                    pe.wait_ge(sem("rms_normed"), 1)
                    for i, k in enumerate((0, 1, 3, 2)):
                        pe.matmul(psum[:, 1 + i, :], w[:, k, :], xr[:, :], start=True,
                                  stop=True).then_inc(sem("products"), 1)
                    pe.wait_ge(sem("gated"), 1)
                    pe.matmul(psum[:, 5, :], w[:, 4, :], h[:, :], start=True, stop=True).then_inc(sem("out"), 1)

                @block.vector
                def _(dve):
                    dve.wait_ge(sem("rms"), 1)
                    dve.reciprocal(rms[:, :], rms[:, :]).then_inc(sem("inverse_rms"), 1)
                    dve.wait_ge(sem("inverse_rms"), 1)
                    dve.scalar_tensor_tensor(xr[:, :], core.xn[:, cols(g, BANK)], norm_w, rms[:, :],
                                             ALU.mult, ALU.mult).then_inc(sem("rms_normed"), 1)
                    dve.wait_ge(sem("gates"), 2)
                    dve.wait_ge(sem("products"), 2)
                    dve.tensor_tensor(db[:, :], d[:, :], psum[:, 2, :], ALU.mult).then_inc(sem("db"), 1)
                    dve.wait_ge(sem("db"), 1)
                    for b in range(BANK // LEN):
                        dve.tensor_tensor_scan(part[:, cols(b, LEN)], a[:, cols(b, LEN)], db[:, cols(b, LEN)],
                                               0.0, ALU.mult, ALU.add).then_inc(sem("scanned"), 1)
                    dve.wait_ge(sem("scanned"), 2)
                    dve.wait_ge(sem("gates"), 3)
                    dve.tensor_tensor(h[:, :], part[:, :], c[:, :], ALU.mult).then_inc(sem("gated"), 1)
                    dve.wait_ge(sem("gated"), 1)
                    dve.tensor_tensor(db[:, :], core.x[:, cols(g, BANK)], core.xn[:, cols(g, BANK)],
                                      ALU.add).then_inc(sem("residual"), 1)
                    dve.wait_ge(sem("residual"), 1)
                    dve.wait_ge(sem("out"), 1)
                    dve.scalar_tensor_tensor(core.x[:, cols(g, BANK)], psum[:, 5, :], out_b, db[:, :],
                                             ALU.add, ALU.add).then_inc(sem("done"), 1)
            st.clear()


def experts(core, level, n_exp, hidden, softmax_first, shared):
    nc, psum, dram = core.nc, core.psum, core.dram
    nic = hidden // P
    wg_d, wu_d, wd_d = (dram[f"{level}_{n}"] for n in ("wg", "wu", "wd"))
    with Stage(core) as st:
        sem = st.sem
        gate_w = core.c[level + "_gate"]
        E = n_exp
        logits = st.sb("logits", [P, TILES, E])
        comb = st.sb("comb", [P, TILES, E])
        top = st.sb("top", [P, TILES])
        total = st.sb("total", [P, TILES])
        gt = st.sb("gt", [P, TILES, E, E])
        eq = st.sb("eq", [P, TILES, E, E])
        rank = st.sb("rank", [P, TILES, E])
        combT = st.sb("combT", [E, TOK])
        mine = (lambda t: t[:, :, :].unsqueeze(3).to_broadcast([P, TILES, E, E]))
        with st.block() as block:
            @block.tensor
            def _(pe):
                for t in range(TILES):
                    mm = pe.matmul(psum[:, 0, cols(t, E)], core.xn[:, cols(t, P)], gate_w[:, :],
                                   start=True, stop=True)
                mm.then_inc(sem("logits"), 1)
                pe.wait_ge(sem("weights"), 1)
                for t in range(TILES):
                    mm = pe.transpose(psum[0:E, 4 + t // 4, cols(t % 4, P)], comb[:, t, :], core.c["ident"][:, :])
                mm.then_inc(sem("turned"), 1)

            @block.vector
            def _(dve):
                step = [0]

                def chained(ins):
                    step[0] += 1
                    ins.then_inc(sem("vector_step"), 1)
                    dve.wait_ge(sem("vector_step"), step[0])

                dve.wait_ge(sem("logits"), 1)
                chained(dve.tensor_copy(logits[:, :, :], psum[:, 0, 0:TILES * E].rearrange("p (t e) -> p t e", e=E)))
                chained(dve.tensor_reduce(top[:, :], logits[:, :, :], AX.X, ALU.max))
                dve.tensor_tensor(comb[:, :, :], logits[:, :, :],
                                  over(top[:, :], [1, TILES], [0, E]), ALU.subtract).then_inc(sem("less_top"), 1)
                dve.wait_ge(sem("exp"), 1)
                if softmax_first:
                    chained(dve.tensor_reduce(total[:, :], comb[:, :, :], AX.X, ALU.add))
                    chained(dve.reciprocal(total[:, :], total[:, :]))
                    chained(dve.tensor_tensor(comb[:, :, :], comb[:, :, :],
                                              over(total[:, :], [1, TILES], [0, E]), ALU.mult))
                    chained(dve.tensor_copy(logits[:, :, :], comb[:, :, :]))
                e_ap = over(logits[:, :, :], [E, TILES], [1, E], [0, E])
                f_ap = over(logits[:, :, :], [E, TILES], [0, E], [1, E])
                chained(dve.tensor_tensor(gt[:, :, :, :], f_ap, e_ap, ALU.is_gt))
                chained(dve.tensor_tensor(eq[:, :, :, :], f_ap, e_ap, ALU.is_equal))
                chained(dve.tensor_tensor(eq[:, :, :, :].rearrange("p t e f -> p t (e f)"),
                                          eq[:, :, :, :].rearrange("p t e f -> p t (e f)"),
                                          over(core.c["below"][:, :], [0, TILES], [1, E * E]), ALU.mult))
                chained(dve.tensor_tensor(gt[:, :, :, :], gt[:, :, :, :], eq[:, :, :, :], ALU.add))
                chained(dve.tensor_reduce(rank[:, :, :], gt[:, :, :, :], AX.X, ALU.add))
                chained(dve.tensor_scalar(rank[:, :, :], rank[:, :, :], 1.5, None, ALU.is_lt))
                chained(dve.tensor_tensor(comb[:, :, :], comb[:, :, :], rank[:, :, :], ALU.mult))
                chained(dve.tensor_reduce(total[:, :], comb[:, :, :], AX.X, ALU.add))
                chained(dve.reciprocal(total[:, :], total[:, :]))
                dve.tensor_tensor(comb[:, :, :], comb[:, :, :], over(total[:, :], [1, TILES], [0, E]),
                                  ALU.mult).then_inc(sem("weights"), 1)
                dve.wait_ge(sem("turned"), 1)
                dve.tensor_copy(combT[:, :], psum[0:E, 4:8, :].rearrange("p b n -> p (b n)")).then_inc(sem("combT"), 1)

            @block.scalar
            def _(act):
                act.wait_ge(sem("less_top"), 1)
                act.activation(comb[:, :, :], comb[:, :, :], ACT.Exp).then_inc(sem("exp"), 1)

            @block.sync
            def _(sp):
                sp.wait_ge(sem("combT"), 1)
                sp.dma_start(core.comb_d, combT[:, :]).then_inc(sem("stored"), 16)
                sp.wait_ge(sem("stored"), 16)
        st.clear()

    with Stage(core) as st:
        sem = st.sem
        sg = st.sb("sg", [P, 2, BANK])
        hid = st.sb("hid", [P, 2, BANK])
        wg = st.sb("wg", [P, 2, hidden])
        wu = st.sb("wu", [P, 2, hidden])
        wd = st.sb("wd", [P, 2, nic, DIM])
        cb = st.sb("cb", [P, 2, TOK])
        xc = st.sb("xc", [P, 2, BANK])

        def run(block, jobs, weigh, first):
            steps = [(j, buf, c, ic) for j, (buf, n) in enumerate(jobs) for c in range(CH) for ic in range(n)]
            units = [(j, buf, c) for j, (buf, n) in enumerate(jobs) for c in range(CH)]

            @block.tensor
            def _(pe):
                if first:
                    for c in range(CH):
                        pe.matmul(psum[:, 4 + c, :], core.c["ident"][:, :], core.x[:, cols(c, BANK)],
                                  start=True, stop=False, skip_group_check=True)

                def up(k):
                    j, buf, c, ic = steps[k]
                    if c == 0 and ic == 0:
                        pe.wait_ge(sem(f"w{j}"), 32)
                    rhs = core.xn[:, cols(c, BANK)]
                    if k >= 2:
                        pe.wait_ge(sem("hidden"), k - 1)
                    pe.matmul(psum[:, k % 2, :], wg[:, buf, cols(ic, P)], rhs, start=True,
                              stop=True).then_inc(sem("gate"), 1)
                    if weigh:
                        pe.wait_ge(sem("weighed"), units.index((j, buf, c)) + 1)
                        rhs = xc[:, units.index((j, buf, c)) % 2, :]
                    pe.matmul(psum[:, 2 + k % 2, :], wu[:, buf, cols(ic, P)], rhs, start=True,
                              stop=True).then_inc(sem("up"), 1)

                def down(k):
                    j, buf, c, ic = steps[k]
                    if c == 0 and ic == 0:
                        pe.wait_ge(sem(f"wd{j}"), 16)
                    pe.wait_ge(sem("hidden"), k + 1)
                    pe.matmul(psum[:, 4 + c, :], wd[:, buf, ic, :], hid[:, k % 2, :], start=False,
                              stop=False, skip_group_check=True).then_inc(sem("down"), 1)

                up(0)
                for k in range(len(steps)):
                    if k + 1 < len(steps):
                        up(k + 1)
                    down(k)

            @block.scalar
            def _(act):
                for k in range(len(steps)):
                    act.wait_ge(sem("gate"), k + 1)
                    if k >= 2:
                        act.wait_ge(sem("hidden"), k - 1)
                    act.activation(sg[:, k % 2, :], psum[:, k % 2, :], ACT.Silu).then_inc(sem("silu"), 1)

            @block.vector
            def _(dve):
                done = [0]

                def weigh_chunk(u):
                    j, buf, c = units[u]
                    if c == 0:
                        dve.wait_ge(sem(f"cb{j}"), 16)
                    if u >= 2:
                        before = sum(1 for s in steps if units.index(s[:3]) <= u - 2)
                        dve.wait_ge(sem("up"), before)
                    dve.tensor_tensor(xc[:, u % 2, :], core.xn[:, cols(c, BANK)], cb[:, buf, cols(c, BANK)],
                                      ALU.mult).then_inc(sem("weighed"), 1)
                if weigh:
                    weigh_chunk(0)
                for k in range(len(steps)):
                    j, buf, c, ic = steps[k]
                    if weigh and ic == 0 and units.index((j, buf, c)) + 1 < len(units):
                        weigh_chunk(units.index((j, buf, c)) + 1)
                    dve.wait_ge(sem("silu"), k + 1)
                    dve.wait_ge(sem("up"), k + 1)
                    if k >= 2:
                        dve.wait_ge(sem("down"), k - 1)
                    dve.tensor_tensor(hid[:, k % 2, :], sg[:, k % 2, :], psum[:, 2 + k % 2, :],
                                      ALU.mult).then_inc(sem("hidden"), 1)

        def load(q, buf, e, j):
            q.dma_start(wg[:, buf, :], wg_d[e, :, :].rearrange("a p n -> p (a n)")).then_inc(sem(f"w{j}"), 16)
            q.dma_start(wu[:, buf, :], wu_d[e, :, :].rearrange("a p n -> p (a n)")).then_inc(sem(f"w{j}"), 16)
            q.dma_start(wd[:, buf, :, :], wd_d[e, :, :].rearrange("a (c p) n -> p (a c) n", p=P)).then_inc(sem(f"wd{j}"), 16)

        with st.block() as block:
            if shared:
                run(block, [(0, dram[shared + "_wg"].shape[1] // P)], False, True)
            else:
                @block.tensor
                def _(pe):
                    for c in range(CH):
                        mm = pe.matmul(psum[:, 4 + c, :], core.c["ident"][:, :], core.x[:, cols(c, BANK)],
                                       start=True, stop=False, skip_group_check=True)
                    mm.then_inc(sem("opened"), 1)

            @block.sync
            def _(sp):
                if shared:
                    n = dram[shared + "_wg"].shape[1]
                    sp.dma_start(wg[:, 0, 0:n], dram[shared + "_wg"]).then_inc(sem("w0"), 16)
                    sp.dma_start(wu[:, 0, 0:n], dram[shared + "_wu"]).then_inc(sem("w0"), 16)
                    sp.dma_start(wd[:, 0, 0:n // P, :],
                                 dram[shared + "_wd"].rearrange("(c p) n -> p c n", p=P)).then_inc(sem("wd0"), 16)
        st.clear()
        with nc.Fori(0, n_exp // 2) as pair:
            with st.block() as block:
                run(block, [(0, nic), (1, nic)], True, False)

                @block.sync
                def _(sp):
                    for j in range(2):
                        load(sp, j, bass.ds(pair * 2 + j, 1), j)
                        sp.dma_start(cb[:, j, :], core.comb_d[bass.ds(pair * 2 + j, 1), :].partition_broadcast(P)
                                     ).then_inc(sem(f"cb{j}"), 16)
            st.clear()
        with st.block() as block:
            @block.vector
            def _(dve):
                for c in range(CH):
                    dve.tensor_copy(core.x[:, cols(c, BANK)], psum[:, 4 + c, :]).then_inc(sem("copied"), 1)
        st.clear()


def delta_rule(core):
    nc, psum = core.nc, core.psum
    C = 64
    NC = BANK // C
    NT = BANK // P
    with Stage(core) as st:
        sem = st.sem
        wide = lambda n: st.sb(n, [P, NT, P])
        flat = lambda t: t[:, :, :].rearrange("p t n -> p (t n)")
        bank = lambda i: psum[:, i, :].rearrange("p (t n) -> p t n", t=NT)
        sq, norm, rk, wk, beta, z, soft, cum, dec, tail = (
            wide(n) for n in ("sq", "norm", "rk", "wk", "beta", "z", "soft", "cum", "dec", "tail"))
        wks, wkd, wkt, rkd, xb, ncum = (wide(n) for n in ("wks", "wkd", "wkt", "rkd", "xb", "ncum"))
        LT, T, N, TD, ND, TO, NO, intraT = (wide(n) for n in ("LT", "T", "N", "TD", "ND", "TO", "NO", "intraT"))
        T2, N2, T4, N4, N8, X1, X2, X3, X4 = (wide(n) for n in ("T2", "N2", "T4", "N4", "N8", "X1", "X2", "X3", "X4"))
        Q, QT, Z1, Z2, PP, R = (wide(n) for n in ("Q", "QT", "Z1", "Z2", "PP", "R"))
        wkd_t, wkt_t, vsc, U, WT, vn, oT = (wide(n) for n in ("wkd_t", "wkt_t", "vsc", "U", "WT", "vn", "oT"))
        S = st.sb("S", [P, 2, P])
        neg_a = st.sb("neg_a", [P, 1])
        dt_bias = core.c["l1_scal"][:, 1:2]
        ident4 = over(core.c["ident"][:, :], [0, NT], [1, P])
        with st.block() as block:
            @block.scalar
            def _(act):
                act.activation(neg_a[:, :], core.c["l1_scal"][:, 0:1], ACT.Exp).then_inc(sem("exp_a"), 1)

            @block.vector
            def _(dve):
                dve.wait_ge(sem("exp_a"), 1)
                dve.tensor_scalar(neg_a[:, :], neg_a[:, :], -1.0, None, ALU.mult).then_inc(sem("neg_a"), 1)
        st.clear()
        with nc.Fori(0, CH) as g:
            with st.block() as block:
                x_g = core.xn[:, cols(g, BANK)]

                @block.scalar
                def _(act):
                    act.activation(flat(sq), x_g, ACT.Square).then_inc(sem("squared"), 1)
                    act.wait_ge(sem("mean_square"), 1)
                    act.activation(flat(norm), psum[:, 0, :], ACT.Sqrt, scale=float(P)).then_inc(sem("norm"), 1)
                    act.wait_ge(sem("beta_logit"), 1)
                    act.activation(flat(beta), psum[:, 1, :], ACT.Exp, scale=-1.0).then_inc(sem("beta_exp"), 1)
                    act.wait_ge(sem("abs_z"), 1)
                    act.activation(flat(soft), flat(soft), ACT.Exp, scale=-1.0).then_inc(sem("exp_z"), 1)
                    act.wait_ge(sem("exp_z"), 1)
                    act.activation(flat(soft), flat(soft), ACT.Ln, bias=core.c["small"][:, 2:3]).then_inc(sem("ln_z"), 1)
                    act.wait_ge(sem("cum"), 1)
                    act.activation(flat(dec), flat(cum), ACT.Exp).then_inc(sem("dec"), 1)
                    act.wait_ge(sem("to_end"), 1)
                    act.activation(flat(tail), flat(tail), ACT.Exp).then_inc(sem("tail"), 1)
                    act.wait_ge(sem("masked"), 1)
                    act.activation(flat(LT), flat(LT), ACT.Exp).then_inc(sem("LT"), 1)
                    act.wait_ge(sem("N_turned"), 1)
                    act.activation(flat(N), psum[:, 6, :], ACT.Copy).then_inc(sem("N"), 1)
                    act.wait_ge(sem("T2"), 1)
                    act.activation(flat(T2), psum[:, 0, :], ACT.Copy).then_inc(sem("T2_kept"), 1)
                    act.wait_ge(sem("T4"), 1)
                    act.activation(flat(T4), psum[:, 2, :], ACT.Copy).then_inc(sem("T4_kept"), 1)
                    for i, (buf, b) in enumerate(((wkd_t, 6), (wkt_t, 7), (vsc, 3))):
                        act.wait_ge(sem("token_major"), i + 1)
                        act.activation(flat(buf), psum[:, b, :], ACT.Copy).then_inc(sem("token_major_kept"), 1)
                    act.wait_ge(sem("N8"), 1)
                    act.activation(flat(N8), psum[:, 4, :], ACT.Copy).then_inc(sem("N8_kept"), 1)
                    act.wait_ge(sem("QT"), 1)
                    act.activation(flat(QT), psum[:, 3, :], ACT.Copy).then_inc(sem("QT_kept"), 1)
                    act.wait_ge(sem("P_turned"), 1)
                    act.activation(flat(PP), psum[:, 4, :], ACT.Copy).then_inc(sem("P_kept"), 1)
                    act.wait_ge(sem("WT"), 1)
                    act.activation(flat(WT), psum[:, 1, :], ACT.Copy).then_inc(sem("WT_kept"), 1)

                @block.tensor
                def _(pe):
                    def tiles(b, lhsT, rhs, name, turn=False):
                        for t in range(NT):
                            if turn:
                                mm = pe.transpose(bank(b)[:, t, :], lhsT[:, t, :], core.c["ident"][:, :])
                            else:
                                mm = pe.matmul(bank(b)[:, t, :], lhsT[:, t, :], rhs[:, t, :], start=True, stop=True)
                        mm.then_inc(sem(name), 1)

                    pe.matmul(psum[:, 1, :], core.c["l1_rows"][:, 0, :], x_g, start=True, stop=True).then_inc(sem("beta_logit"), 1)
                    pe.matmul(psum[:, 2, :], core.c["l1_rows"][:, 1, :], x_g, start=True, stop=True).then_inc(sem("alpha_logit"), 1)
                    pe.wait_ge(sem("squared"), 1)
                    pe.matmul(psum[:, 0, :], core.c["mean"][:, :], flat(sq), start=True, stop=True).then_inc(sem("mean_square"), 1)
                    pe.wait_ge(sem("neg_cum"), 1)
                    for t in range(NT):
                        pe.matmul(bank(3)[:, t, :], core.c["ones"][0:1, :], cum[0:1, t, :], start=True, stop=False)
                        mm = pe.matmul(bank(3)[:, t, :], ncum[0:1, t, :], core.c["ones"][0:1, :], start=False, stop=True)
                    mm.then_inc(sem("cum_diff"), 1)
                    pe.wait_ge(sem("wks"), 1)
                    tiles(4, wk, wks, "gram")
                    tiles(5, wk, rk, "reads")
                    pe.wait_ge(sem("T"), 1)
                    tiles(6, T, None, "N_turned", turn=True)
                    pe.wait_ge(sem("NO"), 1)
                    tiles(0, ND, TD, "T2")
                    tiles(1, TD, ND, "N2")
                    pe.wait_ge(sem("N2_kept"), 1)
                    pe.wait_ge(sem("T2_kept"), 1)
                    tiles(2, N2, T2, "T4")
                    pe.wait_ge(sem("N"), 1)
                    tiles(5, T2, N2, "N4")
                    tiles(1, N2, X1, "X2")
                    pe.wait_ge(sem("scaled"), 1)
                    tiles(6, wkd, None, "token_major", turn=True)
                    tiles(7, wkt, None, "token_major", turn=True)
                    for t in range(NT):
                        mm = pe.matmul(bank(3)[:, t, :], xb[:, t, :], core.c["l1_w"][:, 0, :], start=True, stop=True)
                    mm.then_inc(sem("token_major"), 1)
                    pe.wait_ge(sem("N4_kept"), 1)
                    pe.wait_ge(sem("T4_kept"), 1)
                    tiles(4, T4, N4, "N8")
                    pe.wait_ge(sem("X2_kept"), 1)
                    tiles(0, N4, X2, "X3")
                    pe.wait_ge(sem("X3_kept"), 1)
                    pe.wait_ge(sem("N8_kept"), 1)
                    tiles(1, N8, X3, "X4")
                    pe.wait_ge(sem("X4_kept"), 1)
                    tiles(2, NO, X4, "Q")
                    pe.wait_ge(sem("token_major_kept"), 3)
                    tiles(3, X4, NO, "QT")
                    tiles(4, X4, None, "P_turned", turn=True)
                    pe.wait_ge(sem("QT_kept"), 1)
                    pe.wait_ge(sem("Q_kept"), 1)
                    tiles(5, QT, Q, "Q2")
                    pe.wait_ge(sem("Z1_kept"), 1)
                    tiles(6, QT, Z1, "Z2")
                    pe.wait_ge(sem("P_kept"), 1)
                    pe.wait_ge(sem("Z2_kept"), 1)
                    tiles(7, PP, Z2, "R")
                    pe.wait_ge(sem("R_kept"), 1)
                    tiles(0, R, vsc, "U")
                    tiles(1, wkd_t, R, "WT")
                    done = 0
                    for c in range(4):
                        for b in range(2):
                            t, lo = 2 * b + c // 2, (c % 2) * C
                            half = slice(lo, lo + C)
                            if c > 0:
                                pe.wait_ge(sem("WT_kept"), 1)
                                pe.wait_ge(sem("state"), 2 * (c - 1) + b + 1)
                                pe.matmul(psum[half, 2 + b, 0:P], WT[:, t, half], S[:, b, :],
                                          start=True, stop=True).then_inc(sem("read"), 1)
                        for b in range(2):
                            t, lo = 2 * b + c // 2, (c % 2) * C
                            half = slice(lo, lo + C)
                            if c > 0:
                                pe.matmul(psum[:, 4 + b, cols(c, C)], S[:, b, :], rkd[:, t, half],
                                          start=True, stop=False)
                            pe.wait_ge(sem("v_new"), 2 * c + b + 1)
                            mm = pe.matmul(psum[:, 4 + b, cols(c, C)], vn[half, t, :], intraT[half, t, half],
                                           start=(c == 0), stop=True)
                            if c == 3:
                                mm.then_inc(sem("outputs"), 1)
                            if c < 3:
                                mm = pe.matmul(psum[:, 6 + b, 0:P], wkt_t[half, t, :], vn[half, t, :],
                                               start=True, stop=True)
                                mm.then_inc(sem("write"), 1)
                    pe.wait_ge(sem("oT"), 1)
                    pe.matmul(psum[:, 0, :], core.c["l1_w"][:, 1, :], flat(oT), start=True, stop=True).then_inc(sem("projected"), 1)

                @block.vector
                def _(dve):
                    def keep(buf, b, name, wait):
                        dve.wait_ge(sem(wait), 1)
                        dve.tensor_copy(flat(buf), psum[:, b, :]).then_inc(sem(name), 1)

                    dve.wait_ge(sem("norm"), 1)
                    dve.tensor_scalar(flat(norm), flat(norm), 1e-12, None, ALU.max).then_inc(sem("guarded"), 1)
                    dve.wait_ge(sem("guarded"), 1)
                    dve.reciprocal(flat(norm), flat(norm)).then_inc(sem("inverse"), 1)
                    dve.wait_ge(sem("inverse"), 1)
                    dve.tensor_tensor(flat(rk), x_g, flat(norm), ALU.mult).then_inc(sem("rk"), 1)
                    dve.wait_ge(sem("rk"), 1)
                    wk2 = flat(wk).rearrange("p (b t) -> p b t", b=2)
                    rk2 = flat(rk).rearrange("p (b t) -> p b t", b=2)
                    dve.memset(wk2[:, :, 0:1], 0.0).then_inc(sem("wk"), 1)
                    dve.tensor_copy(wk2[:, :, 1:LEN], rk2[:, :, 0:LEN - 1]).then_inc(sem("wk"), 1)
                    dve.wait_ge(sem("beta_exp"), 1)
                    dve.tensor_scalar(flat(beta), flat(beta), 1.0, None, ALU.add).then_inc(sem("beta_sum"), 1)
                    dve.wait_ge(sem("beta_sum"), 1)
                    dve.reciprocal(flat(beta), flat(beta)).then_inc(sem("beta"), 1)
                    dve.wait_ge(sem("alpha_logit"), 1)
                    dve.tensor_scalar(flat(z), psum[:, 2, :], dt_bias, None, ALU.add).then_inc(sem("z"), 1)
                    dve.wait_ge(sem("z"), 1)
                    dve.scalar_tensor_tensor(flat(soft), flat(z), -1.0, flat(z), ALU.mult, ALU.max).then_inc(sem("abs_z"), 1)
                    dve.wait_ge(sem("ln_z"), 1)
                    dve.scalar_tensor_tensor(flat(z), flat(z), 0.0, flat(soft), ALU.max, ALU.add).then_inc(sem("softplus"), 1)
                    dve.wait_ge(sem("softplus"), 1)
                    dve.tensor_scalar(flat(z), flat(z), neg_a[:, :], None, ALU.mult).then_inc(sem("log_decay"), 1)
                    dve.wait_ge(sem("log_decay"), 1)
                    dve.tensor_tensor_scan(flat(cum), core.c["reset"][:, :], flat(z), 0.0, ALU.mult, ALU.add).then_inc(sem("cum"), 1)
                    dve.wait_ge(sem("cum"), 1)
                    dve.tensor_scalar(flat(ncum)[0:1, :], flat(cum)[0:1, :], -1.0, None, ALU.mult).then_inc(sem("neg_cum"), 1)
                    ends = over(flat(cum)[:, C - 1:], [C, NC], [0, C])
                    dve.tensor_tensor(flat(tail).rearrange("p (c t) -> p c t", c=NC), ends,
                                      flat(cum).rearrange("p (c t) -> p c t", c=NC), ALU.subtract).then_inc(sem("to_end"), 1)
                    dve.wait_ge(sem("wk"), 2)
                    dve.wait_ge(sem("beta"), 1)
                    dve.tensor_tensor(flat(wks), flat(wk), flat(beta), ALU.mult).then_inc(sem("wks"), 1)
                    dve.tensor_tensor(flat(xb), x_g, flat(beta), ALU.mult).then_inc(sem("xb"), 1)
                    dve.wait_ge(sem("cum_diff"), 1)
                    dve.tensor_tensor(flat(LT).rearrange("p (t n) -> p t n", t=NT), bank(3),
                                      over(core.c["chunk_mask"][:, :], [0, NT], [1, P]), ALU.add).then_inc(sem("masked"), 1)
                    dve.wait_ge(sem("dec"), 1)
                    dve.wait_ge(sem("wks"), 1)
                    dve.tensor_tensor(flat(wkd), flat(wks), flat(dec), ALU.mult)
                    dve.tensor_tensor(flat(rkd), flat(rk), flat(dec), ALU.mult)
                    dve.wait_ge(sem("tail"), 1)
                    dve.tensor_tensor(flat(wkt), flat(wk), flat(tail), ALU.mult).then_inc(sem("scaled"), 1)
                    dve.wait_ge(sem("LT"), 1)
                    dve.wait_ge(sem("gram"), 1)
                    dve.scalar_tensor_tensor(flat(T), psum[:, 4, :], -1.0, flat(LT), ALU.mult, ALU.mult).then_inc(sem("T"), 1)
                    dve.wait_ge(sem("reads"), 1)
                    dve.tensor_tensor(flat(intraT), psum[:, 5, :], flat(LT), ALU.mult).then_inc(sem("intraT"), 1)
                    dve.wait_ge(sem("T"), 1)
                    diag = over(core.c["block16"][:, :], [0, NT], [1, P])
                    dve.tensor_tensor(TD[:, :, :], T[:, :, :], diag, ALU.mult).then_inc(sem("TD"), 1)
                    dve.wait_ge(sem("TD"), 1)
                    dve.tensor_tensor(X1[:, :, :], TD[:, :, :], ident4, ALU.add).then_inc(sem("X1"), 1)
                    dve.wait_ge(sem("N"), 1)
                    dve.tensor_tensor(ND[:, :, :], N[:, :, :], diag, ALU.mult).then_inc(sem("ND"), 1)
                    dve.wait_ge(sem("ND"), 1)
                    dve.tensor_tensor(NO[:, :, :], N[:, :, :], ND[:, :, :], ALU.subtract).then_inc(sem("NO"), 1)
                    keep(N2, 1, "N2_kept", "N2")
                    keep(N4, 5, "N4_kept", "N4")

                    def plus(buf, b, old, name, wait):
                        dve.wait_ge(sem(wait), 1)
                        dve.tensor_tensor(flat(buf), psum[:, b, :], flat(old), ALU.add).then_inc(sem(name), 1)

                    plus(X2, 1, X1, "X2_kept", "X2")
                    dve.wait_ge(sem("X2_kept"), 1)
                    plus(X3, 0, X2, "X3_kept", "X3")
                    dve.wait_ge(sem("X3_kept"), 1)
                    plus(X4, 1, X3, "X4_kept", "X4")
                    keep(Q, 2, "Q_kept", "Q")
                    dve.wait_ge(sem("Q2"), 1)
                    dve.tensor_tensor(Z1[:, :, :], bank(5), ident4, ALU.add).then_inc(sem("Z1_kept"), 1)
                    dve.wait_ge(sem("Z1_kept"), 1)
                    plus(Z2, 6, Z1, "Z2_kept", "Z2")
                    keep(R, 7, "R_kept", "R")
                    keep(U, 0, "U_kept", "U")
                    dve.wait_ge(sem("U_kept"), 1)
                    for c in range(4):
                        for b in range(2):
                            t, lo = 2 * b + c // 2, (c % 2) * C
                            half = slice(lo, lo + C)
                            if c == 0:
                                dve.tensor_copy(vn[half, t, :], U[half, t, :]).then_inc(sem("v_new"), 1)
                            else:
                                dve.wait_ge(sem("read"), 2 * (c - 1) + b + 1)
                                dve.tensor_tensor(vn[half, t, :], U[half, t, :], psum[half, 2 + b, 0:P],
                                                  ALU.subtract).then_inc(sem("v_new"), 1)
                        for b in range(2):
                            if c == 3:
                                continue
                            end = flat(dec)[:, b * LEN + (c + 1) * C - 1:b * LEN + (c + 1) * C]
                            dve.wait_ge(sem("write"), 2 * c + b + 1)
                            if c == 0:
                                dve.tensor_copy(S[:, b, :], psum[:, 6 + b, 0:P]).then_inc(sem("state"), 1)
                            else:
                                dve.wait_ge(sem("state"), 2 * (c - 1) + b + 1)
                                dve.scalar_tensor_tensor(S[:, b, :], S[:, b, :], end, psum[:, 6 + b, 0:P],
                                                         ALU.mult, ALU.add).then_inc(sem("state"), 1)
                    dve.wait_ge(sem("outputs"), 2)
                    dve.tensor_copy(flat(oT).rearrange("p (b n) -> p b n", b=2),
                                    psum[:, 4:6, 0:LEN]).then_inc(sem("oT"), 1)
                    dve.tensor_tensor(flat(z), core.x[:, cols(g, BANK)], x_g, ALU.add).then_inc(sem("residual"), 1)
                    dve.wait_ge(sem("residual"), 1)
                    dve.wait_ge(sem("projected"), 1)
                    dve.tensor_tensor(core.x[:, cols(g, BANK)], psum[:, 0, :], flat(z), ALU.add).then_inc(sem("done"), 1)
            st.clear()


def mlp(core, w, prefetch):
    psum = core.psum
    with Stage(core) as st:
        sem = st.sem
        gel = st.sb("gel", [P, 2, BANK])
        hid = st.sb("hid", [P, 2, BANK])
        nic = HIDDEN // P
        steps = [(c, ic) for c in range(CH) for ic in range(nic)]
        with st.block() as block:
            @block.sync
            def _(sp):
                prefetch(sp, sem("prefetched"))
                sp.wait_ge(sem("prefetched"), 48)

            @block.tensor
            def _(pe):
                def up(k):
                    c, ic = steps[k]
                    rhs = core.h[:, cols(c, BANK)]
                    if k >= 2:
                        pe.wait_ge(sem("hidden"), k - 1)
                    pe.matmul(psum[:, k % 2, :], w["w1"][:, HIDDEN + ic * P:HIDDEN + ic * P + P], rhs,
                              start=True, stop=True).then_inc(sem("gate"), 1)
                    pe.matmul(psum[:, 2 + k % 2, :], w["w1"][:, cols(ic, P)], rhs, start=True,
                              stop=True).then_inc(sem("up"), 1)

                up(0)
                for k, (c, ic) in enumerate(steps):
                    if k + 1 < len(steps):
                        up(k + 1)
                    pe.wait_ge(sem("hidden"), k + 1)
                    pe.matmul(psum[:, 4 + c, :], w["w2"][:, ic, :], hid[:, k % 2, :],
                              start=(ic == 0), stop=(ic == nic - 1)).then_inc(sem("down"), 1)

            @block.scalar
            def _(act):
                for k, (c, ic) in enumerate(steps):
                    act.wait_ge(sem("gate"), k + 1)
                    if k >= 2:
                        act.wait_ge(sem("hidden"), k - 1)
                    act.activation(gel[:, k % 2, :], psum[:, k % 2, :], ACT.Gelu,
                                   bias=w["cols"][:, nic + ic:nic + ic + 1]).then_inc(sem("gelu"), 1)

            def residual(dve, c):
                dve.wait_ge(sem("down"), (c + 1) * nic)
                y = core.y[:, cols(c, BANK)]
                dve.scalar_tensor_tensor(y, psum[:, 4 + c, :], w["cols"][:, 2 * nic:2 * nic + 1], y,
                                         ALU.add, ALU.add).then_inc(sem("out"), 1)

            @block.vector
            def _(dve):
                for k, (c, ic) in enumerate(steps):
                    dve.wait_ge(sem("gelu"), k + 1)
                    dve.wait_ge(sem("up"), k + 1)
                    if k >= 2:
                        dve.wait_ge(sem("down"), k - 1)
                    dve.scalar_tensor_tensor(hid[:, k % 2, :], psum[:, 2 + k % 2, :], w["cols"][:, ic:ic + 1],
                                             gel[:, k % 2, :], ALU.add, ALU.mult).then_inc(sem("hidden"), 1)
                    if ic == 0 and c > 0:
                        residual(dve, c - 1)
                residual(dve, CH - 1)
        st.clear()


def local_attention(core, st, heads, window, wqkv, wo, tab, mask):
    nc, psum = core.nc, core.psum
    DH = 64
    G = heads // 8
    NS = 4 * G
    W, KW = window, window + P
    half = P // 2
    sem = st.sem
    hT = st.sb("hT", [P, LEN])
    sq = st.sb("sq", [P, 2, BANK])
    rot = st.sb("rot", [P, 3, BANK])
    qk = st.sb("qk", [P, 3, BANK])
    ss = st.sb("ss", [P, NS, 8])
    rn = st.sb("rn", [P, NS, 8])
    power = st.sb("power", [P, 8])
    rq = st.sb("rq", [P, 2, 2, 2, heads])
    qT = st.sb("qT", [P, 2, 2, heads // 2, P])
    kT = st.sb("kT", [P, 2, heads // 2, LEN])
    v = st.sb("v", [P, 2, 2, G, BANK])
    sm = st.sb("sm", [P, 2, 4, KW])
    pr = st.sb("pr", [P, 2, 4, KW])
    mx = st.sb("mx", [P, 2, heads])
    nb = st.sb("nb", [P, 2, heads])
    total = st.sb("total", [P, 2, heads])
    prT = st.sb("prT", [P, 2, 4, P])
    cornerT = st.sb("cornerT", [P, 2, 4, W])
    o = st.sb("o", [P, G, BANK])
    oT = st.sb("oT", [P, heads // 2, P])
    TURN, SCORES, PROBS, CORNER, OUT = 2, 3, 5, 6, 7
    units = [(t, kind, g) for t in range(2) for kind in range(2) for g in range(G)]
    quads = [(t, q) for t in range(2) for q in range(2 * G)]
    items, place, j = [], [], 0
    for u in range(NS):
        place.append(len(items))
        items.append(("unit", u))
        if u % 2 == 0:
            items.append(("v", j))
            j += 1
    slots = range(NS + 6)

    def group_turned_in(n):
        return (n - 4) // 2 if n >= 4 and n % 2 == 0 and (n - 4) // 2 < 2 * G else None

    def tile_out_in(n):
        return next((t for t in range(2) if n == 2 * G * (t + 1) + 3), None)

    def one_block(block, a, to, b, of):
        A, B = a is not None, b is not None

        @block.tensor
        def _(pe):
            project_at = [0]

            def project_until(u):
                if u >= NS:
                    last = len(items) - 1
                else:
                    last = place[u]
                while project_at[0] <= last:
                    i = project_at[0]
                    kind, k = items[i]
                    if i >= 2:
                        before, m = items[i - 2]
                        if before == "unit":
                            pe.wait_ge(sem("squared"), m + 1)
                            pe.wait_ge(sem("rotated"), 2 * (m + 1))
                        else:
                            pe.wait_ge(sem("v"), m + 1)
                    if kind == "unit":
                        t, which, g = units[k]
                    else:
                        (t, g), which = divmod(k, G), 2
                    pe.matmul(psum[:, i % 2, :], hT[:, cols(t, P)], wqkv[:, cols(which * G + g, BANK)],
                              start=True, stop=True).then_inc(sem("projected"), 1)
                    project_at[0] += 1

            def turn(u):
                pe.wait_ge(sem("unit"), u + 1)
                if u >= 1:
                    pe.wait_ge(sem("unit_kept"), u)
                for i in range(4):
                    mm = pe.transpose(psum[:, TURN, cols(i, P)], qk[:, u % 3, cols(i, P)], core.c["ident"][:, :])
                mm.then_inc(sem("unit_turned"), 1)

            def scores(n):
                t, q = quads[n]
                lo = 0 if t == 0 else P - W
                hi = P if t == 0 else LEN
                if n >= 1:
                    pe.wait_ge(sem("masked"), n)
                for i in range(4):
                    head = 4 * q + i
                    rows = slice((head % 2) * DH, (head % 2) * DH + DH)
                    mm = pe.matmul(psum[:, SCORES + i % 2, (i // 2) * KW:(i // 2) * KW + hi - lo],
                                   qT[rows, of, t, head // 2, :], kT[rows, of, head // 2, lo:hi],
                                   start=True, stop=True)
                mm.then_inc(sem("scores"), 1)

            def turn_probs(n):
                t, q = quads[n]
                pe.wait_ge(sem("exp"), 4 * (n + 1))
                if n >= 1:
                    pe.wait_ge(sem("probs_kept"), n)
                own = W if t == 1 else 0
                for i in range(4):
                    mm = pe.transpose(psum[:, PROBS, cols(i, P)], pr[:, n % 2, i, own:own + P], core.c["ident"][:, :])
                mm.then_inc(sem("probs_turned"), 1)
                if t == 1:
                    if q >= 1:
                        pe.wait_ge(sem("corner_kept"), q)
                    for i in range(4):
                        mm = pe.transpose(psum[0:W, CORNER, cols(i, W)], pr[0:W, n % 2, i, 0:W],
                                          core.c["ident"][0:W, 0:W])
                    mm.then_inc(sem("corner_turned"), 1)

            def weigh(n):
                t, q = quads[n]
                pe.wait_ge(sem("probs_kept"), n + 1)
                if t == 1:
                    pe.wait_ge(sem("corner_kept"), q + 1)
                if n % 2 == 0 and n >= 2:
                    pe.wait_ge(sem("o"), n // 2)
                for i in range(4):
                    g, at = divmod(4 * q + i, 8)
                    mm = pe.matmul(psum[:, OUT, cols(at, DH)], prT[:, n % 2, i, :], v[:, of, t, g, cols(at, DH)],
                                   start=True, stop=(t == 0), skip_group_check=True)
                    if t == 1:
                        mm = pe.matmul(psum[0:W, OUT, cols(at, DH)], cornerT[P - W:, n % 2, i, :],
                                       v[P - W:, of, 0, g, cols(at, DH)], start=False, stop=True,
                                       skip_group_check=True)
                mm.then_inc(sem("weighed"), 1)

            def turn_group(j):
                pe.wait_ge(sem("o"), j + 1)
                pe.wait_ge(sem("probs_kept"), min(2 * j + 4, NS))
                if j >= 1:
                    pe.wait_ge(sem("oT"), j)
                for i in range(4):
                    mm = pe.transpose(psum[:, PROBS, cols(i, P)], o[:, j % G, cols(i, P)], core.c["ident"][:, :])
                mm.then_inc(sem("o_turned"), 1)

            def project_out(t, n):
                pe.wait_ge(sem("oT"), (t + 1) * G)
                if n > 2 * G:
                    pe.wait_ge(sem("corner_kept"), min(n, NS) - 2 * G)
                if t == 1:
                    pe.wait_ge(sem("added"), 1)
                for i in range(heads // 2):
                    mm = pe.matmul(psum[:, CORNER, 3 * P:], wo[:, i, :], oT[:, i, :], start=(i == 0),
                                   stop=(i == heads // 2 - 1))
                mm.then_inc(sem("out"), 1)

            if B:
                scores(0)
            if A:
                pe.wait_ge(sem("shifted"), 3)
                project_until(0)
            for n in slots:
                if B and n + 1 < NS:
                    scores(n + 1)
                if A and 2 <= n <= NS + 1:
                    turn(n - 2)
                j, t = group_turned_in(n), tile_out_in(n)
                if B and j is not None:
                    turn_group(j)
                if B and t is not None:
                    project_out(t, n)
                if B and n < NS:
                    if j is not None:
                        pe.wait_ge(sem("oT"), j + 1)
                    if t is not None:
                        pe.wait_ge(sem("added"), t + 1)
                    turn_probs(n)
                if B and 1 <= n <= NS:
                    weigh(n - 1)
                if A and n < NS:
                    project_until(n + 1)

        @block.scalar
        def _(act):
            def exps(n):
                t, q = quads[n]
                width = P if t == 0 else KW
                act.wait_ge(sem("shift"), n + 1)
                if n >= 2:
                    act.wait_ge(sem("probs_turned"), n - 1)
                    if quads[n - 2][0] == 1:
                        act.wait_ge(sem("corner_turned"), quads[n - 2][1] + 1)
                for i in range(4):
                    head = 4 * q + i
                    act.activation(pr[:, n % 2, i, 0:width], sm[:, n % 2, i, 0:width], ACT.Exp,
                                   scale=rq[:, of, t, 0, head:head + 1], bias=nb[:, t, head:head + 1],
                                   accum_out=total[:, t, head:head + 1]).then_inc(sem("exp"), 1)

            def keep_v(k):
                t, g = divmod(k, G)
                i = items.index(("v", k))
                act.wait_ge(sem("projected"), i + 1)
                act.activation(v[:, to, t, g, :], psum[:, i % 2, :], ACT.Copy).then_inc(sem("v"), 1)

            def keep_unit(u):
                t, kind, g = units[u]
                act.wait_ge(sem("unit_turned"), u + 1)
                src = psum[:, TURN, :].rearrange("p (i n) -> p i n", i=4)
                dst = (qT[:, to, t, 4 * g:4 * g + 4, :] if kind == 0
                       else kT[:, to, 4 * g:4 * g + 4, cols(t, P)])
                act.activation(dst, src, ACT.Copy).then_inc(sem("unit_kept"), 1)

            def keep_group(j):
                t, g = divmod(j, G)
                act.wait_ge(sem("o_turned"), j + 1)
                if t == 1:
                    act.wait_ge(sem("out"), 1)
                act.activation(oT[:, 4 * g:4 * g + 4, :], psum[:, PROBS, :].rearrange("p (i n) -> p i n", i=4),
                               ACT.Copy).then_inc(sem("oT"), 1)

            def keep_probs(n):
                t, q = quads[n]
                act.wait_ge(sem("probs_turned"), n + 1)
                if n >= 2:
                    act.wait_ge(sem("weighed"), n - 1)
                act.activation(prT[:, n % 2, :, :], psum[:, PROBS, :].rearrange("p (i n) -> p i n", i=4),
                               ACT.Copy).then_inc(sem("probs_kept"), 1)
                if t == 1:
                    act.wait_ge(sem("corner_turned"), q + 1)
                    act.activation(cornerT[P - W:, n % 2, :, :], psum[0:W, CORNER, 0:4 * W].rearrange("p (i n) -> p i n", i=4),
                                   ACT.Copy).then_inc(sem("corner_kept"), 1)

            if A:
                act.activation(hT[0:half, :], core.y[0:half, cols(a, LEN)], ACT.Copy).then_inc(sem("shifted"), 1)
            if B:
                exps(0)
            v_kept = 0
            for n in slots:
                while A and v_kept < 2 * G and (n >= NS or items.index(("v", v_kept)) < place[n]):
                    keep_v(v_kept)
                    v_kept += 1
                if A and n < NS:
                    act.wait_ge(sem("projected"), place[n] + 1)
                    if n >= 2:
                        act.wait_ge(sem("summed"), n - 1)
                    act.activation(sq[:, n % 2, :], psum[:, place[n] % 2, :], ACT.Square).then_inc(sem("squared"), 1)
                if A and 2 <= n <= NS + 1:
                    keep_unit(n - 2)
                if B and group_turned_in(n) is not None:
                    keep_group(group_turned_in(n))
                if B and n + 1 < NS:
                    exps(n + 1)
                if B and n < NS:
                    keep_probs(n)

        @block.gpsimd
        def _(pool):
            if not A:
                return
            pool.memset(power[:, :], -0.5).then_inc(sem("power"), 1)
            pool.wait_ge(sem("power"), 1)
            for u, (t, kind, g) in enumerate(units):
                pool.wait_ge(sem("summed"), u + 1)
                pool.tensor_scalar(ss[:, u, :], ss[:, u, :], 1e-24, None, ALU.max).then_inc(sem("guarded"), 1)
                pool.wait_ge(sem("guarded"), u + 1)
                pool.tensor_tensor(rn[:, u, :], ss[:, u, :], power[:, :], ALU.pow).then_inc(sem("inverse"), 1)
                pool.wait_ge(sem("inverse"), u + 1)
                x, r = qk[:, u % 3, :], rot[:, u % 3, :]
                pool.wait_ge(sem("rotated"), 2 * (u + 1))
                if kind == 0:
                    pool.tensor_scalar(rq[:, to, t, 0, cols(g, 8)], rn[:, u, :], 8.0, None, ALU.mult).then_inc(sem("query_scale"), 1)
                    pool.tensor_scalar(rq[:, to, t, 1, cols(g, 8)], rn[:, u, :], -8.0, None, ALU.mult).then_inc(sem("query_scale"), 1)
                    pool.tensor_tensor(x, x, r, ALU.add).then_inc(sem("unit"), 1)
                else:
                    pool.tensor_tensor(r, x, r, ALU.add).then_inc(sem("key_sum"), 1)
                    pool.wait_ge(sem("key_sum"), t * G + g + 1)
                    pool.tensor_tensor(x.rearrange("p (h d) -> p h d", h=8), r.rearrange("p (h d) -> p h d", h=8),
                                       over(rn[:, u, :], [1, 8], [0, DH]), ALU.mult).then_inc(sem("unit"), 1)

        @block.vector
        def _(dve):
            def rotate(u):
                t, kind, g = units[u]
                x = psum[:, place[u] % 2, :].rearrange("p (h d) -> p h d", h=8)
                if u >= 3:
                    dve.wait_ge(sem("unit_turned"), u - 2)
                cos = over(tab[:, t, 2 * kind, :], [0, 8], [1, DH])
                dve.tensor_tensor(qk[:, u % 3, :].rearrange("p (h d) -> p h d", h=8), x, cos,
                                  ALU.mult).then_inc(sem("rotated"), 1)
                hd = DH // 2
                y = rot[:, u % 3, :].rearrange("p (h d) -> p h d", h=8)
                dve.tensor_tensor(y[:, :, 0:hd], x[:, :, hd:DH],
                                  over(tab[:, t, 2 * kind + 1, 0:hd], [0, 8], [1, hd]), ALU.mult)
                dve.tensor_tensor(y[:, :, hd:DH], x[:, :, 0:hd],
                                  over(tab[:, t, 2 * kind + 1, hd:DH], [0, 8], [1, hd]),
                                  ALU.mult).then_inc(sem("rotated"), 1)

            def soft(n):
                t, q = quads[n]
                width = P if t == 0 else KW
                dve.wait_ge(sem("scores"), n + 1)
                if n >= 2:
                    dve.wait_ge(sem("exp"), 4 * (n - 1))
                bank2 = psum[:, SCORES:SCORES + 2, 0:2 * KW].rearrange("p e (j k) -> p j e k", j=2)
                band = over(mask[:, P - width + W:], [0, 2], [0, 2], [1, width])
                out = sm[:, n % 2, :, :].rearrange("p (j e) k -> p j e k", e=2)
                dve.tensor_tensor(out[:, :, :, 0:width], bank2[:, :, :, 0:width], band,
                                  ALU.add).then_inc(sem("masked"), 1)
                dve.wait_ge(sem("masked"), n + 1)
                dve.tensor_reduce(mx[:, t, cols(q, 4)], sm[:, n % 2, :, 0:width], AX.X, ALU.max).then_inc(sem("max"), 1)
                dve.wait_ge(sem("max"), n + 1)
                dve.tensor_tensor(nb[:, t, cols(q, 4)], mx[:, t, cols(q, 4)], rq[:, of, t, 1, cols(q, 4)],
                                  ALU.mult).then_inc(sem("shift"), 1)

            def normal_group(j):
                t, g = divmod(j, G)
                dve.wait_ge(sem("weighed"), 2 * j + 2)
                if t == 1:
                    dve.wait_ge(sem("o_turned"), g + 1)
                sums = total[:, t, cols(g, 8)]
                dve.reciprocal(sums, sums).then_inc(sem("inverse_total"), 1)
                dve.wait_ge(sem("inverse_total"), j + 1)
                dve.tensor_tensor(o[:, g, :].rearrange("p (h d) -> p h d", h=8),
                                  psum[:, OUT, :].rearrange("p (h d) -> p h d", h=8),
                                  over(sums, [1, 8], [0, DH]), ALU.mult).then_inc(sem("o"), 1)

            def add(t):
                y = core.y[:, bass.ds(b * LEN + t * P, P)]
                dve.wait_ge(sem("out"), t + 1)
                dve.tensor_tensor(y, y, psum[:, CORNER, 3 * P:], ALU.add).then_inc(sem("added"), 1)

            if A:
                dve.memset(hT[half:, 0:1], 0.0).then_inc(sem("shifted"), 1)
                dve.tensor_copy(hT[half:, 1:LEN], core.y[half:, bass.ds(a * LEN, LEN - 1)]).then_inc(sem("shifted"), 1)
            if B:
                soft(0)
            for n in slots:
                if B and n >= 3 and n % 2 == 1 and (n - 3) // 2 < 2 * G:
                    normal_group((n - 3) // 2)
                if B and n + 1 < NS:
                    soft(n + 1)
                if B and tile_out_in(n) is not None:
                    add(tile_out_in(n))
                if A and n < NS:
                    dve.wait_ge(sem("squared"), n + 1)
                    dve.tensor_reduce(ss[:, n, :], sq[:, n % 2, :].rearrange("p (h d) -> p h d", h=8),
                                      AX.X, ALU.add).then_inc(sem("summed"), 1)
                    rotate(n)

    with st.block() as block:
        one_block(block, 0, 0, None, None)
    st.clear()
    with nc.Fori(0, BATCH // 2 - 1) as pair:
        with st.block() as block:
            one_block(block, pair * 2 + 1, 1, pair * 2, 0)
        st.clear()
        with st.block() as block:
            one_block(block, pair * 2 + 2, 0, pair * 2 + 1, 1)
        st.clear()
    with st.block() as block:
        one_block(block, BATCH - 1, 1, BATCH - 2, 0)
    st.clear()
    with st.block() as block:
        one_block(block, None, None, BATCH - 1, 1)
    st.clear()


def relative_scores(core):
    nc, psum = core.nc, core.psum
    W3 = 384
    H = 16
    with Stage(core) as st:
        sem = st.sem
        rT = st.sb("rT", [P, BANK])
        r_bd = st.sb("r_bd", [P, H, BANK])
        qv = st.sb("qv", [P, LEN])
        raw = st.sb("raw", [P, 4, 4, W3])
        with st.block() as block:
            @block.tensor
            def _(pe):
                pe.matmul(psum[:, 0, :], core.c["l3_w"][:, 3, :], core.c["l3_remb"][:, :], start=True,
                          stop=True).then_inc(sem("r"), 1)

            @block.vector
            def _(dve):
                dve.wait_ge(sem("r"), 1)
                dve.tensor_copy(rT[:, :], psum[:, 0, :]).then_inc(sem("rT"), 1)
                dve.wait_ge(sem("rT"), 1)
                for h in range(H):
                    dve.tensor_scalar(r_bd[:, h, :], rT[:, :], core.c["head_mask"][:, h:h + 1], None,
                                      ALU.mult).then_inc(sem("r_bd"), 1)
        st.clear()
        with nc.Fori(0, BATCH) as b:
            groups = [(t, k) for t in range(2) for k in range(4)]
            with st.block() as block:
                @block.tensor
                def _(pe):
                    pe.matmul(psum[:, 7, 0:LEN], core.c["l3_w"][:, 0, :], core.h[:, cols(b, LEN)], start=True,
                              stop=True).then_inc(sem("q"), 1)
                    pe.wait_ge(sem("qv"), 1)
                    for n in range(8 * 4):
                        t, h = divmod(n, H)
                        if n >= 6:
                            pe.wait_ge(sem("kept_even" if n % 2 == 0 else "kept_odd"), (n - 6) // 2 + 1)
                        pe.matmul(psum[:, n % 6, 0:W3], qv[:, cols(t, P)], r_bd[:, h, P - P * t:P - P * t + W3],
                                  start=True, stop=True).then_inc(sem("product"), 1)

                @block.vector
                def _(dve):
                    dve.wait_ge(sem("q"), 1)
                    dve.tensor_scalar(qv[:, :], psum[:, 7, 0:LEN], core.c["l3_cols"][:, 1:2], None,
                                      ALU.add).then_inc(sem("qv"), 1)
                    for n in range(0, 32, 2):
                        dve.wait_ge(sem("product"), n + 1)
                        if n >= 16:
                            dve.wait_ge(sem(f"stored{(n - 16) // 4}"), 16)
                        dve.tensor_copy(raw[:, (n // 4) % 4, n % 4, :], psum[:, n % 6, 0:W3]).then_inc(sem("kept_even"), 1)

                @block.scalar
                def _(act):
                    for n in range(1, 32, 2):
                        act.wait_ge(sem("product"), n + 1)
                        if n >= 16:
                            act.wait_ge(sem(f"stored{(n - 16) // 4}"), 16)
                        act.activation(raw[:, (n // 4) % 4, n % 4, :], psum[:, n % 6, 0:W3],
                                       ACT.Copy).then_inc(sem("kept_odd"), 1)

                @block.sync
                def _(sp):
                    for i, (t, k) in enumerate(groups):
                        sp.wait_ge(sem("kept_even"), 2 * i + 2)
                        sp.wait_ge(sem("kept_odd"), 2 * i + 2)
                        dst = core.rel_d[bass.ds(b * 2 + t, 1), :].rearrange("a (p n) -> (a p) n", p=P)
                        sp.dma_start(dst[:, 4 * k * W3:4 * (k + 1) * W3],
                                     raw[:, i % 4, :, :].rearrange("p h n -> p (h n)")).then_inc(sem(f"stored{i}"), 16)
                    for i in range(len(groups)):
                        sp.wait_ge(sem(f"stored{i}"), 16)
            st.clear()


def wide_attention(core, causal):
    nc, psum = core.nc, core.psum
    H, DH = 16, 8
    scale = 1.0 / float(np.sqrt(DH))
    src = core.xn if causal else core.h
    with Stage(core) as st:
        sem = st.sem
        xs = st.sb("xs", [P, LEN])
        lat = st.sb("lat", [P // 2, LEN])
        qT = st.sb("qT", [P, LEN])
        k_bd = st.sb("k_bd", [P, H, LEN])
        v = st.sb("v", [P, 2, P])
        rel = st.sb("rel", [P, 1 if causal else 8, 4, LEN])
        sm = st.sb("sm", [P, 2, BANK])
        pr = st.sb("pr", [P, 2, BANK])
        prT = st.sb("prT", [P, 2, BANK])
        mx = st.sb("mx", [P, 2, H])
        nb = st.sb("nb", [P, 2, H])
        total = st.sb("total", [P, 2, H])
        o = st.sb("o", [P, 2, P])
        oT = st.sb("oT", [P, LEN])
        units = []
        for t in range(2):
            keys = P if causal and t == 0 else LEN
            nh = BANK // keys
            units += [(t, h, nh, keys) for h in range(0, H, nh)]
        n_of = [sum(1 for u in units if u[0] <= t) for t in range(2)]
        with nc.Fori(0, BATCH) as b:
            with st.block() as block:
                @block.sync
                def _(sp):
                    if not causal:
                        for i in range(8):
                            t, k = divmod(i, 4)
                            row = core.rel_d[bass.ds(b * 2 + t, 1), P - 1:P - 1 + P * (core.rel_pitch - 1)]
                            skew = row.rearrange("a (p n) -> (a p) n", p=P)[:, 4 * k * 384:4 * (k + 1) * 384]
                            sp.dma_start(rel[:, i, :, :], skew.rearrange("p (h n) -> p h n", h=4)[:, :, 0:LEN]
                                         ).then_inc(sem(f"rel{i}"), 16)
                        for i in range(8):
                            sp.wait_ge(sem(f"rel{i}"), 16)

                @block.tensor
                def _(pe):
                    pe.wait_ge(sem("x"), 1)
                    if causal:
                        w = core.c["l2_w"]
                        pe.matmul(psum[0:P // 2, 0, 0:LEN], core.c["l2_down"][:, :], xs[:, :], start=True,
                                  stop=True).then_inc(sem("latent"), 1)
                        pe.wait_ge(sem("lat"), 1)
                        pe.matmul(psum[:, 1, 0:LEN], w[:, 0:P], lat[:, :], start=True, stop=True).then_inc(sem("q"), 1)
                        pe.matmul(psum[:, 2, 0:LEN], w[:, P:2 * P], lat[:, :], start=True, stop=True).then_inc(sem("k"), 1)
                        for t in range(2):
                            mm = pe.matmul(psum[:, 3, t * P:t * P + DH], lat[:, cols(t, P)], w[:, 2 * P:2 * P + DH],
                                           start=True, stop=True)
                        mm.then_inc(sem("v"), 1)
                    else:
                        w = core.c["l3_w"]
                        pe.matmul(psum[:, 1, 0:LEN], w[:, 0, :], xs[:, :], start=True, stop=True).then_inc(sem("q"), 1)
                        pe.matmul(psum[:, 2, 0:LEN], w[:, 1, :], xs[:, :], start=True, stop=True).then_inc(sem("k"), 1)
                        for t in range(2):
                            mm = pe.matmul(psum[:, 3, cols(t, P)], xs[:, cols(t, P)], w[:, 2, :], start=True, stop=True)
                        mm.then_inc(sem("v"), 1)

                    def scores(n):
                        t, h, nh, keys = units[n]
                        if n == 0:
                            pe.wait_ge(sem("qT"), 1)
                            pe.wait_ge(sem("v_kept"), 1)
                        if t == 0:
                            pe.wait_ge(sem("k_bd"), (h + nh + 3) // 4)
                        if n >= 2:
                            pe.wait_ge(sem("biased"), n - 1)
                        pe.matmul(psum[:, n % 2, :], qT[:, cols(t, P)], k_bd[:, h:h + nh, 0:keys], start=True,
                                  stop=True).then_inc(sem("scores"), 1)

                    def turn(n):
                        pe.wait_ge(sem("exp"), sum(u[2] for u in units[:n + 1]))
                        if n >= 2:
                            pe.wait_ge(sem("probs_kept"), n - 1)
                        for i in range(4):
                            mm = pe.transpose(psum[:, 2 + n % 2, cols(i, P)], pr[:, n % 2, cols(i, P)], core.c["ident"][:, :])
                        mm.then_inc(sem("probs_turned"), 1)

                    def weigh(n):
                        t, h, nh, keys = units[n]
                        pe.wait_ge(sem("probs_kept"), n + 1)
                        blocks = keys // P
                        for i in range(nh):
                            head = h + i
                            for s in range(blocks):
                                val = v[:, s, 0:DH] if causal else v[:, s, cols(head, DH)]
                                mm = pe.matmul(psum[:, 6 + t, cols(head, DH)], prT[:, n % 2, cols(i * blocks + s, P)],
                                               val, start=(s == 0), stop=(s == blocks - 1))
                        mm.then_inc(sem("weighed"), 1)

                    scores(0)
                    scores(1)
                    for n in range(len(units)):
                        if n + 2 < len(units):
                            scores(n + 2)
                        turn(n)
                        if n >= 1:
                            weigh(n - 1)
                        if n == n_of[0] + 3:
                            pe.wait_ge(sem("o"), 1)
                            pe.transpose(psum[:, 4, 0:P], o[:, 0, :], core.c["ident"][:, :]).then_inc(sem("o_turned"), 1)
                    weigh(len(units) - 1)
                    pe.wait_ge(sem("o"), 2)
                    pe.wait_ge(sem("oT"), 1)
                    pe.transpose(psum[:, 4, 0:P], o[:, 1, :], core.c["ident"][:, :]).then_inc(sem("o_turned"), 1)
                    pe.wait_ge(sem("oT"), 2)
                    proj = core.c["l2_proj"][:, :] if causal else core.c["l3_w"][:, 4, :]
                    pe.matmul(psum[:, 5, 0:LEN], proj, oT[:, :], start=True, stop=True).then_inc(sem("out"), 1)

                @block.scalar
                def _(act):
                    act.activation(xs[:, :], src[:, cols(b, LEN)], ACT.Copy).then_inc(sem("x"), 1)
                    if causal:
                        act.wait_ge(sem("latent"), 1)
                        act.activation(lat[:, :], psum[0:P // 2, 0, 0:LEN], ACT.Copy).then_inc(sem("lat"), 1)
                    act.wait_ge(sem("q"), 1)
                    bias = core.c["small"][:, 3:4] if causal else core.c["l3_cols"][:, 0:1]
                    act.activation(qT[:, :], psum[:, 1, 0:LEN], ACT.Identity, bias=bias).then_inc(sem("qT"), 1)
                    act.wait_ge(sem("v"), 1)
                    act.activation(v[:, :, 0:DH] if causal else v[:, :, :],
                                   psum[:, 3, 0:LEN].rearrange("p (t n) -> p t n", t=2)[:, :, 0:DH if causal else P],
                                   ACT.Copy).then_inc(sem("v_kept"), 1)

                    def exps(n):
                        t, h, nh, keys = units[n]
                        act.wait_ge(sem("shift"), n + 1)
                        if n >= 2:
                            act.wait_ge(sem("probs_turned"), n - 1)
                        for i in range(nh):
                            act.activation(pr[:, n % 2, cols(i, keys)], sm[:, n % 2, cols(i, keys)], ACT.Exp,
                                           scale=scale, bias=nb[:, t, h + i:h + i + 1],
                                           accum_out=total[:, t, h + i:h + i + 1]).then_inc(sem("exp"), 1)

                    exps(0)
                    for n, (t, h, nh, keys) in enumerate(units):
                        if n + 1 < len(units):
                            exps(n + 1)
                        act.wait_ge(sem("probs_turned"), n + 1)
                        if n >= 2:
                            act.wait_ge(sem("weighed"), n - 1)
                        act.activation(prT[:, n % 2, :], psum[:, 2 + n % 2, :], ACT.Copy).then_inc(sem("probs_kept"), 1)
                    for t in range(2):
                        act.wait_ge(sem("o_turned"), t + 1)
                        act.activation(oT[:, cols(t, P)], psum[:, 4, 0:P], ACT.Copy).then_inc(sem("oT"), 1)

                @block.vector
                def _(dve):
                    dve.wait_ge(sem("k"), 1)
                    for i in range(4):
                        dve.tensor_tensor(k_bd[:, 4 * i:4 * i + 4, :], over(psum[:, 2, 0:LEN], [0, 4], [1, LEN]),
                                          over(core.c["head_mask"][:, 4 * i:4 * i + 4], [1, 4], [0, LEN]),
                                          ALU.mult).then_inc(sem("k_bd"), 1)

                    def normal(t):
                        dve.wait_ge(sem("weighed"), n_of[t])
                        dve.reciprocal(total[:, t, :], total[:, t, :]).then_inc(sem("inverse"), 1)
                        dve.wait_ge(sem("inverse"), t + 1)
                        dve.tensor_tensor(o[:, t, :].rearrange("p (h d) -> p h d", h=H),
                                          psum[:, 6 + t, 0:P].rearrange("p (h d) -> p h d", h=H),
                                          over(total[:, t, :], [1, H], [0, DH]), ALU.mult).then_inc(sem("o"), 1)

                    heads_before = 0
                    for n, (t, h, nh, keys) in enumerate(units):
                        dve.wait_ge(sem("scores"), n + 1)
                        if n >= 2:
                            dve.wait_ge(sem("exp"), heads_before - units[n - 1][2])
                        heads_before += nh
                        out = sm[:, n % 2, :].rearrange("p (h k) -> p h k", h=nh)
                        bank = psum[:, n % 2, :].rearrange("p (h k) -> p h k", h=nh)
                        if causal:
                            bias = over(core.c["causal"][:, LEN - keys:], [0, nh], [1, keys])
                        else:
                            i = 4 * t + h // 4
                            if h % 4 == 0:
                                dve.wait_ge(sem(f"rel{i}"), 16)
                            bias = rel[:, i, h % 4:h % 4 + nh, :]
                        dve.tensor_tensor(out, bank, bias, ALU.add).then_inc(sem("biased"), 1)
                        dve.wait_ge(sem("biased"), n + 1)
                        dve.tensor_reduce(mx[:, t, h:h + nh], out, AX.X, ALU.max).then_inc(sem("max"), 1)
                        dve.wait_ge(sem("max"), n + 1)
                        dve.tensor_scalar(nb[:, t, h:h + nh], mx[:, t, h:h + nh], -scale, None,
                                          ALU.mult).then_inc(sem("shift"), 1)
                        if n == n_of[0] + 2:
                            normal(0)
                    normal(1)
                    dve.wait_ge(sem("out"), 1)
                    x = core.x[:, cols(b, LEN)]
                    bo = core.c["small"][:, 3:4] if causal else core.c["l3_cols"][:, 2:3]
                    dve.scalar_tensor_tensor(x, psum[:, 5, 0:LEN], bo, x, ALU.add, ALU.add).then_inc(sem("done"), 1)
            st.clear()


def constants():
    c = {}
    f = np.float32
    c["ident"] = np.eye(P, dtype=f)
    c["mean"] = np.full((P, P), 1.0 / P, f)
    c["small"] = np.tile(np.array([1e-5, 1e-6, 1.0, 0.0], f), (P, 1))
    c["below"] = np.tile(np.tril(np.ones((8, 8), f), -1).reshape(1, 64), (P, 1))
    i = np.arange(P)
    c["ones"] = np.ones((P, P), f)
    inside = (i[:, None] < i[None, :]) & (i[:, None] // 64 == i[None, :] // 64)
    c["chunk_mask"] = np.where(inside, 0.0, NEG).astype(f)
    c["block16"] = (i[:, None] // 16 == i[None, :] // 16).astype(f)
    c["reset"] = np.tile((np.arange(BANK) % 64 != 0).astype(f), (P, 1))
    for name, window in (("l1", 64), ("l2", 32)):
        behind = i[:, None] + window - np.arange(window + P)[None, :]
        band = np.where((behind >= 0) & (behind <= window), 0.0, NEG).astype(f)
        c[name + "_band"] = band
        pos = np.arange(LEN, dtype=f)
        half = np.arange(0, 64, 2, dtype=f)
        freqs = pos[:, None] * (f(1.0) / f(10000.0) ** (half / f(64)))[None, :]
        base = (half + f(0.4 * 64)) / f(1.4 * 64)
        scale = base[None, :] ** ((pos - LEN // 2) / f(window // 2))[:, None]
        two = lambda a: np.concatenate([a, a], -1)
        freqs, scale = two(freqs), two(scale)
        sign = np.where(np.arange(64) < 32, -1.0, 1.0).astype(f)
        tab = np.stack([np.cos(freqs) * scale, np.sin(freqs) * scale * sign,
                        np.cos(freqs) / scale, np.sin(freqs) / scale * sign], 1)
        c[name + "_rotary"] = tab.reshape(2, P, 4, 64).transpose(1, 0, 2, 3).astype(f)
    c["head_mask"] = (i[:, None] // 8 == np.arange(16)[None, :]).astype(f)
    c["causal"] = np.where(np.arange(LEN)[None, :] <= P + i[:, None], 0.0, NEG).astype(f)
    return c


def laid_out(inp):
    c = constants()
    f = np.float32
    col = lambda *v: np.ascontiguousarray(np.stack([np.asarray(x, f) for x in v], 1))
    pad = lambda a, n, ax: np.pad(a, [(0, n - a.shape[ax]) if i == ax % a.ndim else (0, 0) for i in range(a.ndim)])
    c["x"] = inp["L0_attn_x"].reshape(TOK, DIM)
    c["l0_w"] = np.stack([inp[f"L0_attn_{n}_w"].T for n in ("A", "B", "C", "D", "out")], 1)
    c["l0_cols"] = col(inp["L0_attn_A_b"], inp["L0_attn_out_b"], inp["L0_attn_norm_w"])
    c["l0_gate"] = inp["L0_ffn_gate_w"]
    c["l0_wg"] = pad(inp["L0_ffn_Wg"], HIDDEN, -1)
    c["l0_wu"] = pad(inp["L0_ffn_Wu"], HIDDEN, -1)
    c["l0_wd"] = pad(inp["L0_ffn_Wd"], HIDDEN, 1)
    c["l0s_wg"] = pad(inp["L0_ffn_Sg"], 256, -1)
    c["l0s_wu"] = pad(inp["L0_ffn_Su"], 256, -1)
    c["l0s_wd"] = pad(inp["L0_ffn_Sd"], 256, 0)
    c["l1_rows"] = np.stack([np.repeat(inp[n].reshape(DIM, 1), P, 1)
                             for n in ("L1_attn_W_beta", "L1_attn_W_alpha")], 1)
    c["l1_w"] = np.stack([inp["L1_attn_W_write"].T, inp["L1_attn_W_read"].T], 1)
    c["l1_scal"] = np.repeat(np.stack([inp["L1_attn_A_log"], inp["L1_attn_dt_bias"]], 1), P, 0)
    for name, heads in (("l1", 8), ("l2", 16)):
        g = lambda n: inp[next(k for k in inp if k.lower() == f"{name}_ffn_{n}".lower())]
        depth, inner = g("wqkv").shape[0], heads * 64
        more = lambda a: np.concatenate([a, a[:1]])
        c[name + "_wqkv"] = more(g("wqkv"))
        c[name + "_wo"] = more(g("wo").reshape(depth, heads // 2, P, DIM).transpose(0, 2, 1, 3))
        w1 = g("w1").reshape(depth, DIM, 2, -1)
        b1 = g("b1").reshape(depth, 2, -1)
        c[name + "_w1"] = pad(w1, HIDDEN, -1).reshape(depth, DIM, 2 * HIDDEN)
        c[name + "_w2"] = pad(g("w2"), HIDDEN, 1).reshape(depth, 3, P, DIM).transpose(0, 2, 1, 3)
        b1 = pad(b1, HIDDEN, -1).reshape(depth, 6, P)
        c[name + "_cols"] = np.concatenate([b1, g("b2")[:, None], g("ln_g")[:, None], g("ln_b")[:, None]],
                                           1).transpose(0, 2, 1)
        qs, ks = g("q_scale"), g("k_scale")
        c[name + "_scales"] = more(np.stack([qs, np.roll(qs, 32, -1), ks, np.roll(ks, 32, -1)], 1))
    c["l2_down"] = inp["L2_attn_Wc_down"]
    kv = inp["L2_attn_Wkv_up"]
    c["l2_w"] = np.concatenate([inp["L2_attn_Wq_up"], np.tile(kv[:, :8], (1, 16)), kv[:, 8:]], 1)
    c["l2_proj"] = inp["L2_attn_Wc_proj"]
    c["l3_w"] = np.stack([inp[f"L3_attn_W{n}"] for n in ("q", "k", "v", "r", "o")], 1)
    c["l3_cols"] = col(inp["L3_attn_u_bias"].reshape(-1), inp["L3_attn_v_bias"].reshape(-1), inp["L3_attn_bo"],
                       inp["L3_attn_gamma"], inp["L3_attn_beta"])
    first = (inp["L3_attn_rel_pos_emb"].shape[0] - 1) // 2 - (LEN - 1)
    c["l3_remb"] = pad(inp["L3_attn_rel_pos_emb"][first:first + 2 * LEN - 1].T, 2 * LEN, -1)
    c["l3_gate"] = inp["L3_ffn_gate_w"]
    gate_up = inp["L3_ffn_gate_up_w"]
    c["l3_wg"], c["l3_wu"] = np.split(gate_up, 2, -1)
    c["l3_wd"] = inp["L3_ffn_down_w"]
    return {k: np.ascontiguousarray(v, f) for k, v in c.items()}


CONST_ALL = ("ident", "mean", "small", "below", "l0_w", "l0_cols", "l0_gate", "ones", "chunk_mask", "block16", "reset",
             "l1_rows", "l1_w", "l1_scal", "l1_band", "l1_rotary", "l2_band",
             "l2_rotary", "head_mask", "causal", "l2_down", "l2_w", "l2_proj", "l3_w", "l3_cols",
             "l3_remb", "l3_gate")


def local_stack(core, level, depth, heads, window):
    nc, dram = core.nc, core.dram
    inner = 3 * heads * 64
    with Stage(core) as st:
        sem = st.sem
        wqkv = st.sb("wqkv", [P, inner])
        wo = st.sb("wo", [P, heads // 2, DIM])
        w1 = st.sb("w1", [P, 2 * HIDDEN])
        w2 = st.sb("w2", [P, HIDDEN // P, DIM])
        wcols = st.sb("cols", [P, 9])
        scales = st.sb("scales", [P, 4, 64])
        tab = st.sb("tab", [P, 2, 4, 64])

        def load_attention(sp, done, at):
            sp.dma_start(wqkv[:, :], dram[level + "_wqkv"][at].rearrange("a p n -> p (a n)")).then_inc(done, 16)
            sp.dma_start(wo[:, :, :], dram[level + "_wo"][at].rearrange("a p i n -> p (a i) n")).then_inc(done, 16)
            sp.dma_start(scales[:, :, :].rearrange("p i n -> p (i n)"),
                         dram[level + "_scales"][at].rearrange("a i n -> a (i n)").partition_broadcast(P)
                         ).then_inc(done, 16)

        with st.block() as block:
            @block.vector
            def _(dve):
                for c in range(CH):
                    dve.tensor_copy(core.y[:, cols(c, BANK)], core.xn[:, cols(c, BANK)]).then_inc(sem("started"), 1)

            @block.sync
            def _(sp):
                load_attention(sp, sem("first"), bass.ds(0, 1))
                sp.wait_ge(sem("first"), 48)
        st.clear()
        with nc.Fori(0, depth) as layer:
            at = bass.ds(layer, 1)
            with st.block() as block:
                @block.vector
                def _(dve):
                    for t in range(2):
                        dve.tensor_tensor(tab[:, t, :, :], core.c[level + "_rotary"][:, t, :, :],
                                          scales[:, :, :], ALU.mult).then_inc(sem("tables"), 1)

                @block.sync
                def _(sp):
                    sp.dma_start(w2[:, :, :], dram[level + "_w2"][at].rearrange("a p i n -> p (a i) n")
                                 ).then_inc(sem("weights"), 16)
                    for buf, name in ((w1, "_w1"), (wcols, "_cols")):
                        sp.dma_start(buf[:, :], dram[level + name][at].rearrange("a p n -> p (a n)")
                                     ).then_inc(sem("weights"), 16)
                    sp.wait_ge(sem("weights"), 48)
            st.clear()
            with Stage(core) as attention:
                local_attention(core, attention, heads, window, wqkv, wo, tab, core.c[level + "_band"])
            layernorm(core, core.y, core.h, 0, wcols[:, 7:8], wcols[:, 8:9], shift=True)
            mlp(core, {"w1": w1, "w2": w2, "cols": wcols},
                lambda sp, done: load_attention(sp, done, bass.ds(layer + 1, 1)))
        with st.block() as block:
            @block.vector
            def _(dve):
                for c in range(CH):
                    dve.tensor_tensor(core.x[:, cols(c, BANK)], core.x[:, cols(c, BANK)],
                                      core.y[:, cols(c, BANK)], ALU.add).then_inc(sem("summed"), 1)
        st.clear()


def program(nc, dram, out, upto=99, start=0):
    with ExitStack() as ctx:
        core = Core(nc, ctx, dram)
        core.comb_d = nc.dram_tensor("comb_d", (8, TOK), F32, kind="Internal").ap()
        core.rel_pitch = 17 * 384
        core.rel_d = nc.dram_tensor("rel_d", (TILES, P * core.rel_pitch), F32, kind="Internal").ap()
        load_constants(core, CONST_ALL)
        load_stream(core)
        if start <= 0:
            layernorm(core, core.x, core.xn, 0)
            if upto >= 1:
                gated_scan(core)
            if upto >= 2:
                experts(core, "l0", 8, HIDDEN, False, "l0s")
        if start <= 1 and upto >= 3:
            layernorm(core, core.x, core.xn, 0)
            delta_rule(core)
        if start <= 1 and upto >= 4:
            local_stack(core, "l1", 2, 8, 64)
        if start <= 2 and upto >= 5:
            layernorm(core, core.x, core.xn, 0)
            wide_attention(core, True)
        if start <= 2 and upto >= 6:
            local_stack(core, "l2", 6, 16, 32)
        if start <= 3 and upto >= 7:
            layernorm(core, core.x, core.xn, 0)
            layernorm(core, core.xn, core.h, 1, core.c["l3_cols"][:, 3:4], core.c["l3_cols"][:, 4:5])
            relative_scores(core)
            wide_attention(core, False)
        if start <= 3 and upto >= 8:
            experts(core, "l3", 8, 256, True, None)
        store_stream(core, core.x, out)


def kernel(**inputs):
    import concourse.bacc as bacc
    from concourse.bass_utils import run_bass_kernel_spmd

    arrays = laid_out({k: np.asarray(v) for k, v in inputs.items()})
    nc = bacc.Bacc("TRN2", target_bir_lowering=False, num_devices=1)
    dram = {k: nc.dram_tensor("in_" + k, v.shape, F32, kind="ExternalInput").ap() for k, v in arrays.items()}
    out = nc.dram_tensor("out", (TOK, DIM), F32, kind="ExternalOutput").ap()
    program(nc, dram, out)
    r = run_bass_kernel_spmd(nc, [{"in_" + k: v for k, v in arrays.items()}], core_ids=[0])
    return r.results[0]["out"].reshape(BATCH, LEN, DIM)
```

```python
from contextlib import ExitStack

import numpy as np

import concourse.bass as bass
from concourse import mybir
from concourse.alu_op_type import AluOpType as ALU

F32 = mybir.dt.float32
ACT = mybir.ActivationFunctionType
AX = mybir.AxisListType

P = 128
BATCH, LEN, DIM = 8, 256, 128
TOK = BATCH * LEN
BANK = 512
CH = TOK // BANK
TILES = TOK // P
HIDDEN = 384
NEG = -1.0e30


class Core:

    def __init__(self, nc, ctx, dram):
        self.nc, self.ctx, self.dram = nc, ctx, dram
        self.psum = ctx.enter_context(nc.psum_tensor("psum", [P, 8, BANK], F32))
        self.x, self.xn, self.y, self.h = (
            ctx.enter_context(nc.sbuf_tensor("stream_" + n, [P, TOK], F32)) for n in ("x", "xn", "y", "h"))
        self.c = {}

    def keep(self, name, shape):
        self.c[name] = self.ctx.enter_context(self.nc.sbuf_tensor("c_" + name, shape, F32))
        return self.c[name]


class Stage:

    count = 0

    def __init__(self, core):
        self.nc, self.core = core.nc, core
        self.ctx = ExitStack()
        self.sems = {}
        Stage.count += 1
        self.tag = f"s{Stage.count}"

    def __enter__(self):
        return self

    def __exit__(self, *args):
        self.ctx.close()

    def sb(self, name, shape):
        return self.ctx.enter_context(self.nc.sbuf_tensor(f"{self.tag}_{name}", shape, F32))

    def sem(self, name):
        if name not in self.sems:
            self.sems[name] = self.ctx.enter_context(self.nc.semaphore(f"{self.tag}_{name}"))
        return self.sems[name]

    def block(self):
        return self.nc.Block(no_gpsimd_drain=True)

    def clear(self):
        nums = sorted(s.num for s in self.sems.values())
        first = last = nums[0]
        for n in nums[1:] + [None]:
            if n != last + 1:
                self.nc.gpsimd.sem_clear(range(first, last + 1))
                first = n
            last = n
        self.nc.all_engine_barrier(sem_only=True)


def cols(i, width, size=None):
    return bass.ds(i * width, size or width)


def over(ap, *dims):
    return bass.AP(ap.tensor, ap.offset, [list(ap.ap[0])] + [list(d) for d in dims])


def load(core, names):
    nc, psum = core.nc, core.psum
    with Stage(core) as st:
        sem = st.sem
        bufs = [(core.keep(n, list(core.dram[n].shape)), core.dram[n]) for n in names]
        rows = st.sb("rows", [P, TILES, P])
        x = core.dram["x"].rearrange("(t p) d -> p t d", p=P)

        def load_rows(q, c):
            q.dma_start(rows[:, 4 * c:4 * c + 4, :], x[:, 4 * c:4 * c + 4, :]).then_inc(sem(f"rows{c}"), 16)

        with st.block() as block:
            @block.sync
            def _(sp):
                sp.dma_start(bufs[0][0][:], bufs[0][1]).then_inc(sem("identity"), 16)
                load_rows(sp, 1)
                load_rows(sp, 3)
                for buf, src in bufs[1::2]:
                    sp.dma_start(buf[:], src).then_inc(sem("loaded_sp"), 16)
                sp.wait_ge(sem("loaded_sp"), 16 * len(bufs[1::2]))

            @block.scalar
            def _(act):
                load_rows(act, 0)
                load_rows(act, 2)
                for buf, src in bufs[2::2]:
                    act.dma_start(buf[:], src).then_inc(sem("loaded_act"), 16)
                act.wait_ge(sem("loaded_act"), 16 * len(bufs[2::2]))

            @block.tensor
            def _(pe):
                pe.wait_ge(sem("identity"), 16)
                for t in range(TILES):
                    if t % 4 == 0:
                        pe.wait_ge(sem(f"rows{t // 4}"), 16)
                    pe.transpose(psum[:, t // 4, cols(t % 4, P)], rows[:, t, :],
                                 core.c["ident"][:, :]).then_inc(sem("turned"), 1)

            @block.vector
            def _(dve):
                for c in range(CH):
                    dve.wait_ge(sem("turned"), 4 * c + 4)
                    dve.tensor_copy(core.x[:, cols(c, BANK)], psum[:, c, :]).then_inc(sem("copied"), 1)
        st.clear()


def store_stream(core, src, out):
    nc, psum = core.nc, core.psum
    with Stage(core) as st:
        sem = st.sem
        rows = st.sb("rows", [P, TILES, P])
        with st.block() as block:
            @block.tensor
            def _(pe):
                for t in range(TILES):
                    pe.transpose(psum[:, t // 4, cols(t % 4, P)], src[:, cols(t, P)],
                                 core.c["ident"][:, :]).then_inc(sem("turned"), 1)

            @block.vector
            def _(dve):
                for c in range(CH):
                    dve.wait_ge(sem("turned"), 4 * c + 4)
                    dve.tensor_copy(rows[:, 4 * c:4 * c + 4, :],
                                    psum[:, c, :].rearrange("p (t d) -> p t d", t=4)).then_inc(sem("copied"), 1)

            @block.sync
            def _(sp):
                for c in range(CH):
                    sp.wait_ge(sem("copied"), c + 1)
                    dst = out.rearrange("(t p) d -> p t d", p=P)[:, 4 * c:4 * c + 4, :]
                    sp.dma_start(dst, rows[:, 4 * c:4 * c + 4, :]).then_inc(sem("stored"), 16)
                sp.wait_ge(sem("stored"), 16 * CH)
        st.clear()


def norm_programs(core, st, src, dst, eps, gain=None, bias=None, shift=False):
    nc, psum = core.nc, core.psum
    sem = st.sem
    sq = st.sb("sq", [P, CH, BANK])
    rstd = st.sb("rstd", [P, TILES])
    ones = st.sb("ones", [P, P])
    diagonal = st.sb("diagonal", [P, CH, BANK])
    shifted = st.sb("shifted", [P, TOK]) if shift else None
    x = shifted if shift else src
    half = P // 2

    def tensor(pe):
        for c in range(CH):
            if shift:
                pe.wait_ge(sem("shifted"), c + 1)
                pe.wait_ge(sem("kept"), c + 1)
            pe.matmul(psum[:, c, :], core.c["mean"][:, :], x[:, cols(c, BANK)],
                      start=True, stop=True).then_inc(sem("mean"), 1)

        def spread(c):
            pe.wait_ge(sem("diagonal"), c + 1)
            pe.matmul(psum[:, 4 + c, :], ones[:, :], diagonal[:, c, :],
                      start=True, stop=True).then_inc(sem("spread"), 1)

        pe.wait_ge(sem("ones"), 1)
        for c in range(CH):
            pe.wait_ge(sem("squared"), c + 1)
            for i in range(4):
                mm = pe.matmul(psum[:, c, i:i + 1], sq[:, c, cols(i, P)], core.c["mean"][:, 0:1],
                               start=True, stop=True)
            mm.then_inc(sem("var"), 1)
        for c in range(CH):
            spread(c)

    def vector(dve):
        for c in range(CH):
            if shift:
                two = shifted[half:, cols(c, BANK)].rearrange("p (b t) -> p b t", b=2)
                of = src[half:, cols(c, BANK)].rearrange("p (b t) -> p b t", b=2)
                dve.memset(two[:, :, 0:1], 0.0)
                dve.tensor_copy(two[:, :, 1:LEN], of[:, :, 0:LEN - 1]).then_inc(sem("shifted"), 1)
        if shift:
            dve.wait_ge(sem("shifted"), CH)
        for c in range(CH):
            if shift:
                dve.wait_ge(sem("kept"), c + 1)
            dve.wait_ge(sem("mean"), c + 1)
            dve.tensor_tensor(dst[:, cols(c, BANK)], x[:, cols(c, BANK)], psum[:, c, :],
                              ALU.subtract).then_inc(sem("centred"), 1)

        def norm(c):
            dve.wait_ge(sem("spread"), c + 1)
            x_c = dst[:, cols(c, BANK)]
            if gain is None:
                dve.tensor_tensor(x_c, x_c, psum[:, 4 + c, :], ALU.mult).then_inc(sem("normed"), 1)
            else:
                dve.scalar_tensor_tensor(x_c, x_c, gain, psum[:, 4 + c, :],
                                         ALU.mult, ALU.mult).then_inc(sem("normed"), 1)

        for c in range(CH):
            dve.wait_ge(sem("centred"), CH)
            dve.wait_ge(sem("std"), c + 1)
            dve.reciprocal(rstd[:, cols(c, 4)], rstd[:, cols(c, 4)]).then_inc(sem("inverse"), 1)
            dve.wait_ge(sem("inverse"), c + 1)
            dve.tensor_tensor(diagonal[:, c, :].rearrange("p (i n) -> p i n", i=4),
                              over(core.c["ident"][:, :], [0, 4], [1, P]),
                              over(rstd[:, cols(c, 4)], [1, 4], [0, P]), ALU.mult).then_inc(sem("diagonal"), 1)
            if c >= 1:
                norm(c - 1)
        norm(CH - 1)

    def scalar(act):
        if shift:
            for c in range(CH):
                act.activation(shifted[0:half, cols(c, BANK)], src[0:half, cols(c, BANK)],
                               ACT.Copy).then_inc(sem("kept"), 1)
        for c in range(CH):
            act.wait_ge(sem("centred"), c + 1)
            act.activation(sq[:, c, :], dst[:, cols(c, BANK)], ACT.Square).then_inc(sem("squared"), 1)
        for c in range(CH):
            act.wait_ge(sem("var"), c + 1)
            act.activation(rstd[:, cols(c, 4)], psum[:, c, 0:4], ACT.Sqrt,
                           bias=core.c["small"][:, eps:eps + 1]).then_inc(sem("std"), 1)

    def add_bias(act, c):
        act.wait_ge(sem("normed"), c + 1)
        act.activation(dst[:, cols(c, BANK)], dst[:, cols(c, BANK)], ACT.Identity,
                       bias=bias).then_inc(sem("scaled"), 1)

    def gpsimd(pool):
        pool.memset(ones[:, :], 1.0).then_inc(sem("ones"), 1)

    return tensor, vector, gpsimd, scalar, add_bias


def layernorm(core, src, dst, eps, gain=None, bias=None):
    with Stage(core) as st:
        tensor, vector, gpsimd, scalar, add_bias = norm_programs(core, st, src, dst, eps, gain, bias)
        with st.block() as block:
            block.tensor(tensor)
            block.vector(vector)
            block.gpsimd(gpsimd)

            @block.scalar
            def _(act):
                scalar(act)
                if gain is not None:
                    for c in range(CH):
                        add_bias(act, c)
        st.clear()


def gated_scan(core):
    nc, psum = core.nc, core.psum
    with Stage(core) as st:
        sem = st.sem
        sq, diagonal, xr, part, residual = (
            st.sb(n, [P, CH, BANK]) for n in ("sq", "diagonal", "xr", "part", "residual"))
        a, c, d, db, h = (st.sb(n, [P, 2, BANK]) for n in ("a", "c", "d", "db", "h"))
        rrms = st.sb("rrms", [P, TILES])
        ones = st.sb("ones", [P, P])
        w = core.c["l0_w"]
        A_b, out_b, norm_w = (core.c["l0_cols"][:, i:i + 1] for i in range(3))
        A_BANK, B_BANK, D_BANK, C_BANK = 4, 5, 6, 7
        with st.block() as block:
            @block.gpsimd
            def _(pool):
                pool.memset(ones[:, :], 1.0).then_inc(sem("ones"), 1)

            @block.scalar
            def _(act):
                for g in range(CH):
                    act.activation(sq[:, g, :], core.xn[:, cols(g, BANK)], ACT.Square).then_inc(sem("squared"), 1)
                for g in range(CH):
                    act.wait_ge(sem("mean_square"), g + 1)
                    act.activation(rrms[:, cols(g, 4)], psum[:, g, 0:4], ACT.Sqrt,
                                   bias=core.c["small"][:, 0:1]).then_inc(sem("rms"), 1)
                for g in range(CH):
                    act.wait_ge(sem("products"), 4 * g + 1)
                    if g >= 2:
                        act.wait_ge(sem("scanned"), 2 * (g - 1))
                    act.activation(a[:, g % 2, :], psum[:, A_BANK, :], ACT.Sigmoid, bias=A_b).then_inc(sem("a"), 1)
                    act.wait_ge(sem("products"), 4 * g + 3)
                    if g >= 2:
                        act.wait_ge(sem("db"), g - 1)
                    act.activation(d[:, g % 2, :], psum[:, D_BANK, :], ACT.Sigmoid).then_inc(sem("d"), 1)
                    act.wait_ge(sem("products"), 4 * g + 4)
                    if g >= 2:
                        act.wait_ge(sem("gated"), g - 1)
                    act.activation(c[:, g % 2, :], psum[:, C_BANK, :], ACT.Sigmoid).then_inc(sem("c"), 1)

            @block.tensor
            def _(pe):
                for g in range(CH):
                    pe.wait_ge(sem("squared"), g + 1)
                    for i in range(4):
                        mm = pe.matmul(psum[:, g, i:i + 1], sq[:, g, cols(i, P)], core.c["mean"][:, 0:1],
                                       start=True, stop=True)
                    mm.then_inc(sem("mean_square"), 1)
                pe.wait_ge(sem("ones"), 1)
                for g in range(CH):
                    pe.wait_ge(sem("diagonal"), g + 1)
                    pe.matmul(psum[:, 4 + g, :], ones[:, :], diagonal[:, g, :], start=True,
                              stop=True).then_inc(sem("spread"), 1)

                def project_out(g):
                    pe.wait_ge(sem("gated"), g + 1)
                    pe.matmul(psum[:, g, :], w[:, 4, :], h[:, g % 2, :], start=True, stop=True).then_inc(sem("out"), 1)

                pe.wait_ge(sem("rms_normed"), CH)
                for g in range(CH):
                    for bank, k, read in ((A_BANK, 0, "a"), (B_BANK, 1, "db"), (D_BANK, 3, "d"), (C_BANK, 2, "c")):
                        if g >= 1:
                            pe.wait_ge(sem(read), g)
                        pe.matmul(psum[:, bank, :], w[:, k, :], xr[:, g, :], start=True,
                                  stop=True).then_inc(sem("products"), 1)
                    if g >= 1:
                        project_out(g - 1)
                project_out(CH - 1)

            @block.vector
            def _(dve):
                for g in range(CH):
                    dve.wait_ge(sem("rms"), g + 1)
                    dve.reciprocal(rrms[:, cols(g, 4)], rrms[:, cols(g, 4)]).then_inc(sem("inverse_rms"), 1)
                    dve.wait_ge(sem("inverse_rms"), g + 1)
                    dve.tensor_tensor(diagonal[:, g, :].rearrange("p (i n) -> p i n", i=4),
                                      over(core.c["ident"][:, :], [0, 4], [1, P]),
                                      over(rrms[:, cols(g, 4)], [1, 4], [0, P]), ALU.mult).then_inc(sem("diagonal"), 1)
                for g in range(CH):
                    dve.wait_ge(sem("spread"), g + 1)
                    dve.scalar_tensor_tensor(xr[:, g, :], core.xn[:, cols(g, BANK)], norm_w, psum[:, 4 + g, :],
                                             ALU.mult, ALU.mult).then_inc(sem("rms_normed"), 1)

                def finish(g):
                    dve.wait_ge(sem("out"), g + 1)
                    dve.wait_ge(sem("residual"), g + 1)
                    dve.scalar_tensor_tensor(core.x[:, cols(g, BANK)], psum[:, g, :], out_b, residual[:, g, :],
                                             ALU.add, ALU.add).then_inc(sem("done"), 1)

                for g in range(CH):
                    dve.tensor_tensor(residual[:, g, :], core.x[:, cols(g, BANK)], core.xn[:, cols(g, BANK)],
                                      ALU.add).then_inc(sem("residual"), 1)
                    dve.wait_ge(sem("d"), g + 1)
                    dve.wait_ge(sem("products"), 4 * g + 2)
                    dve.tensor_tensor(db[:, g % 2, :], d[:, g % 2, :], psum[:, B_BANK, :], ALU.mult).then_inc(sem("db"), 1)
                    dve.wait_ge(sem("db"), g + 1)
                    dve.wait_ge(sem("a"), g + 1)
                    for b in range(BANK // LEN):
                        dve.tensor_tensor_scan(part[:, g, cols(b, LEN)], a[:, g % 2, cols(b, LEN)],
                                               db[:, g % 2, cols(b, LEN)], 0.0, ALU.mult, ALU.add).then_inc(sem("scanned"), 1)
                    dve.wait_ge(sem("scanned"), 2 * (g + 1))
                    dve.wait_ge(sem("c"), g + 1)
                    if g >= 2:
                        dve.wait_ge(sem("out"), g - 1)
                    dve.tensor_tensor(h[:, g % 2, :], part[:, g, :], c[:, g % 2, :], ALU.mult).then_inc(sem("gated"), 1)
                    if g >= 1:
                        finish(g - 1)
                finish(CH - 1)
        st.clear()


def experts(core, level, n_exp, hidden, softmax_first, shared):
    nc, psum, dram = core.nc, core.psum, core.dram
    nic = hidden // P
    wg_d, wu_d, wd_d = (dram[f"{level}_{n}"] for n in ("wg", "wu", "wd"))
    with Stage(core) as st:
        sem = st.sem
        gate_w = core.c[level + "_gate"]
        E = n_exp
        logits = st.sb("logits", [P, TILES, E])
        comb = st.sb("comb", [P, TILES, E])
        top = st.sb("top", [P, TILES])
        total = st.sb("total", [P, TILES])
        gt = st.sb("gt", [P, TILES, E, E])
        eq = st.sb("eq", [P, TILES, E, E])
        rank = st.sb("rank", [P, TILES, E])
        combT = st.sb("combT", [E, TOK])
        mine = (lambda t: t[:, :, :].unsqueeze(3).to_broadcast([P, TILES, E, E]))
        with st.block() as block:
            @block.tensor
            def _(pe):
                for t in range(TILES):
                    mm = pe.matmul(psum[:, 0, cols(t, E)], core.xn[:, cols(t, P)], gate_w[:, :],
                                   start=True, stop=True)
                mm.then_inc(sem("logits"), 1)
                pe.wait_ge(sem("weights"), 1)
                for t in range(TILES):
                    mm = pe.transpose(psum[0:E, 4 + t // 4, cols(t % 4, P)], comb[:, t, :], core.c["ident"][:, :])
                mm.then_inc(sem("turned"), 1)

            @block.vector
            def _(dve):
                step = [0]

                def chained(ins):
                    step[0] += 1
                    ins.then_inc(sem("vector_step"), 1)
                    dve.wait_ge(sem("vector_step"), step[0])

                dve.wait_ge(sem("logits"), 1)
                chained(dve.tensor_copy(logits[:, :, :], psum[:, 0, 0:TILES * E].rearrange("p (t e) -> p t e", e=E)))
                chained(dve.tensor_reduce(top[:, :], logits[:, :, :], AX.X, ALU.max))
                dve.tensor_tensor(comb[:, :, :], logits[:, :, :],
                                  over(top[:, :], [1, TILES], [0, E]), ALU.subtract).then_inc(sem("less_top"), 1)
                dve.wait_ge(sem("exp"), 1)
                if softmax_first:
                    chained(dve.tensor_reduce(total[:, :], comb[:, :, :], AX.X, ALU.add))
                    chained(dve.reciprocal(total[:, :], total[:, :]))
                    chained(dve.tensor_tensor(comb[:, :, :], comb[:, :, :],
                                              over(total[:, :], [1, TILES], [0, E]), ALU.mult))
                    chained(dve.tensor_copy(logits[:, :, :], comb[:, :, :]))
                e_ap = over(logits[:, :, :], [E, TILES], [1, E], [0, E])
                f_ap = over(logits[:, :, :], [E, TILES], [0, E], [1, E])
                chained(dve.tensor_tensor(gt[:, :, :, :], f_ap, e_ap, ALU.is_gt))
                chained(dve.tensor_tensor(eq[:, :, :, :], f_ap, e_ap, ALU.is_equal))
                chained(dve.tensor_tensor(eq[:, :, :, :].rearrange("p t e f -> p t (e f)"),
                                          eq[:, :, :, :].rearrange("p t e f -> p t (e f)"),
                                          over(core.c["below"][:, :], [0, TILES], [1, E * E]), ALU.mult))
                chained(dve.tensor_tensor(gt[:, :, :, :], gt[:, :, :, :], eq[:, :, :, :], ALU.add))
                chained(dve.tensor_reduce(rank[:, :, :], gt[:, :, :, :], AX.X, ALU.add))
                chained(dve.tensor_scalar(rank[:, :, :], rank[:, :, :], 1.5, None, ALU.is_lt))
                chained(dve.tensor_tensor(comb[:, :, :], comb[:, :, :], rank[:, :, :], ALU.mult))
                chained(dve.tensor_reduce(total[:, :], comb[:, :, :], AX.X, ALU.add))
                chained(dve.reciprocal(total[:, :], total[:, :]))
                dve.tensor_tensor(comb[:, :, :], comb[:, :, :], over(total[:, :], [1, TILES], [0, E]),
                                  ALU.mult).then_inc(sem("weights"), 1)
                dve.wait_ge(sem("turned"), 1)
                dve.tensor_copy(combT[:, :], psum[0:E, 4:8, :].rearrange("p b n -> p (b n)")).then_inc(sem("combT"), 1)

            @block.scalar
            def _(act):
                act.wait_ge(sem("less_top"), 1)
                act.activation(comb[:, :, :], comb[:, :, :], ACT.Exp).then_inc(sem("exp"), 1)

            @block.sync
            def _(sp):
                sp.wait_ge(sem("combT"), 1)
                sp.dma_start(core.comb_d, combT[:, :]).then_inc(sem("stored"), 16)
                sp.wait_ge(sem("stored"), 16)
        st.clear()

    with Stage(core) as st:
        sem = st.sem
        sg = st.sb("sg", [P, 2, BANK])
        hid = st.sb("hid", [P, 2, BANK])
        wg = st.sb("wg", [P, 2, hidden])
        wu = st.sb("wu", [P, 2, hidden])
        wd = st.sb("wd", [P, 2, nic, DIM])
        cb = st.sb("cb", [P, 2, TOK])
        xc = st.sb("xc", [P, 2, BANK])

        def run(block, jobs, weigh, first):
            steps = [(j, buf, c, ic) for j, (buf, n) in enumerate(jobs) for c in range(CH) for ic in range(n)]
            units = [(j, buf, c) for j, (buf, n) in enumerate(jobs) for c in range(CH)]

            @block.tensor
            def _(pe):
                if first:
                    for c in range(CH):
                        pe.matmul(psum[:, 4 + c, :], core.c["ident"][:, :], core.x[:, cols(c, BANK)],
                                  start=True, stop=False, skip_group_check=True)

                def up(k):
                    j, buf, c, ic = steps[k]
                    if c == 0 and ic == 0 and not (weigh and j == 0):
                        pe.wait_ge(sem(f"w{j}"), 32)
                    rhs = core.xn[:, cols(c, BANK)]
                    if k >= 2:
                        pe.wait_ge(sem("hidden"), k - 1)
                    pe.matmul(psum[:, k % 2, :], wg[:, buf, cols(ic, P)], rhs, start=True,
                              stop=True).then_inc(sem("gate"), 1)
                    if weigh:
                        pe.wait_ge(sem("weighed"), units.index((j, buf, c)) + 1)
                        rhs = xc[:, units.index((j, buf, c)) % 2, :]
                    pe.matmul(psum[:, 2 + k % 2, :], wu[:, buf, cols(ic, P)], rhs, start=True,
                              stop=True).then_inc(sem("up"), 1)

                def down(k):
                    j, buf, c, ic = steps[k]
                    if c == 0 and ic == 0 and not (weigh and j == 0):
                        pe.wait_ge(sem(f"wd{j}"), 16)
                    pe.wait_ge(sem("hidden"), k + 1)
                    pe.matmul(psum[:, 4 + c, :], wd[:, buf, ic, :], hid[:, k % 2, :], start=False,
                              stop=False, skip_group_check=True).then_inc(sem("down"), 1)

                up(0)
                for k in range(len(steps)):
                    if k + 1 < len(steps):
                        up(k + 1)
                    down(k)

            @block.scalar
            def _(act):
                for k in range(len(steps)):
                    act.wait_ge(sem("gate"), k + 1)
                    if k >= 2:
                        act.wait_ge(sem("hidden"), k - 1)
                    act.activation(sg[:, k % 2, :], psum[:, k % 2, :], ACT.Silu).then_inc(sem("silu"), 1)

            @block.vector
            def _(dve):
                done = [0]

                def weigh_chunk(u):
                    j, buf, c = units[u]
                    if c == 0 and j > 0:
                        dve.wait_ge(sem(f"cb{j}"), 16)
                    if u >= 2:
                        before = sum(1 for s in steps if units.index(s[:3]) <= u - 2)
                        dve.wait_ge(sem("up"), before)
                    dve.tensor_tensor(xc[:, u % 2, :], core.xn[:, cols(c, BANK)], cb[:, buf, cols(c, BANK)],
                                      ALU.mult).then_inc(sem("weighed"), 1)
                if weigh:
                    weigh_chunk(0)
                for k in range(len(steps)):
                    j, buf, c, ic = steps[k]
                    if weigh and ic == 0 and units.index((j, buf, c)) + 1 < len(units):
                        weigh_chunk(units.index((j, buf, c)) + 1)
                    dve.wait_ge(sem("silu"), k + 1)
                    dve.wait_ge(sem("up"), k + 1)
                    if k >= 2:
                        dve.wait_ge(sem("down"), k - 1)
                    dve.tensor_tensor(hid[:, k % 2, :], sg[:, k % 2, :], psum[:, 2 + k % 2, :],
                                      ALU.mult).then_inc(sem("hidden"), 1)

        def load(q, buf, e, j):
            q.dma_start(wg[:, buf, :], wg_d[e, :, :].rearrange("a p n -> p (a n)")).then_inc(sem(f"w{j}"), 16)
            q.dma_start(wu[:, buf, :], wu_d[e, :, :].rearrange("a p n -> p (a n)")).then_inc(sem(f"w{j}"), 16)
            q.dma_start(wd[:, buf, :, :], wd_d[e, :, :].rearrange("a (c p) n -> p (a c) n", p=P)).then_inc(sem(f"wd{j}"), 16)
            q.dma_start(cb[:, buf, :], core.comb_d[e, :].partition_broadcast(P)).then_inc(sem(f"cb{j}"), 16)

        def loaded(q, j):
            q.wait_ge(sem(f"w{j}"), 32)
            q.wait_ge(sem(f"wd{j}"), 16)
            q.wait_ge(sem(f"cb{j}"), 16)

        with st.block() as block:
            if shared:
                run(block, [(0, dram[shared + "_wg"].shape[1] // P)], False, True)
            else:
                @block.tensor
                def _(pe):
                    for c in range(CH):
                        mm = pe.matmul(psum[:, 4 + c, :], core.c["ident"][:, :], core.x[:, cols(c, BANK)],
                                       start=True, stop=False, skip_group_check=True)
                    mm.then_inc(sem("opened"), 1)

            @block.sync
            def _(sp):
                if shared:
                    n = dram[shared + "_wg"].shape[1]
                    sp.dma_start(wg[:, 0, 0:n], dram[shared + "_wg"]).then_inc(sem("w0"), 16)
                    sp.dma_start(wu[:, 0, 0:n], dram[shared + "_wu"]).then_inc(sem("w0"), 16)
                    sp.dma_start(wd[:, 0, 0:n // P, :],
                                 dram[shared + "_wd"].rearrange("(c p) n -> p c n", p=P)).then_inc(sem("wd0"), 16)
                load(sp, 1, bass.ds(0, 1), "_next")
                loaded(sp, "_next")
        st.clear()
        per = n_exp // 2
        with nc.Fori(0, 2) as half:
            with st.block() as block:
                run(block, [(1 - j % 2, nic) for j in range(per)], True, False)

                @block.sync
                def _(sp):
                    for j in range(1, per + 1):
                        if j >= 2:
                            sp.wait_ge(sem("down"), CH * nic * (j - 1))
                        if j < per:
                            load(sp, 1 - j % 2, bass.ds(half * per + j, 1), j)
                        else:
                            load(sp, 1 - j % 2, bass.ds(per - half * per, 1), "_next")
                    loaded(sp, "_next")
            st.clear()
        with st.block() as block:
            @block.vector
            def _(dve):
                for c in range(CH):
                    dve.tensor_copy(core.x[:, cols(c, BANK)], psum[:, 4 + c, :]).then_inc(sem("copied"), 1)
        st.clear()


def delta_rule(core):
    nc, psum = core.nc, core.psum
    C = 64
    NC = BANK // C
    NT = BANK // P
    with Stage(core) as st:
        sem = st.sem
        wide = lambda n: st.sb(n, [P, NT, P])
        flat = lambda t: t[:, :, :].rearrange("p t n -> p (t n)")
        bank = lambda i: psum[:, i, :].rearrange("p (t n) -> p t n", t=NT)
        sq, norm, rk, wk, beta, z, soft, cum, dec, tail = (
            wide(n) for n in ("sq", "norm", "rk", "wk", "beta", "z", "soft", "cum", "dec", "tail"))
        wks, wkd, wkt, rkd, xb, ncum = (wide(n) for n in ("wks", "wkd", "wkt", "rkd", "xb", "ncum"))
        LT, T, N, TD, ND, TO, NO, intraT = (wide(n) for n in ("LT", "T", "N", "TD", "ND", "TO", "NO", "intraT"))
        T2, N2, T4, N4, N8, X1, X2, X3, X4 = (wide(n) for n in ("T2", "N2", "T4", "N4", "N8", "X1", "X2", "X3", "X4"))
        Q, QT, Z1, Z2, PP, R = (wide(n) for n in ("Q", "QT", "Z1", "Z2", "PP", "R"))
        wkd_t, wkt_t, vsc, U, WT, vn, oT = (wide(n) for n in ("wkd_t", "wkt_t", "vsc", "U", "WT", "vn", "oT"))
        S = st.sb("S", [P, 2, P])
        neg_a = st.sb("neg_a", [P, 1])
        dt_bias = core.c["l1_scal"][:, 1:2]
        ident4 = over(core.c["ident"][:, :], [0, NT], [1, P])
        with st.block() as block:
            @block.scalar
            def _(act):
                act.activation(neg_a[:, :], core.c["l1_scal"][:, 0:1], ACT.Exp).then_inc(sem("exp_a"), 1)

            @block.vector
            def _(dve):
                dve.wait_ge(sem("exp_a"), 1)
                dve.tensor_scalar(neg_a[:, :], neg_a[:, :], -1.0, None, ALU.mult).then_inc(sem("neg_a"), 1)
        st.clear()
        with nc.Fori(0, CH) as g:
            with st.block() as block:
                x_g = core.xn[:, cols(g, BANK)]

                @block.scalar
                def _(act):
                    act.activation(flat(sq), x_g, ACT.Square).then_inc(sem("squared"), 1)
                    act.wait_ge(sem("mean_square"), 1)
                    act.activation(flat(norm), psum[:, 0, :], ACT.Sqrt, scale=float(P)).then_inc(sem("norm"), 1)
                    act.wait_ge(sem("abs_z"), 1)
                    act.activation(flat(soft), flat(soft), ACT.Exp, scale=-1.0).then_inc(sem("exp_z"), 1)
                    act.wait_ge(sem("exp_z"), 1)
                    act.activation(flat(soft), flat(soft), ACT.Ln, bias=core.c["small"][:, 2:3]).then_inc(sem("ln_z"), 1)
                    act.wait_ge(sem("beta_logit"), 1)
                    act.activation(flat(beta), psum[:, 1, :], ACT.Sigmoid).then_inc(sem("beta"), 1)
                    act.wait_ge(sem("cum"), 1)
                    act.activation(flat(dec), flat(cum), ACT.Exp).then_inc(sem("dec"), 1)
                    act.wait_ge(sem("to_end"), 1)
                    act.activation(flat(tail), flat(tail), ACT.Exp).then_inc(sem("tail"), 1)
                    act.wait_ge(sem("masked"), 1)
                    act.activation(flat(LT), flat(LT), ACT.Exp).then_inc(sem("LT"), 1)
                    act.wait_ge(sem("N_turned"), 1)
                    act.activation(flat(N), psum[:, 6, :], ACT.Copy).then_inc(sem("N"), 1)
                    act.wait_ge(sem("T2"), 1)
                    act.activation(flat(T2), psum[:, 0, :], ACT.Copy).then_inc(sem("T2_kept"), 1)
                    act.wait_ge(sem("T4"), 1)
                    act.activation(flat(T4), psum[:, 2, :], ACT.Copy).then_inc(sem("T4_kept"), 1)
                    for i, (buf, b) in enumerate(((wkd_t, 6), (wkt_t, 7), (vsc, 3))):
                        act.wait_ge(sem("token_major"), i + 1)
                        act.activation(flat(buf), psum[:, b, :], ACT.Copy).then_inc(sem("token_major_kept"), 1)
                    act.wait_ge(sem("N8"), 1)
                    act.activation(flat(N8), psum[:, 4, :], ACT.Copy).then_inc(sem("N8_kept"), 1)
                    act.wait_ge(sem("QT"), 1)
                    act.activation(flat(QT), psum[:, 3, :], ACT.Copy).then_inc(sem("QT_kept"), 1)
                    act.wait_ge(sem("P_turned"), 1)
                    act.activation(flat(PP), psum[:, 4, :], ACT.Copy).then_inc(sem("P_kept"), 1)
                    act.wait_ge(sem("WT"), 1)
                    act.activation(flat(WT), psum[:, 1, :], ACT.Copy).then_inc(sem("WT_kept"), 1)

                @block.tensor
                def _(pe):
                    def tiles(b, lhsT, rhs, name, turn=False):
                        for t in range(NT):
                            if turn:
                                mm = pe.transpose(bank(b)[:, t, :], lhsT[:, t, :], core.c["ident"][:, :])
                            else:
                                mm = pe.matmul(bank(b)[:, t, :], lhsT[:, t, :], rhs[:, t, :], start=True, stop=True)
                        mm.then_inc(sem(name), 1)

                    pe.matmul(psum[:, 2, :], core.c["l1_rows"][:, 1, :], x_g, start=True, stop=True).then_inc(sem("alpha_logit"), 1)
                    pe.wait_ge(sem("squared"), 1)
                    pe.matmul(psum[:, 0, :], core.c["mean"][:, :], flat(sq), start=True, stop=True).then_inc(sem("mean_square"), 1)
                    pe.matmul(psum[:, 1, :], core.c["l1_rows"][:, 0, :], x_g, start=True, stop=True).then_inc(sem("beta_logit"), 1)
                    pe.wait_ge(sem("neg_cum"), 1)
                    for t in range(NT):
                        pe.matmul(bank(3)[:, t, :], core.c["ones"][0:1, :], cum[0:1, t, :], start=True, stop=False)
                        mm = pe.matmul(bank(3)[:, t, :], ncum[0:1, t, :], core.c["ones"][0:1, :], start=False, stop=True)
                    mm.then_inc(sem("cum_diff"), 1)
                    pe.wait_ge(sem("wks"), 1)
                    tiles(4, wk, wks, "gram")
                    tiles(5, wk, rk, "reads")
                    pe.wait_ge(sem("T"), 1)
                    tiles(6, T, None, "N_turned", turn=True)
                    pe.wait_ge(sem("NO"), 1)
                    tiles(0, ND, TD, "T2")
                    tiles(1, TD, ND, "N2")
                    pe.wait_ge(sem("N2_kept"), 1)
                    pe.wait_ge(sem("T2_kept"), 1)
                    tiles(2, N2, T2, "T4")
                    pe.wait_ge(sem("N"), 1)
                    tiles(5, T2, N2, "N4")
                    tiles(1, N2, X1, "X2")
                    pe.wait_ge(sem("scaled"), 1)
                    tiles(6, wkd, None, "token_major", turn=True)
                    tiles(7, wkt, None, "token_major", turn=True)
                    for t in range(NT):
                        mm = pe.matmul(bank(3)[:, t, :], xb[:, t, :], core.c["l1_w"][:, 0, :], start=True, stop=True)
                    mm.then_inc(sem("token_major"), 1)
                    pe.wait_ge(sem("N4_kept"), 1)
                    pe.wait_ge(sem("T4_kept"), 1)
                    tiles(4, T4, N4, "N8")
                    pe.wait_ge(sem("X2_kept"), 1)
                    tiles(0, N4, X2, "X3")
                    pe.wait_ge(sem("X3_kept"), 1)
                    pe.wait_ge(sem("N8_kept"), 1)
                    tiles(1, N8, X3, "X4")
                    pe.wait_ge(sem("X4_kept"), 1)
                    tiles(2, NO, X4, "Q")
                    pe.wait_ge(sem("token_major_kept"), 3)
                    tiles(3, X4, NO, "QT")
                    tiles(4, X4, None, "P_turned", turn=True)
                    pe.wait_ge(sem("QT_kept"), 1)
                    pe.wait_ge(sem("Q_kept"), 1)
                    tiles(5, QT, Q, "Q2")
                    pe.wait_ge(sem("Z1_kept"), 1)
                    tiles(6, QT, Z1, "Z2")
                    pe.wait_ge(sem("P_kept"), 1)
                    pe.wait_ge(sem("Z2_kept"), 1)
                    tiles(7, PP, Z2, "R")
                    pe.wait_ge(sem("R_kept"), 1)
                    tiles(0, R, vsc, "U")
                    tiles(1, wkd_t, R, "WT")
                    done = 0
                    for c in range(4):
                        for b in range(2):
                            t, lo = 2 * b + c // 2, (c % 2) * C
                            half = slice(lo, lo + C)
                            if c > 0:
                                pe.wait_ge(sem("WT_kept"), 1)
                                pe.wait_ge(sem("state"), 2 * (c - 1) + b + 1)
                                pe.matmul(psum[half, 2 + b, 0:P], WT[:, t, half], S[:, b, :],
                                          start=True, stop=True).then_inc(sem("read"), 1)
                        for b in range(2):
                            t, lo = 2 * b + c // 2, (c % 2) * C
                            half = slice(lo, lo + C)
                            if c > 0:
                                pe.matmul(psum[:, 4 + b, cols(c, C)], S[:, b, :], rkd[:, t, half],
                                          start=True, stop=False)
                            pe.wait_ge(sem("v_new"), 2 * c + b + 1)
                            mm = pe.matmul(psum[:, 4 + b, cols(c, C)], vn[half, t, :], intraT[half, t, half],
                                           start=(c == 0), stop=True)
                            if c == 3:
                                mm.then_inc(sem("outputs"), 1)
                            if c < 3:
                                mm = pe.matmul(psum[:, 6 + b, 0:P], wkt_t[half, t, :], vn[half, t, :],
                                               start=True, stop=True)
                                mm.then_inc(sem("write"), 1)
                    pe.wait_ge(sem("oT"), 1)
                    pe.matmul(psum[:, 0, :], core.c["l1_w"][:, 1, :], flat(oT), start=True, stop=True).then_inc(sem("projected"), 1)

                @block.vector
                def _(dve):
                    def keep(buf, b, name, wait):
                        dve.wait_ge(sem(wait), 1)
                        dve.tensor_copy(flat(buf), psum[:, b, :]).then_inc(sem(name), 1)

                    dve.wait_ge(sem("alpha_logit"), 1)
                    dve.tensor_scalar(flat(z), psum[:, 2, :], dt_bias, None, ALU.add).then_inc(sem("z"), 1)
                    dve.wait_ge(sem("z"), 1)
                    dve.scalar_tensor_tensor(flat(soft), flat(z), -1.0, flat(z), ALU.mult, ALU.max).then_inc(sem("abs_z"), 1)
                    dve.wait_ge(sem("norm"), 1)
                    dve.tensor_scalar(flat(norm), flat(norm), 1e-12, None, ALU.max).then_inc(sem("guarded"), 1)
                    dve.wait_ge(sem("guarded"), 1)
                    dve.reciprocal(flat(norm), flat(norm)).then_inc(sem("inverse"), 1)
                    dve.wait_ge(sem("inverse"), 1)
                    dve.tensor_tensor(flat(rk), x_g, flat(norm), ALU.mult).then_inc(sem("rk"), 1)
                    dve.wait_ge(sem("rk"), 1)
                    wk2 = flat(wk).rearrange("p (b t) -> p b t", b=2)
                    rk2 = flat(rk).rearrange("p (b t) -> p b t", b=2)
                    dve.memset(wk2[:, :, 0:1], 0.0).then_inc(sem("wk"), 1)
                    dve.tensor_copy(wk2[:, :, 1:LEN], rk2[:, :, 0:LEN - 1]).then_inc(sem("wk"), 1)
                    dve.wait_ge(sem("ln_z"), 1)
                    dve.scalar_tensor_tensor(flat(z), flat(z), 0.0, flat(soft), ALU.max, ALU.add).then_inc(sem("softplus"), 1)
                    dve.wait_ge(sem("softplus"), 1)
                    dve.tensor_scalar(flat(z), flat(z), neg_a[:, :], None, ALU.mult).then_inc(sem("log_decay"), 1)
                    dve.wait_ge(sem("log_decay"), 1)
                    dve.tensor_tensor_scan(flat(cum), core.c["reset"][:, :], flat(z), 0.0, ALU.mult, ALU.add).then_inc(sem("cum"), 1)
                    dve.wait_ge(sem("cum"), 1)
                    dve.tensor_scalar(flat(ncum)[0:1, :], flat(cum)[0:1, :], -1.0, None, ALU.mult).then_inc(sem("neg_cum"), 1)
                    ends = over(flat(cum)[:, C - 1:], [C, NC], [0, C])
                    dve.tensor_tensor(flat(tail).rearrange("p (c t) -> p c t", c=NC), ends,
                                      flat(cum).rearrange("p (c t) -> p c t", c=NC), ALU.subtract).then_inc(sem("to_end"), 1)
                    dve.wait_ge(sem("wk"), 2)
                    dve.wait_ge(sem("beta"), 1)
                    dve.tensor_tensor(flat(wks), flat(wk), flat(beta), ALU.mult).then_inc(sem("wks"), 1)
                    dve.tensor_tensor(flat(xb), x_g, flat(beta), ALU.mult).then_inc(sem("xb"), 1)
                    dve.wait_ge(sem("cum_diff"), 1)
                    dve.tensor_tensor(flat(LT).rearrange("p (t n) -> p t n", t=NT), bank(3),
                                      over(core.c["chunk_mask"][:, :], [0, NT], [1, P]), ALU.add).then_inc(sem("masked"), 1)
                    dve.wait_ge(sem("dec"), 1)
                    dve.wait_ge(sem("wks"), 1)
                    dve.tensor_tensor(flat(wkd), flat(wks), flat(dec), ALU.mult)
                    dve.tensor_tensor(flat(rkd), flat(rk), flat(dec), ALU.mult)
                    dve.wait_ge(sem("tail"), 1)
                    dve.tensor_tensor(flat(wkt), flat(wk), flat(tail), ALU.mult).then_inc(sem("scaled"), 1)
                    dve.wait_ge(sem("LT"), 1)
                    dve.wait_ge(sem("gram"), 1)
                    dve.scalar_tensor_tensor(flat(T), psum[:, 4, :], -1.0, flat(LT), ALU.mult, ALU.mult).then_inc(sem("T"), 1)
                    dve.wait_ge(sem("reads"), 1)
                    dve.tensor_tensor(flat(intraT), psum[:, 5, :], flat(LT), ALU.mult).then_inc(sem("intraT"), 1)
                    dve.wait_ge(sem("T"), 1)
                    diag = over(core.c["block16"][:, :], [0, NT], [1, P])
                    dve.tensor_tensor(TD[:, :, :], T[:, :, :], diag, ALU.mult).then_inc(sem("TD"), 1)
                    dve.wait_ge(sem("TD"), 1)
                    dve.tensor_tensor(X1[:, :, :], TD[:, :, :], ident4, ALU.add).then_inc(sem("X1"), 1)
                    dve.wait_ge(sem("N"), 1)
                    dve.tensor_tensor(ND[:, :, :], N[:, :, :], diag, ALU.mult).then_inc(sem("ND"), 1)
                    dve.wait_ge(sem("ND"), 1)
                    dve.tensor_tensor(NO[:, :, :], N[:, :, :], ND[:, :, :], ALU.subtract).then_inc(sem("NO"), 1)
                    keep(N2, 1, "N2_kept", "N2")
                    keep(N4, 5, "N4_kept", "N4")

                    def plus(buf, b, old, name, wait):
                        dve.wait_ge(sem(wait), 1)
                        dve.tensor_tensor(flat(buf), psum[:, b, :], flat(old), ALU.add).then_inc(sem(name), 1)

                    plus(X2, 1, X1, "X2_kept", "X2")
                    dve.wait_ge(sem("X2_kept"), 1)
                    plus(X3, 0, X2, "X3_kept", "X3")
                    dve.wait_ge(sem("X3_kept"), 1)
                    plus(X4, 1, X3, "X4_kept", "X4")
                    keep(Q, 2, "Q_kept", "Q")
                    dve.wait_ge(sem("Q2"), 1)
                    dve.tensor_tensor(Z1[:, :, :], bank(5), ident4, ALU.add).then_inc(sem("Z1_kept"), 1)
                    dve.wait_ge(sem("Z1_kept"), 1)
                    plus(Z2, 6, Z1, "Z2_kept", "Z2")
                    keep(R, 7, "R_kept", "R")
                    keep(U, 0, "U_kept", "U")
                    dve.wait_ge(sem("U_kept"), 1)
                    for c in range(4):
                        for b in range(2):
                            t, lo = 2 * b + c // 2, (c % 2) * C
                            half = slice(lo, lo + C)
                            if c == 0:
                                dve.tensor_copy(vn[half, t, :], U[half, t, :]).then_inc(sem("v_new"), 1)
                            else:
                                dve.wait_ge(sem("read"), 2 * (c - 1) + b + 1)
                                dve.tensor_tensor(vn[half, t, :], U[half, t, :], psum[half, 2 + b, 0:P],
                                                  ALU.subtract).then_inc(sem("v_new"), 1)
                        for b in range(2):
                            if c == 3:
                                continue
                            end = flat(dec)[:, b * LEN + (c + 1) * C - 1:b * LEN + (c + 1) * C]
                            dve.wait_ge(sem("write"), 2 * c + b + 1)
                            if c == 0:
                                dve.tensor_copy(S[:, b, :], psum[:, 6 + b, 0:P]).then_inc(sem("state"), 1)
                            else:
                                dve.wait_ge(sem("state"), 2 * (c - 1) + b + 1)
                                dve.scalar_tensor_tensor(S[:, b, :], S[:, b, :], end, psum[:, 6 + b, 0:P],
                                                         ALU.mult, ALU.add).then_inc(sem("state"), 1)
                    dve.wait_ge(sem("outputs"), 2)
                    dve.tensor_copy(flat(oT).rearrange("p (b n) -> p b n", b=2),
                                    psum[:, 4:6, 0:LEN]).then_inc(sem("oT"), 1)
                    dve.tensor_tensor(flat(z), core.x[:, cols(g, BANK)], x_g, ALU.add).then_inc(sem("residual"), 1)
                    dve.wait_ge(sem("residual"), 1)
                    dve.wait_ge(sem("projected"), 1)
                    dve.tensor_tensor(core.x[:, cols(g, BANK)], psum[:, 0, :], flat(z), ALU.add).then_inc(sem("done"), 1)
            st.clear()


def mlp(core, w, prefetch):
    psum = core.psum
    with Stage(core) as st:
        sem = st.sem
        gel = st.sb("gel", [P, 2, BANK])
        hid = st.sb("hid", [P, 2, BANK])
        nic = HIDDEN // P
        norm_tensor, norm_vector, norm_gpsimd, norm_scalar, add_bias = norm_programs(
            core, st, core.y, core.h, 0, w["cols"][:, 7:8], w["cols"][:, 8:9], shift=True)
        steps = [(c, ic) for c in range(CH) for ic in range(nic)]
        with st.block() as block:
            block.gpsimd(norm_gpsimd)

            @block.sync
            def _(sp):
                prefetch(sp, sem("prefetched"))
                sp.wait_ge(sem("prefetched"), 48)

            @block.tensor
            def _(pe):
                norm_tensor(pe)
                pe.wait_ge(sem("std"), CH)

                def up(k):
                    c, ic = steps[k]
                    rhs = core.h[:, cols(c, BANK)]
                    if ic == 0:
                        pe.wait_ge(sem("scaled"), c + 1)
                    if k >= 2:
                        pe.wait_ge(sem("hidden"), k - 1)
                    pe.matmul(psum[:, k % 2, :], w["w1"][:, HIDDEN + ic * P:HIDDEN + ic * P + P], rhs,
                              start=True, stop=True).then_inc(sem("gate"), 1)
                    pe.matmul(psum[:, 2 + k % 2, :], w["w1"][:, cols(ic, P)], rhs, start=True,
                              stop=True).then_inc(sem("up"), 1)

                up(0)
                for k, (c, ic) in enumerate(steps):
                    if k + 1 < len(steps):
                        up(k + 1)
                    pe.wait_ge(sem("hidden"), k + 1)
                    pe.matmul(psum[:, 4 + c, :], w["w2"][:, ic, :], hid[:, k % 2, :],
                              start=(ic == 0), stop=(ic == nic - 1)).then_inc(sem("down"), 1)

            @block.scalar
            def _(act):
                norm_scalar(act)
                add_bias(act, 0)
                for k, (c, ic) in enumerate(steps):
                    act.wait_ge(sem("gate"), k + 1)
                    if k >= 2:
                        act.wait_ge(sem("hidden"), k - 1)
                    act.activation(gel[:, k % 2, :], psum[:, k % 2, :], ACT.Gelu,
                                   bias=w["cols"][:, nic + ic:nic + ic + 1]).then_inc(sem("gelu"), 1)
                    if ic == 0 and c + 1 < CH:
                        add_bias(act, c + 1)

            def residual(dve, c):
                dve.wait_ge(sem("down"), (c + 1) * nic)
                y = core.y[:, cols(c, BANK)]
                dve.scalar_tensor_tensor(y, psum[:, 4 + c, :], w["cols"][:, 2 * nic:2 * nic + 1], y,
                                         ALU.add, ALU.add).then_inc(sem("out"), 1)

            @block.vector
            def _(dve):
                norm_vector(dve)
                for k, (c, ic) in enumerate(steps):
                    dve.wait_ge(sem("gelu"), k + 1)
                    dve.wait_ge(sem("up"), k + 1)
                    if k >= 2:
                        dve.wait_ge(sem("down"), k - 1)
                    dve.scalar_tensor_tensor(hid[:, k % 2, :], psum[:, 2 + k % 2, :], w["cols"][:, ic:ic + 1],
                                             gel[:, k % 2, :], ALU.add, ALU.mult).then_inc(sem("hidden"), 1)
                    if ic == 0 and c > 0:
                        residual(dve, c - 1)
                residual(dve, CH - 1)
        st.clear()


def local_attention(core, st, heads, window, wqkv, wo, tab, mask):
    nc, psum = core.nc, core.psum
    DH = 64
    G = heads // 8
    NS = 4 * G
    W, KW = window, window + P
    half = P // 2
    sem = st.sem
    hT = st.sb("hT", [P, LEN])
    sq = st.sb("sq", [P, 2, BANK])
    rot = st.sb("rot", [P, 3, BANK])
    qk = st.sb("qk", [P, 3, BANK])
    ss = st.sb("ss", [P, NS, 8])
    rn = st.sb("rn", [P, NS, 8])
    power = st.sb("power", [P, 8])
    rq = st.sb("rq", [P, 2, 2, 2, heads])
    qT = st.sb("qT", [P, 2, 2, heads // 2, P])
    kT = st.sb("kT", [P, 2, heads // 2, LEN])
    v = st.sb("v", [P, 2, 2, G, BANK])
    sm = st.sb("sm", [P, 2, 4, KW])
    pr = st.sb("pr", [P, 2, 4, KW])
    mx = st.sb("mx", [P, 2, heads])
    nb = st.sb("nb", [P, 2, heads])
    total = st.sb("total", [P, 2, heads])
    prT = st.sb("prT", [P, 2, 4, P])
    cornerT = st.sb("cornerT", [P, 2, 4, W])
    o = st.sb("o", [P, G, BANK])
    oT = st.sb("oT", [P, heads // 2, P])
    TURN, SCORES, PROBS, CORNER, OUT = 2, 3, 5, 6, 7
    units = [(t, kind, g) for t in range(2) for kind in range(2) for g in range(G)]
    quads = [(t, q) for t in range(2) for q in range(2 * G)]
    items, place, j = [], [], 0
    for u in range(NS):
        place.append(len(items))
        items.append(("unit", u))
        if u % 2 == 0:
            items.append(("v", j))
            j += 1
    slots = range(NS + 6)

    def group_turned_in(n):
        return (n - 4) // 2 if n >= 4 and n % 2 == 0 and (n - 4) // 2 < 2 * G else None

    def tile_out_in(n):
        return next((t for t in range(2) if n == 2 * G * (t + 1) + 4 - t), None)

    def one_block(block, a, to, b, of):
        A, B = a is not None, b is not None
        ahead = 1 if A else 2
        group_bank = PROBS if A else TURN

        def score_bank(n):
            return SCORES if A or n % 2 == 0 else 0

        @block.tensor
        def _(pe):
            project_at = [0]

            def project_until(u):
                project_items(place[u] if u < NS else len(items) - 1)

            def project_items(last):
                while project_at[0] <= last:
                    i = project_at[0]
                    kind, k = items[i]
                    if i >= 2:
                        before, m = items[i - 2]
                        if before == "unit":
                            pe.wait_ge(sem("squared"), m + 1)
                            pe.wait_ge(sem("rotated"), 2 * (m + 1))
                        else:
                            pe.wait_ge(sem("v"), m + 1)
                    if kind == "unit":
                        t, which, g = units[k]
                    else:
                        (t, g), which = divmod(k, G), 2
                    pe.matmul(psum[:, i % 2, :], hT[:, cols(t, P)], wqkv[:, cols(which * G + g, BANK)],
                              start=True, stop=True).then_inc(sem("projected"), 1)
                    project_at[0] += 1

            def turn(u):
                pe.wait_ge(sem("unit"), u + 1)
                if u >= 1:
                    pe.wait_ge(sem("unit_kept"), u)
                for i in range(4):
                    mm = pe.transpose(psum[:, TURN, cols(i, P)], qk[:, u % 3, cols(i, P)], core.c["ident"][:, :])
                mm.then_inc(sem("unit_turned"), 1)

            def scores(n):
                t, q = quads[n]
                lo = 0 if t == 0 else P - W
                hi = P if t == 0 else LEN
                if n >= ahead:
                    pe.wait_ge(sem("masked"), n + 1 - ahead)
                for i in range(4):
                    head = 4 * q + i
                    rows = slice((head % 2) * DH, (head % 2) * DH + DH)
                    mm = pe.matmul(psum[:, score_bank(n) + i % 2, (i // 2) * KW:(i // 2) * KW + hi - lo],
                                   qT[rows, of, t, head // 2, :], kT[rows, of, head // 2, lo:hi],
                                   start=True, stop=True)
                mm.then_inc(sem("scores"), 1)

            def turn_probs(n):
                t, q = quads[n]
                pe.wait_ge(sem("exp"), 4 * (n + 1))
                if n >= 1:
                    pe.wait_ge(sem("probs_kept"), n)
                own = W if t == 1 else 0
                for i in range(4):
                    mm = pe.transpose(psum[:, PROBS, cols(i, P)], pr[:, n % 2, i, own:own + P], core.c["ident"][:, :])
                mm.then_inc(sem("probs_turned"), 1)
                if t == 1:
                    if q >= 1:
                        pe.wait_ge(sem("corner_kept"), q)
                    for i in range(4):
                        mm = pe.transpose(psum[0:W, CORNER, cols(i, W)], pr[0:W, n % 2, i, 0:W],
                                          core.c["ident"][0:W, 0:W])
                    mm.then_inc(sem("corner_turned"), 1)

            def weigh(n):
                t, q = quads[n]
                pe.wait_ge(sem("probs_kept"), n + 1)
                if t == 1:
                    pe.wait_ge(sem("corner_kept"), q + 1)
                if n % 2 == 0 and n >= 2:
                    pe.wait_ge(sem("o"), n // 2)
                for i in range(4):
                    g, at = divmod(4 * q + i, 8)
                    mm = pe.matmul(psum[:, OUT, cols(at, DH)], prT[:, n % 2, i, :], v[:, of, t, g, cols(at, DH)],
                                   start=True, stop=(t == 0), skip_group_check=True)
                    if t == 1:
                        mm = pe.matmul(psum[0:W, OUT, cols(at, DH)], cornerT[P - W:, n % 2, i, :],
                                       v[P - W:, of, 0, g, cols(at, DH)], start=False, stop=True,
                                       skip_group_check=True)
                mm.then_inc(sem("weighed"), 1)

            def turn_group(j):
                pe.wait_ge(sem("o"), j + 1)
                if A:
                    pe.wait_ge(sem("probs_kept"), min(2 * j + 5, NS))
                if j >= 1:
                    pe.wait_ge(sem("oT"), j)
                for i in range(4):
                    mm = pe.transpose(psum[:, group_bank, cols(i, P)], o[:, j % G, cols(i, P)], core.c["ident"][:, :])
                mm.then_inc(sem("o_turned"), 1)

            def project_out(t, n):
                pe.wait_ge(sem("oT"), (t + 1) * G)
                pe.wait_ge(sem("corner_kept"), min(n + 1, NS) - 2 * G)
                if t == 1:
                    pe.wait_ge(sem("added"), 1)
                for i in range(heads // 2):
                    mm = pe.matmul(psum[:, CORNER, 3 * P:], wo[:, i, :], oT[:, i, :], start=(i == 0),
                                   stop=(i == heads // 2 - 1))
                mm.then_inc(sem("out"), 1)

            if B:
                scores(0)
                if not A:
                    scores(1)
            if A:
                pe.wait_ge(sem("shifted"), 3)
                project_until(0)
            for n in slots:
                j, t = group_turned_in(n), tile_out_in(n)
                if B and n + ahead < NS:
                    scores(n + ahead)
                if A and n == 0:
                    project_items(1)
                if A and B and n == 1:
                    project_until(1)
                if A and 2 <= n <= NS + 1:
                    turn(n - 2)
                if B and n < NS:
                    if A and group_turned_in(n - 1) is not None:
                        pe.wait_ge(sem("oT"), group_turned_in(n - 1) + 1)
                    before = tile_out_in(n - 1)
                    if before is not None:
                        pe.wait_ge(sem("added"), before + 1)
                    turn_probs(n)
                if B and 1 <= n <= NS:
                    weigh(n - 1)
                if A and n < NS and not (B and n == 0):
                    project_until(n + 1)
                if B and j is not None:
                    turn_group(j)
                if B and t is not None:
                    project_out(t, n)

        @block.scalar
        def _(act):
            def exps(n):
                t, q = quads[n]
                width = P if t == 0 else KW
                act.wait_ge(sem("shift"), n + 1)
                if n >= 2:
                    act.wait_ge(sem("probs_turned"), n - 1)
                    if quads[n - 2][0] == 1:
                        act.wait_ge(sem("corner_turned"), quads[n - 2][1] + 1)
                for i in range(4):
                    head = 4 * q + i
                    act.activation(pr[:, n % 2, i, 0:width], sm[:, n % 2, i, 0:width], ACT.Exp,
                                   scale=rq[:, of, t, 0, head:head + 1], bias=nb[:, t, head:head + 1],
                                   accum_out=total[:, t, head:head + 1]).then_inc(sem("exp"), 1)

            def keep_v(k):
                t, g = divmod(k, G)
                i = items.index(("v", k))
                act.wait_ge(sem("projected"), i + 1)
                act.activation(v[:, to, t, g, :], psum[:, i % 2, :], ACT.Copy).then_inc(sem("v"), 1)

            def square(u):
                act.wait_ge(sem("projected"), place[u] + 1)
                if u >= 2:
                    act.wait_ge(sem("summed"), u - 1)
                act.activation(sq[:, u % 2, :], psum[:, place[u] % 2, :], ACT.Square).then_inc(sem("squared"), 1)

            def keep_unit(u):
                t, kind, g = units[u]
                act.wait_ge(sem("unit_turned"), u + 1)
                src = psum[:, TURN, :].rearrange("p (i n) -> p i n", i=4)
                dst = (qT[:, to, t, 4 * g:4 * g + 4, :] if kind == 0
                       else kT[:, to, 4 * g:4 * g + 4, cols(t, P)])
                act.activation(dst, src, ACT.Copy).then_inc(sem("unit_kept"), 1)

            def keep_group(j):
                t, g = divmod(j, G)
                act.wait_ge(sem("o_turned"), j + 1)
                if t == 1:
                    act.wait_ge(sem("out"), 1)
                act.activation(oT[:, 4 * g:4 * g + 4, :], psum[:, group_bank, :].rearrange("p (i n) -> p i n", i=4),
                               ACT.Copy).then_inc(sem("oT"), 1)

            def keep_probs(n):
                t, q = quads[n]
                act.wait_ge(sem("probs_turned"), n + 1)
                if n >= 2:
                    act.wait_ge(sem("weighed"), n - 1)
                act.activation(prT[:, n % 2, :, :], psum[:, PROBS, :].rearrange("p (i n) -> p i n", i=4),
                               ACT.Copy).then_inc(sem("probs_kept"), 1)
                if t == 1:
                    act.wait_ge(sem("corner_turned"), q + 1)
                    act.activation(cornerT[P - W:, n % 2, :, :], psum[0:W, CORNER, 0:4 * W].rearrange("p (i n) -> p i n", i=4),
                                   ACT.Copy).then_inc(sem("corner_kept"), 1)

            if A:
                act.activation(hT[0:half, :], core.y[0:half, cols(a, LEN)], ACT.Copy).then_inc(sem("shifted"), 1)
                square(0)
            if B:
                exps(0)
            v_kept = 0
            for n in slots:
                while A and v_kept < 2 * G and (n >= NS or items.index(("v", v_kept)) < place[n]):
                    keep_v(v_kept)
                    v_kept += 1
                if A and 1 <= n < NS:
                    square(n)
                if B and group_turned_in(n - 1) is not None:
                    keep_group(group_turned_in(n - 1))
                if A and 2 <= n <= NS + 1:
                    keep_unit(n - 2)
                if B and n + 1 < NS:
                    exps(n + 1)
                if B and n < NS:
                    keep_probs(n)

        @block.gpsimd
        def _(pool):
            if not A:
                return
            pool.memset(power[:, :], -0.5).then_inc(sem("power"), 1)
            pool.wait_ge(sem("power"), 1)
            for u, (t, kind, g) in enumerate(units):
                pool.wait_ge(sem("summed"), u + 1)
                pool.tensor_scalar(ss[:, u, :], ss[:, u, :], 1e-24, None, ALU.max).then_inc(sem("guarded"), 1)
                pool.wait_ge(sem("guarded"), u + 1)
                pool.tensor_tensor(rn[:, u, :], ss[:, u, :], power[:, :], ALU.pow).then_inc(sem("inverse"), 1)
                pool.wait_ge(sem("inverse"), u + 1)
                x, r = qk[:, u % 3, :], rot[:, u % 3, :]
                pool.wait_ge(sem("rotated"), 2 * (u + 1))
                if kind == 0:
                    pool.tensor_scalar(rq[:, to, t, 0, cols(g, 8)], rn[:, u, :], 8.0, None, ALU.mult).then_inc(sem("query_scale"), 1)
                    if B:
                        pool.tensor_scalar(rq[:, to, t, 1, cols(g, 8)], rn[:, u, :], -8.0, None, ALU.mult).then_inc(sem("query_scale"), 1)
                        pool.tensor_tensor(x, x, r, ALU.add).then_inc(sem("unit"), 1)
                    else:
                        pool.wait_ge(sem("sum"), u + 1)
                        pool.tensor_scalar(rq[:, to, t, 1, cols(g, 8)], rn[:, u, :], -8.0, None, ALU.mult).then_inc(sem("unit"), 1)
                else:
                    if B:
                        pool.tensor_tensor(r, x, r, ALU.add).then_inc(sem("key_sum"), 1)
                        pool.wait_ge(sem("key_sum"), t * G + g + 1)
                    else:
                        pool.wait_ge(sem("sum"), u + 1)
                    pool.tensor_tensor(x.rearrange("p (h d) -> p h d", h=8), r.rearrange("p (h d) -> p h d", h=8),
                                       over(rn[:, u, :], [1, 8], [0, DH]), ALU.mult).then_inc(sem("unit"), 1)

        @block.vector
        def _(dve):
            def norms(u):
                dve.wait_ge(sem("squared"), u + 1)
                dve.tensor_reduce(ss[:, u, :], sq[:, u % 2, :].rearrange("p (h d) -> p h d", h=8),
                                  AX.X, ALU.add).then_inc(sem("summed"), 1)

            def rotate(u):
                t, kind, g = units[u]
                x = psum[:, place[u] % 2, :].rearrange("p (h d) -> p h d", h=8)
                if u >= 3:
                    dve.wait_ge(sem("unit_turned"), u - 2)
                cos = over(tab[:, t, 2 * kind, :], [0, 8], [1, DH])
                dve.tensor_tensor(qk[:, u % 3, :].rearrange("p (h d) -> p h d", h=8), x, cos,
                                  ALU.mult).then_inc(sem("rotated"), 1)
                hd = DH // 2
                y = rot[:, u % 3, :].rearrange("p (h d) -> p h d", h=8)
                dve.tensor_tensor(y[:, :, 0:hd], x[:, :, hd:DH],
                                  over(tab[:, t, 2 * kind + 1, 0:hd], [0, 8], [1, hd]), ALU.mult)
                dve.tensor_tensor(y[:, :, hd:DH], x[:, :, 0:hd],
                                  over(tab[:, t, 2 * kind + 1, hd:DH], [0, 8], [1, hd]),
                                  ALU.mult).then_inc(sem("rotated"), 1)
                if not B:
                    dve.wait_ge(sem("rotated"), 2 * (u + 1))
                    x, r = qk[:, u % 3, :], rot[:, u % 3, :]
                    dve.tensor_tensor(x if kind == 0 else r, x, r, ALU.add).then_inc(sem("sum"), 1)

            def soft(n):
                t, q = quads[n]
                width = P if t == 0 else KW
                dve.wait_ge(sem("scores"), n + 1)
                if n >= 2:
                    dve.wait_ge(sem("exp"), 4 * (n - 1))
                bank2 = psum[:, score_bank(n):score_bank(n) + 2, 0:2 * KW].rearrange("p e (j k) -> p j e k", j=2)
                band = over(mask[:, P - width + W:], [0, 2], [0, 2], [1, width])
                out = sm[:, n % 2, :, :].rearrange("p (j e) k -> p j e k", e=2)
                dve.tensor_tensor(out[:, :, :, 0:width], bank2[:, :, :, 0:width], band,
                                  ALU.add).then_inc(sem("masked"), 1)
                dve.wait_ge(sem("masked"), n + 1)
                dve.tensor_reduce(mx[:, t, cols(q, 4)], sm[:, n % 2, :, 0:width], AX.X, ALU.max).then_inc(sem("max"), 1)
                dve.wait_ge(sem("max"), n + 1)
                dve.tensor_tensor(nb[:, t, cols(q, 4)], mx[:, t, cols(q, 4)], rq[:, of, t, 1, cols(q, 4)],
                                  ALU.mult).then_inc(sem("shift"), 1)

            def normal_group(j):
                t, g = divmod(j, G)
                dve.wait_ge(sem("weighed"), 2 * j + 2)
                if t == 1:
                    dve.wait_ge(sem("o_turned"), g + 1)
                sums = total[:, t, cols(g, 8)]
                dve.reciprocal(sums, sums).then_inc(sem("inverse_total"), 1)
                dve.wait_ge(sem("inverse_total"), j + 1)
                dve.tensor_tensor(o[:, g, :].rearrange("p (h d) -> p h d", h=8),
                                  psum[:, OUT, :].rearrange("p (h d) -> p h d", h=8),
                                  over(sums, [1, 8], [0, DH]), ALU.mult).then_inc(sem("o"), 1)

            def add(t):
                y = core.y[:, bass.ds(b * LEN + t * P, P)]
                dve.wait_ge(sem("out"), t + 1)
                dve.tensor_tensor(y, y, psum[:, CORNER, 3 * P:], ALU.add).then_inc(sem("added"), 1)

            if A:
                dve.memset(hT[half:, 0:1], 0.0).then_inc(sem("shifted"), 1)
                dve.tensor_copy(hT[half:, 1:LEN], core.y[half:, bass.ds(a * LEN, LEN - 1)]).then_inc(sem("shifted"), 1)
            if B:
                soft(0)
                soft(1)
            if A:
                norms(0)
                rotate(0)
            for n in slots:
                if B and n >= 3 and n % 2 == 1 and (n - 3) // 2 < 2 * G:
                    normal_group((n - 3) // 2)
                if B and tile_out_in(n - 1) is not None:
                    add(tile_out_in(n - 1))
                if B and 1 <= n < NS - 1:
                    soft(n + 1)
                if A and 1 <= n < NS:
                    norms(n)
                    rotate(n)

    with st.block() as block:
        one_block(block, 0, 0, None, None)
    st.clear()
    with nc.Fori(0, BATCH // 2 - 1) as pair:
        with st.block() as block:
            one_block(block, pair * 2 + 1, 1, pair * 2, 0)
        st.clear()
        with st.block() as block:
            one_block(block, pair * 2 + 2, 0, pair * 2 + 1, 1)
        st.clear()
    with st.block() as block:
        one_block(block, BATCH - 1, 1, BATCH - 2, 0)
    st.clear()
    with st.block() as block:
        one_block(block, None, None, BATCH - 1, 1)
    st.clear()


def wide_attention(core, causal):
    nc, psum = core.nc, core.psum
    H, DH = 16, 8
    scale = 1.0 / float(np.sqrt(DH))
    src = core.xn if causal else core.h
    with Stage(core) as st:
        sem = st.sem
        xs = st.sb("xs", [P, LEN])
        lat = st.sb("lat", [P // 2, LEN])
        qT = st.sb("qT", [P, LEN])
        kT = st.sb("kT", [P, LEN])
        k_bd = st.sb("k_bd", [P, H, LEN])
        v = st.sb("v", [P, 2, P])
        rel = st.sb("rel", [P, 1 if causal else 8, 4, LEN])
        sm = st.sb("sm", [P, 2, BANK])
        pr = st.sb("pr", [P, 2, BANK])
        prT = st.sb("prT", [P, 2, BANK])
        mx = st.sb("mx", [P, 2, H])
        nb = st.sb("nb", [P, 2, H])
        total = st.sb("total", [P, 2, H])
        o = st.sb("o", [P, 2, P])
        oT = st.sb("oT", [P, LEN])
        if not causal:
            W3 = 384
            rT = st.sb("rT", [P, BANK])
            r_bd = st.sb("r_bd", [P, H, BANK])
            qv = st.sb("qv", [P, LEN])
            raw = st.sb("raw", [P, 4, 4, W3])
            REL = 4
        units = []
        for t in range(2):
            keys = P if causal and t == 0 else LEN
            nh = BANK // keys
            units += [(t, h, nh, keys) for h in range(0, H, nh)]
        n_of = [sum(1 for u in units if u[0] <= t) for t in range(2)]

        def one_block(block, b, ahead):
            attend = b is not None

            @block.sync
            def _(sp):
                if not causal and attend:
                    for i in range(8):
                        t, k = divmod(i, 4)
                        row = core.rel_d[bass.ds(b * 2 + t, 1), P - 1:P - 1 + P * (core.rel_pitch - 1)]
                        skew = row.rearrange("a (p n) -> (a p) n", p=P)[:, 4 * k * 384:4 * (k + 1) * 384]
                        sp.dma_start(rel[:, i, :, :], skew.rearrange("p (h n) -> p h n", h=4)[:, :, 0:LEN]
                                     ).then_inc(sem(f"rel{i}"), 16)
                if ahead is not None:
                    for i in range(8):
                        sp.wait_ge(sem("kept_even"), 2 * i + 2)
                        sp.wait_ge(sem("kept_odd"), 2 * i + 2)
                        t, k = divmod(i, 4)
                        dst = core.rel_d[bass.ds(ahead * 2 + t, 1), :].rearrange("a (p n) -> (a p) n", p=P)
                        sp.dma_start(dst[:, 4 * k * W3:4 * (k + 1) * W3],
                                     raw[:, i % 4, :, :].rearrange("p h n -> p (h n)")).then_inc(sem(f"stored{i}"), 16)
                    for i in range(8):
                        sp.wait_ge(sem(f"stored{i}"), 16)
                if not causal and attend:
                    for i in range(8):
                        sp.wait_ge(sem(f"rel{i}"), 16)

            @block.tensor
            def _(pe):
                def relative_query():
                    pe.matmul(psum[:, REL, 0:LEN], core.c["l3_w"][:, 0, :], core.h[:, cols(ahead, LEN)], start=True,
                              stop=True).then_inc(sem("next_q"), 1)

                def relative(n):
                    t, h = divmod(n, H)
                    if n == 0:
                        pe.wait_ge(sem("qv"), 1)
                    if n >= 2:
                        pe.wait_ge(sem("kept_even" if n % 2 == 0 else "kept_odd"), n // 2)
                    pe.matmul(psum[:, REL + n % 2, 0:W3], qv[:, cols(t, P)], r_bd[:, h, P - P * t:P - P * t + W3],
                              start=True, stop=True).then_inc(sem("product"), 1)

                if not attend:
                    relative_query()
                    for n in range(2 * H):
                        relative(n)
                    return
                if causal:
                    w = core.c["l2_w"]
                    pe.matmul(psum[0:P // 2, 0, 0:LEN], core.c["l2_down"][:, :], src[:, cols(b, LEN)], start=True,
                              stop=True).then_inc(sem("latent"), 1)
                    pe.wait_ge(sem("lat"), 1)
                    pe.matmul(psum[:, 1, 0:LEN], w[:, 0:P], lat[:, :], start=True, stop=True).then_inc(sem("q"), 1)
                    pe.matmul(psum[:, 2, 0:LEN], w[:, P:2 * P], lat[:, :], start=True, stop=True).then_inc(sem("k"), 1)
                    for t in range(2):
                        mm = pe.matmul(psum[:, 3, t * P:t * P + DH], lat[:, cols(t, P)], w[:, 2 * P:2 * P + DH],
                                       start=True, stop=True)
                    mm.then_inc(sem("v"), 1)
                else:
                    w = core.c["l3_w"]
                    pe.matmul(psum[:, 1, 0:LEN], w[:, 0, :], src[:, cols(b, LEN)], start=True, stop=True).then_inc(sem("q"), 1)
                    pe.matmul(psum[:, 2, 0:LEN], w[:, 1, :], src[:, cols(b, LEN)], start=True, stop=True).then_inc(sem("k"), 1)
                    if ahead is not None:
                        relative_query()
                    pe.wait_ge(sem("x"), 1)
                    for t in range(2):
                        mm = pe.matmul(psum[:, 3, cols(t, P)], xs[:, cols(t, P)], w[:, 2, :], start=True, stop=True)
                    mm.then_inc(sem("v"), 1)

                def scores(n):
                    t, h, nh, keys = units[n]
                    if n == 0:
                        pe.wait_ge(sem("qT"), 1)
                    if t == 0:
                        pe.wait_ge(sem("k_bd"), min((h + nh + 3) // 4, 2))
                        if h + nh > H // 2:
                            pe.wait_ge(sem("k_bd_late"), (h + nh + 3) // 4 - 2)
                    if n >= 2:
                        pe.wait_ge(sem("biased"), n - 1)
                    pe.matmul(psum[:, n % 2, :], qT[:, cols(t, P)], k_bd[:, h:h + nh, 0:keys], start=True,
                              stop=True).then_inc(sem("scores"), 1)

                def turn(n):
                    if n == 0:
                        pe.wait_ge(sem("kT"), 1)
                    if n == 1:
                        pe.wait_ge(sem("v_kept"), 1)
                    pe.wait_ge(sem("exp"), sum(u[2] for u in units[:n + 1]))
                    if n >= 2:
                        pe.wait_ge(sem("probs_kept"), n - 1)
                    for i in range(4):
                        mm = pe.transpose(psum[:, 2 + n % 2, cols(i, P)], pr[:, n % 2, cols(i, P)], core.c["ident"][:, :])
                    mm.then_inc(sem("probs_turned"), 1)

                def weigh(n):
                    t, h, nh, keys = units[n]
                    pe.wait_ge(sem("probs_kept"), n + 1)
                    blocks = keys // P
                    for i in range(nh):
                        head = h + i
                        for s in range(blocks):
                            val = v[:, s, 0:DH] if causal else v[:, s, cols(head, DH)]
                            mm = pe.matmul(psum[:, 6 + t, cols(head, DH)], prT[:, n % 2, cols(i * blocks + s, P)],
                                           val, start=(s == 0), stop=(s == blocks - 1))
                    mm.then_inc(sem("weighed"), 1)

                scores(0)
                scores(1)
                for n in range(len(units)):
                    if n + 2 < len(units):
                        scores(n + 2)
                    if ahead is not None:
                        relative(2 * n)
                    turn(n)
                    if ahead is not None:
                        relative(2 * n + 1)
                    if n >= 1:
                        weigh(n - 1)
                    if n == n_of[0] + 3:
                        pe.wait_ge(sem("o"), 1)
                        pe.transpose(psum[:, 6, P:2 * P], o[:, 0, :], core.c["ident"][:, :]).then_inc(sem("o_turned"), 1)
                weigh(len(units) - 1)
                pe.wait_ge(sem("o"), 2)
                pe.wait_ge(sem("oT"), 1)
                pe.transpose(psum[:, 6, P:2 * P], o[:, 1, :], core.c["ident"][:, :]).then_inc(sem("o_turned"), 1)
                pe.wait_ge(sem("oT"), 2)
                proj = core.c["l2_proj"][:, :] if causal else core.c["l3_w"][:, 4, :]
                pe.matmul(psum[:, 7, LEN:], proj, oT[:, :], start=True, stop=True).then_inc(sem("out"), 1)

            @block.scalar
            def _(act):
                def keep_relative(n):
                    act.wait_ge(sem("product"), n + 1)
                    if n >= 16:
                        act.wait_ge(sem(f"stored{(n - 16) // 4}"), 16)
                    act.activation(raw[:, (n // 4) % 4, n % 4, :], psum[:, REL + 1, 0:W3],
                                   ACT.Copy).then_inc(sem("kept_odd"), 1)

                if not attend:
                    for n in range(1, 2 * H, 2):
                        keep_relative(n)
                    return
                if causal:
                    act.wait_ge(sem("latent"), 1)
                    act.activation(lat[:, :], psum[0:P // 2, 0, 0:LEN], ACT.Copy).then_inc(sem("lat"), 1)
                act.wait_ge(sem("q"), 1)
                bias = core.c["small"][:, 3:4] if causal else core.c["l3_cols"][:, 0:1]
                act.activation(qT[:, :], psum[:, 1, 0:LEN], ACT.Identity, bias=bias).then_inc(sem("qT"), 1)
                act.wait_ge(sem("k"), 1)
                act.activation(kT[:, :], psum[:, 2, 0:LEN], ACT.Copy).then_inc(sem("kT"), 1)
                act.wait_ge(sem("v"), 1)
                act.activation(v[:, :, 0:DH] if causal else v[:, :, :],
                               psum[:, 3, 0:LEN].rearrange("p (t n) -> p t n", t=2)[:, :, 0:DH if causal else P],
                               ACT.Copy).then_inc(sem("v_kept"), 1)

                def exps(n):
                    t, h, nh, keys = units[n]
                    act.wait_ge(sem("shift"), n + 1)
                    if n >= 2:
                        act.wait_ge(sem("probs_turned"), n - 1)
                    for i in range(nh):
                        act.activation(pr[:, n % 2, cols(i, keys)], sm[:, n % 2, cols(i, keys)], ACT.Exp,
                                       scale=scale, bias=nb[:, t, h + i:h + i + 1],
                                       accum_out=total[:, t, h + i:h + i + 1]).then_inc(sem("exp"), 1)

                exps(0)
                for n, (t, h, nh, keys) in enumerate(units):
                    if n + 1 < len(units):
                        exps(n + 1)
                    if ahead is not None and n >= 1:
                        keep_relative(2 * n - 1)
                    act.wait_ge(sem("probs_turned"), n + 1)
                    if n >= 2:
                        act.wait_ge(sem("weighed"), n - 1)
                    act.activation(prT[:, n % 2, :], psum[:, 2 + n % 2, :], ACT.Copy).then_inc(sem("probs_kept"), 1)
                if ahead is not None:
                    keep_relative(2 * H - 1)
                for t in range(2):
                    act.wait_ge(sem("o_turned"), t + 1)
                    act.activation(oT[:, cols(t, P)], psum[:, 6, P:2 * P], ACT.Copy).then_inc(sem("oT"), 1)

            def own_rows(engine, i, name):
                engine.tensor_tensor(k_bd[:, 4 * i:4 * i + 4, :], over(kT[:, :], [0, 4], [1, LEN]),
                                     over(core.c["head_mask"][:, 4 * i:4 * i + 4], [1, 4], [0, LEN]),
                                     ALU.mult).then_inc(sem(name), 1)

            @block.gpsimd
            def _(pool):
                if attend:
                    pool.wait_ge(sem("kT"), 1)
                    for i in range(2, 4):
                        own_rows(pool, i, "k_bd_late")

            @block.vector
            def _(dve):
                def add_v_bias():
                    dve.wait_ge(sem("next_q"), 1)
                    dve.tensor_scalar(qv[:, :], psum[:, REL, 0:LEN], core.c["l3_cols"][:, 1:2], None,
                                      ALU.add).then_inc(sem("qv"), 1)

                def keep_relative(n):
                    dve.wait_ge(sem("product"), n + 1)
                    if n >= 16:
                        dve.wait_ge(sem(f"stored{(n - 16) // 4}"), 16)
                    dve.tensor_copy(raw[:, (n // 4) % 4, n % 4, :], psum[:, REL, 0:W3]).then_inc(sem("kept_even"), 1)

                if not attend:
                    add_v_bias()
                    for n in range(0, 2 * H, 2):
                        keep_relative(n)
                    return
                if not causal:
                    dve.tensor_copy(xs[:, :], src[:, cols(b, LEN)]).then_inc(sem("x"), 1)
                dve.wait_ge(sem("kT"), 1)
                for i in range(2):
                    own_rows(dve, i, "k_bd")
                if ahead is not None:
                    add_v_bias()

                def normal(t):
                    dve.wait_ge(sem("weighed"), n_of[t])
                    dve.reciprocal(total[:, t, :], total[:, t, :]).then_inc(sem("inverse"), 1)
                    dve.wait_ge(sem("inverse"), t + 1)
                    dve.tensor_tensor(o[:, t, :].rearrange("p (h d) -> p h d", h=H),
                                      psum[:, 6 + t, 0:P].rearrange("p (h d) -> p h d", h=H),
                                      over(total[:, t, :], [1, H], [0, DH]), ALU.mult).then_inc(sem("o"), 1)

                heads_before = 0
                for n, (t, h, nh, keys) in enumerate(units):
                    dve.wait_ge(sem("scores"), n + 1)
                    if n >= 2:
                        dve.wait_ge(sem("exp"), heads_before - units[n - 1][2])
                    heads_before += nh
                    out = sm[:, n % 2, :].rearrange("p (h k) -> p h k", h=nh)
                    bank = psum[:, n % 2, :].rearrange("p (h k) -> p h k", h=nh)
                    if causal:
                        bias = over(core.c["causal"][:, LEN - keys:], [0, nh], [1, keys])
                    else:
                        i = 4 * t + h // 4
                        if h % 4 == 0:
                            dve.wait_ge(sem(f"rel{i}"), 16)
                        bias = rel[:, i, h % 4:h % 4 + nh, :]
                    dve.tensor_tensor(out, bank, bias, ALU.add).then_inc(sem("biased"), 1)
                    dve.wait_ge(sem("biased"), n + 1)
                    dve.tensor_reduce(mx[:, t, h:h + nh], out, AX.X, ALU.max).then_inc(sem("max"), 1)
                    dve.wait_ge(sem("max"), n + 1)
                    dve.tensor_scalar(nb[:, t, h:h + nh], mx[:, t, h:h + nh], -scale, None,
                                      ALU.mult).then_inc(sem("shift"), 1)
                    if n == n_of[0] + 2:
                        normal(0)
                    if ahead is not None and n >= 2:
                        keep_relative(2 * (n - 2))
                if ahead is not None:
                    keep_relative(2 * H - 4)
                    keep_relative(2 * H - 2)
                normal(1)
                dve.wait_ge(sem("out"), 1)
                x = core.x[:, cols(b, LEN)]
                bo = core.c["small"][:, 3:4] if causal else core.c["l3_cols"][:, 2:3]
                dve.scalar_tensor_tensor(x, psum[:, 7, LEN:], bo, x, ALU.add, ALU.add).then_inc(sem("done"), 1)

        if causal:
            with nc.Fori(0, BATCH) as b:
                with st.block() as block:
                    one_block(block, b, None)
                st.clear()
            return
        with st.block() as block:
            @block.tensor
            def _(pe):
                pe.matmul(psum[:, 0, :], core.c["l3_w"][:, 3, :], core.c["l3_remb"][:, :], start=True,
                          stop=True).then_inc(sem("r"), 1)

            @block.vector
            def _(dve):
                dve.wait_ge(sem("r"), 1)
                dve.tensor_copy(rT[:, :], psum[:, 0, :]).then_inc(sem("rT"), 1)
                dve.wait_ge(sem("rT"), 1)
                for h in range(H):
                    dve.tensor_scalar(r_bd[:, h, :], rT[:, :], core.c["head_mask"][:, h:h + 1], None,
                                      ALU.mult).then_inc(sem("r_bd"), 1)
        st.clear()
        with st.block() as block:
            one_block(block, None, 0)
        st.clear()
        with nc.Fori(0, BATCH - 1) as b:
            with st.block() as block:
                one_block(block, b, b + 1)
            st.clear()
        with st.block() as block:
            one_block(block, BATCH - 1, None)
        st.clear()


def constants():
    c = {}
    f = np.float32
    c["ident"] = np.eye(P, dtype=f)
    c["mean"] = np.full((P, P), 1.0 / P, f)
    c["small"] = np.tile(np.array([1e-5, 1e-6, 1.0, 0.0], f), (P, 1))
    c["below"] = np.tile(np.tril(np.ones((8, 8), f), -1).reshape(1, 64), (P, 1))
    i = np.arange(P)
    c["ones"] = np.ones((P, P), f)
    inside = (i[:, None] < i[None, :]) & (i[:, None] // 64 == i[None, :] // 64)
    c["chunk_mask"] = np.where(inside, 0.0, NEG).astype(f)
    c["block16"] = (i[:, None] // 16 == i[None, :] // 16).astype(f)
    c["reset"] = np.tile((np.arange(BANK) % 64 != 0).astype(f), (P, 1))
    for name, window in (("l1", 64), ("l2", 32)):
        behind = i[:, None] + window - np.arange(window + P)[None, :]
        band = np.where((behind >= 0) & (behind <= window), 0.0, NEG).astype(f)
        c[name + "_band"] = band
        pos = np.arange(LEN, dtype=f)
        half = np.arange(0, 64, 2, dtype=f)
        freqs = pos[:, None] * (f(1.0) / f(10000.0) ** (half / f(64)))[None, :]
        base = (half + f(0.4 * 64)) / f(1.4 * 64)
        scale = base[None, :] ** ((pos - LEN // 2) / f(window // 2))[:, None]
        two = lambda a: np.concatenate([a, a], -1)
        freqs, scale = two(freqs), two(scale)
        sign = np.where(np.arange(64) < 32, -1.0, 1.0).astype(f)
        tab = np.stack([np.cos(freqs) * scale, np.sin(freqs) * scale * sign,
                        np.cos(freqs) / scale, np.sin(freqs) / scale * sign], 1)
        c[name + "_rotary"] = tab.reshape(2, P, 4, 64).transpose(1, 0, 2, 3).astype(f)
    c["head_mask"] = (i[:, None] // 8 == np.arange(16)[None, :]).astype(f)
    c["causal"] = np.where(np.arange(LEN)[None, :] <= P + i[:, None], 0.0, NEG).astype(f)
    return c


def laid_out(inp):
    c = constants()
    f = np.float32
    col = lambda *v: np.ascontiguousarray(np.stack([np.asarray(x, f) for x in v], 1))
    pad = lambda a, n, ax: np.pad(a, [(0, n - a.shape[ax]) if i == ax % a.ndim else (0, 0) for i in range(a.ndim)])
    c["x"] = inp["L0_attn_x"].reshape(TOK, DIM)
    c["l0_w"] = np.stack([inp[f"L0_attn_{n}_w"].T for n in ("A", "B", "C", "D", "out")], 1)
    c["l0_cols"] = col(inp["L0_attn_A_b"], inp["L0_attn_out_b"], inp["L0_attn_norm_w"])
    c["l0_gate"] = inp["L0_ffn_gate_w"]
    c["l0_wg"] = pad(inp["L0_ffn_Wg"], HIDDEN, -1)
    c["l0_wu"] = pad(inp["L0_ffn_Wu"], HIDDEN, -1)
    c["l0_wd"] = pad(inp["L0_ffn_Wd"], HIDDEN, 1)
    c["l0s_wg"] = pad(inp["L0_ffn_Sg"], 256, -1)
    c["l0s_wu"] = pad(inp["L0_ffn_Su"], 256, -1)
    c["l0s_wd"] = pad(inp["L0_ffn_Sd"], 256, 0)
    c["l1_rows"] = np.stack([np.repeat(inp[n].reshape(DIM, 1), P, 1)
                             for n in ("L1_attn_W_beta", "L1_attn_W_alpha")], 1)
    c["l1_w"] = np.stack([inp["L1_attn_W_write"].T, inp["L1_attn_W_read"].T], 1)
    c["l1_scal"] = np.repeat(np.stack([inp["L1_attn_A_log"], inp["L1_attn_dt_bias"]], 1), P, 0)
    for name, heads in (("l1", 8), ("l2", 16)):
        g = lambda n: inp[next(k for k in inp if k.lower() == f"{name}_ffn_{n}".lower())]
        depth, inner = g("wqkv").shape[0], heads * 64
        more = lambda a: np.concatenate([a, a[:1]])
        c[name + "_wqkv"] = more(g("wqkv"))
        c[name + "_wo"] = more(g("wo").reshape(depth, heads // 2, P, DIM).transpose(0, 2, 1, 3))
        w1 = g("w1").reshape(depth, DIM, 2, -1)
        b1 = g("b1").reshape(depth, 2, -1)
        c[name + "_w1"] = pad(w1, HIDDEN, -1).reshape(depth, DIM, 2 * HIDDEN)
        c[name + "_w2"] = pad(g("w2"), HIDDEN, 1).reshape(depth, 3, P, DIM).transpose(0, 2, 1, 3)
        b1 = pad(b1, HIDDEN, -1).reshape(depth, 6, P)
        c[name + "_cols"] = np.concatenate([b1, g("b2")[:, None], g("ln_g")[:, None], g("ln_b")[:, None]],
                                           1).transpose(0, 2, 1)
        qs, ks = g("q_scale"), g("k_scale")
        c[name + "_scales"] = more(np.stack([qs, np.roll(qs, 32, -1), ks, np.roll(ks, 32, -1)], 1))
    c["l2_down"] = inp["L2_attn_Wc_down"]
    kv = inp["L2_attn_Wkv_up"]
    c["l2_w"] = np.concatenate([inp["L2_attn_Wq_up"], np.tile(kv[:, :8], (1, 16)), kv[:, 8:]], 1)
    c["l2_proj"] = inp["L2_attn_Wc_proj"]
    c["l3_w"] = np.stack([inp[f"L3_attn_W{n}"] for n in ("q", "k", "v", "r", "o")], 1)
    c["l3_cols"] = col(inp["L3_attn_u_bias"].reshape(-1), inp["L3_attn_v_bias"].reshape(-1), inp["L3_attn_bo"],
                       inp["L3_attn_gamma"], inp["L3_attn_beta"])
    first = (inp["L3_attn_rel_pos_emb"].shape[0] - 1) // 2 - (LEN - 1)
    c["l3_remb"] = pad(inp["L3_attn_rel_pos_emb"][first:first + 2 * LEN - 1].T, 2 * LEN, -1)
    c["l3_gate"] = inp["L3_ffn_gate_w"]
    gate_up = inp["L3_ffn_gate_up_w"]
    c["l3_wg"], c["l3_wu"] = np.split(gate_up, 2, -1)
    c["l3_wd"] = inp["L3_ffn_down_w"]
    return {k: np.ascontiguousarray(v, f) for k, v in c.items()}


CONST_ALL = ("ident", "mean", "small", "below", "l0_w", "l0_cols", "l0_gate", "ones", "chunk_mask", "block16", "reset",
             "l1_rows", "l1_w", "l1_scal", "l1_band", "l1_rotary", "l2_band",
             "l2_rotary", "head_mask", "causal", "l2_down", "l2_w", "l2_proj", "l3_w", "l3_cols",
             "l3_remb", "l3_gate")


def local_stack(core, level, depth, heads, window):
    nc, dram = core.nc, core.dram
    inner = 3 * heads * 64
    with Stage(core) as st:
        sem = st.sem
        wqkv = st.sb("wqkv", [P, inner])
        wo = st.sb("wo", [P, heads // 2, DIM])
        w1 = st.sb("w1", [P, 2 * HIDDEN])
        w2 = st.sb("w2", [P, HIDDEN // P, DIM])
        wcols = st.sb("cols", [P, 9])
        scales = st.sb("scales", [P, 4, 64])
        tab = st.sb("tab", [P, 2, 4, 64])

        def load_attention(sp, done, at):
            sp.dma_start(wqkv[:, :], dram[level + "_wqkv"][at].rearrange("a p n -> p (a n)")).then_inc(done, 16)
            sp.dma_start(wo[:, :, :], dram[level + "_wo"][at].rearrange("a p i n -> p (a i) n")).then_inc(done, 16)
            sp.dma_start(scales[:, :, :].rearrange("p i n -> p (i n)"),
                         dram[level + "_scales"][at].rearrange("a i n -> a (i n)").partition_broadcast(P)
                         ).then_inc(done, 16)

        with st.block() as block:
            @block.vector
            def _(dve):
                for c in range(CH):
                    dve.tensor_copy(core.y[:, cols(c, BANK)], core.xn[:, cols(c, BANK)]).then_inc(sem("started"), 1)

            @block.sync
            def _(sp):
                load_attention(sp, sem("first"), bass.ds(0, 1))
                sp.wait_ge(sem("first"), 48)
        st.clear()
        with nc.Fori(0, depth) as layer:
            at = bass.ds(layer, 1)
            with st.block() as block:
                @block.vector
                def _(dve):
                    for t in range(2):
                        dve.tensor_tensor(tab[:, t, :, :], core.c[level + "_rotary"][:, t, :, :],
                                          scales[:, :, :], ALU.mult).then_inc(sem("tables"), 1)

                @block.sync
                def _(sp):
                    sp.dma_start(w2[:, :, :], dram[level + "_w2"][at].rearrange("a p i n -> p (a i) n")
                                 ).then_inc(sem("weights"), 16)
                    for buf, name in ((w1, "_w1"), (wcols, "_cols")):
                        sp.dma_start(buf[:, :], dram[level + name][at].rearrange("a p n -> p (a n)")
                                     ).then_inc(sem("weights"), 16)
                    sp.wait_ge(sem("weights"), 48)
            st.clear()
            with Stage(core) as attention:
                local_attention(core, attention, heads, window, wqkv, wo, tab, core.c[level + "_band"])
            mlp(core, {"w1": w1, "w2": w2, "cols": wcols},
                lambda sp, done: load_attention(sp, done, bass.ds(layer + 1, 1)))
        with st.block() as block:
            @block.vector
            def _(dve):
                for c in range(CH):
                    dve.tensor_tensor(core.x[:, cols(c, BANK)], core.x[:, cols(c, BANK)],
                                      core.y[:, cols(c, BANK)], ALU.add).then_inc(sem("summed"), 1)
        st.clear()


def program(nc, dram, out, upto=99, start=0):
    with ExitStack() as ctx:
        core = Core(nc, ctx, dram)
        core.comb_d = nc.dram_tensor("comb_d", (8, TOK), F32, kind="Internal").ap()
        core.rel_pitch = 17 * 384
        core.rel_d = nc.dram_tensor("rel_d", (TILES, P * core.rel_pitch), F32, kind="Internal").ap()
        load(core, CONST_ALL)
        if start <= 0:
            layernorm(core, core.x, core.xn, 0)
            if upto >= 1:
                gated_scan(core)
            if upto >= 2:
                experts(core, "l0", 8, HIDDEN, False, "l0s")
        if start <= 1 and upto >= 3:
            layernorm(core, core.x, core.xn, 0)
            delta_rule(core)
        if start <= 1 and upto >= 4:
            local_stack(core, "l1", 2, 8, 64)
        if start <= 2 and upto >= 5:
            layernorm(core, core.x, core.xn, 0)
            wide_attention(core, True)
        if start <= 2 and upto >= 6:
            local_stack(core, "l2", 6, 16, 32)
        if start <= 3 and upto >= 7:
            layernorm(core, core.x, core.xn, 0)
            layernorm(core, core.xn, core.h, 1, core.c["l3_cols"][:, 3:4], core.c["l3_cols"][:, 4:5])
            wide_attention(core, False)
        if start <= 3 and upto >= 8:
            experts(core, "l3", 8, 256, True, None)
        store_stream(core, core.x, out)


def kernel(**inputs):
    import concourse.bacc as bacc
    from concourse.bass_utils import run_bass_kernel_spmd

    arrays = laid_out({k: np.asarray(v) for k, v in inputs.items()})
    nc = bacc.Bacc("TRN2", target_bir_lowering=False, num_devices=1)
    dram = {k: nc.dram_tensor("in_" + k, v.shape, F32, kind="ExternalInput").ap() for k, v in arrays.items()}
    out = nc.dram_tensor("out", (TOK, DIM), F32, kind="ExternalOutput").ap()
    program(nc, dram, out)
    r = run_bass_kernel_spmd(nc, [{"in_" + k: v for k, v in arrays.items()}], core_ids=[0])
    return r.results[0]["out"].reshape(BATCH, LEN, DIM)
```
